# Optimizing a Trainium2 kernel written in Bass

```python
import numpy as np
import jax
import jax.numpy as jnp

def _softmax(x, axis=-1):
    return jax.nn.softmax(x, axis=axis)
def _gelu(x):
    return jax.nn.gelu(x, approximate=True)
def _silu(x):
    return jax.nn.silu(x)
def _sigmoid(x):
    return jax.nn.sigmoid(x)
def _layernorm(x, axis=-1, eps=1e-5):
    m = jnp.mean(x, axis=axis, keepdims=True)
    v = jnp.var(x, axis=axis, keepdims=True)
    return (x - m) / jnp.sqrt(v + eps)
def _scatter_add(tgt, idx, src, axis=0):
    return tgt.at[idx].add(src)
def _segment_sum(src, seg, n):
    return jax.ops.segment_sum(src, seg, n)

kernel_name = 'mk_conv_seq_d4_conv_nchw128_e41cab'

def setup_inputs(seed: int = 0):
    np.random.seed(seed)
    _w = jnp.asarray
    def _rec_inputs():
        import jax
        import jax.numpy as jnp
        _gk = jax.random.key(seed)
        x = -0.0002928 + 1 * jax.random.normal(jax.random.fold_in(_gk, 1), (8, 128, 64, 64), jnp.float32)
        return x
    x = _rec_inputs()
    def _L0_conv_setup():
        import jax, jax.numpy as jnp
        import numpy as np
        key = jax.random.key(seed)
        k = jax.random.split(key, 5)
        C, Cb = (128, 64)
        x = jax.random.normal(k[0], (8, C, 64, 64), dtype=jnp.float32)
        s_in = 1.0 / np.sqrt(C)
        s_b = 1.0 / np.sqrt(Cb)
        w_theta = jax.random.normal(k[1], (Cb, C), dtype=jnp.float32) * s_in
        w_phi = jax.random.normal(k[2], (Cb, C), dtype=jnp.float32) * s_in
        w_g = jax.random.normal(k[3], (Cb, C), dtype=jnp.float32) * s_in
        w_last = jax.random.normal(k[4], (C, Cb), dtype=jnp.float32) * s_b
        return {'x': x, 'w_theta': w_theta, 'w_phi': w_phi, 'w_g': w_g, 'w_last': w_last}
    _L0_conv_all = _L0_conv_setup()
    _L0_conv_in = {k: v for k, v in _L0_conv_all.items() if k in ('w_theta', 'w_phi', 'w_g', 'w_last', )}
    del _L0_conv_all

    def _L1_conv_setup():
        import jax, jax.numpy as jnp
        import numpy as np
        from functools import partial
        IN_DIM = 128
        NUM_HEADS = 8
        DOWN_DIM = IN_DIM // 2
        HEAD_DIM = DOWN_DIM // NUM_HEADS
        MID = max(1, DOWN_DIM // 16)
        DIL = 3
        BN_EPS = 1e-05

        def conv2d(x, w, padding=0, dilation=1):
            return jax.lax.conv_general_dilated(x, w, window_strides=(1, 1), padding=[(padding, padding), (padding, padding)], rhs_dilation=(dilation, dilation), dimension_numbers=('NCHW', 'OIHW', 'NCHW'))

        def batchnorm(x, gamma, beta, mean, var):
            scale = (gamma / jnp.sqrt(var + BN_EPS))[None, :, None, None]
            shift = (beta - mean * gamma / jnp.sqrt(var + BN_EPS))[None, :, None, None]
            return x * scale + shift

        def complex_l2_norm(z, eps=1e-06):
            denom = jnp.sqrt(jnp.sum(z.real ** 2 + z.imag ** 2, axis=-1, keepdims=True) + eps)
            return z / denom

        def complex_softmax(z):
            return jax.lax.complex(jax.nn.softmax(z.real, axis=-1), jax.nn.softmax(z.imag, axis=-1))
        key = jax.random.key(seed)
        ks = jax.random.split(key, 6)
        B, H, W = (8, 128, 128)
        inp = {}
        inp['x'] = jax.random.normal(ks[0], (B, IN_DIM, H, W), dtype=jnp.float32)
        inp['conv_w'] = jax.random.normal(ks[1], (DOWN_DIM, IN_DIM, 3, 3), dtype=jnp.float32) * 0.02
        inp['bn1_g'] = jnp.ones((DOWN_DIM,), jnp.float32)
        inp['bn1_b'] = jnp.zeros((DOWN_DIM,), jnp.float32)
        inp['bn1_m'] = jnp.zeros((DOWN_DIM,), jnp.float32)
        inp['bn1_v'] = jnp.ones((DOWN_DIM,), jnp.float32)
        inp['cg1_w'] = jax.random.normal(ks[2], (MID, DOWN_DIM, 1, 1), dtype=jnp.float32) * 0.1
        inp['cg1_b'] = jnp.zeros((MID,), jnp.float32)
        inp['cgbn_g'] = jnp.ones((MID,), jnp.float32)
        inp['cgbn_b'] = jnp.zeros((MID,), jnp.float32)
        inp['cgbn_m'] = jnp.zeros((MID,), jnp.float32)
        inp['cgbn_v'] = jnp.ones((MID,), jnp.float32)
        inp['cg2_w'] = jax.random.normal(ks[3], (DOWN_DIM, MID, 1, 1), dtype=jnp.float32) * 0.1
        inp['cg2_b'] = jnp.zeros((DOWN_DIM,), jnp.float32)
        inp['tau'] = jnp.ones((NUM_HEADS, 1, 1), jnp.float32) * HEAD_DIM ** (-0.5)
        return inp
    _L1_conv_all = _L1_conv_setup()
    _L1_conv_in = {k: v for k, v in _L1_conv_all.items() if k in ('conv_w', 'bn1_g', 'bn1_b', 'bn1_m', 'bn1_v', 'cg1_w', 'cg1_b', 'cgbn_g', 'cgbn_b', 'cgbn_m', 'cgbn_v', 'cg2_w', 'cg2_b', 'tau', )}
    del _L1_conv_all

    def _L2_conv_setup():
        import jax, jax.numpy as jnp
        import numpy as np
        UP = 2
        DOWN = 2
        SLOPE = 0.2
        GAIN = float(np.sqrt(2.0))
        PAD = [9, 8, 9, 8]
        DN = ('NCHW', 'OIHW', 'NCHW')

        def _kaiser_beta(a):
            if a > 50.0:
                return 0.1102 * (a - 8.7)
            if a > 21.0:
                return 0.5842 * (a - 21.0) ** 0.4 + 0.07886 * (a - 21.0)
            return 0.0

        def design_lowpass_filter(numtaps, cutoff, width, fs):
            nyq = fs / 2.0
            atten = 2.285 * (numtaps - 1) * np.pi * (width / nyq) + 7.95
            beta = _kaiser_beta(atten)
            m = np.arange(numtaps) - (numtaps - 1) / 2.0
            c = cutoff / nyq
            h = c * np.sinc(c * m)
            h *= np.kaiser(numtaps, beta)
            h /= h.sum()
            return h.astype(np.float32)

        def _sep_pass(x, f1d, axis, up=1, down=1, pad=(0, 0), gain=1.0):
            C = x.shape[1]
            f = (f1d * gain)[::-1]
            taps = f.shape[0]
            if axis == 2:
                k = jnp.broadcast_to(f.reshape(1, 1, taps, 1), (C, 1, taps, 1))
                strides, ld = ((down, 1), (up, 1))
                padding = ((pad[0], pad[1] + up - 1), (0, 0))
            else:
                k = jnp.broadcast_to(f.reshape(1, 1, 1, taps), (C, 1, 1, taps))
                strides, ld = ((1, down), (1, up))
                padding = ((0, 0), (pad[0], pad[1] + up - 1))
            return jax.lax.conv_general_dilated(x, k, strides, padding, lhs_dilation=ld, dimension_numbers=DN, feature_group_count=C)
        key = jax.random.key(seed)
        kx, kw, kbc, kb = jax.random.split(key, 4)
        B, Cin, Cout, S, K = (8, 128, 128, 128, 3)
        x = jax.random.normal(kx, (B, Cin, S, S), dtype=jnp.float32)
        w = jax.random.normal(kw, (Cout, Cin, K, K), dtype=jnp.float32) / np.sqrt(Cin * K * K)
        b_conv = jax.random.normal(kbc, (Cout,), dtype=jnp.float32) * 0.1
        bias = jax.random.normal(kb, (Cout,), dtype=jnp.float32) * 0.1
        up_filter = jnp.asarray(design_lowpass_filter(12, 64.0, 32.0, 256.0))
        down_filter = jnp.asarray(design_lowpass_filter(12, 64.0, 32.0, 256.0))
        return {'x': x, 'w': w, 'b_conv': b_conv, 'bias': bias, 'up_filter': up_filter, 'down_filter': down_filter}
    _L2_conv_all = _L2_conv_setup()
    _L2_conv_in = {k: v for k, v in _L2_conv_all.items() if k in ('w', 'b_conv', 'bias', 'up_filter', 'down_filter', )}
    del _L2_conv_all

    def _L3_conv_setup():
        import jax, jax.numpy as jnp
        import numpy as np
        MIDC = 128
        HEADS = 8
        HEADC = MIDC // HEADS
        EPS = 1e-05

        def _ln(t, w, b):
            m = t.mean(-1, keepdims=True)
            s = jnp.std(t, axis=-1, ddof=1, keepdims=True)
            return w * ((t - m) / (s + EPS)) + b
        key = jax.random.key(seed)
        ks = jax.random.split(key, 8)
        B, C, H, W = (8, MIDC, 256, 256)
        s = 1.0 / np.sqrt(C)
        x = jax.random.normal(ks[0], (B, C, H, W), dtype=jnp.float32)
        qkv_w = jax.random.normal(ks[1], (3 * C, C), dtype=jnp.float32) * s
        o1_w = jax.random.normal(ks[2], (C, C), dtype=jnp.float32) * s
        o2_w = jax.random.normal(ks[3], (C, C), dtype=jnp.float32) * s
        kln_w = 1.0 + 0.1 * jax.random.normal(ks[4], (HEADS, 1, HEADC), dtype=jnp.float32)
        kln_b = 0.1 * jax.random.normal(ks[5], (HEADS, 1, HEADC), dtype=jnp.float32)
        vln_w = 1.0 + 0.1 * jax.random.normal(ks[6], (HEADS, 1, HEADC), dtype=jnp.float32)
        vln_b = 0.1 * jax.random.normal(ks[7], (HEADS, 1, HEADC), dtype=jnp.float32)
        return {'x': x, 'qkv_w': qkv_w, 'o1_w': o1_w, 'o2_w': o2_w, 'kln_w': kln_w, 'kln_b': kln_b, 'vln_w': vln_w, 'vln_b': vln_b}
    _L3_conv_all = _L3_conv_setup()
    _L3_conv_in = {k: v for k, v in _L3_conv_all.items() if k in ('qkv_w', 'o1_w', 'o2_w', 'kln_w', 'kln_b', 'vln_w', 'vln_b', )}
    del _L3_conv_all

    return {
        "x": x,
        "L0_conv_w_theta": _L0_conv_in["w_theta"],
        "L0_conv_w_phi": _L0_conv_in["w_phi"],
        "L0_conv_w_g": _L0_conv_in["w_g"],
        "L0_conv_w_last": _L0_conv_in["w_last"],
        "L1_conv_conv_w": _L1_conv_in["conv_w"],
        "L1_conv_bn1_g": _L1_conv_in["bn1_g"],
        "L1_conv_bn1_b": _L1_conv_in["bn1_b"],
        "L1_conv_bn1_m": _L1_conv_in["bn1_m"],
        "L1_conv_bn1_v": _L1_conv_in["bn1_v"],
        "L1_conv_cg1_w": _L1_conv_in["cg1_w"],
        "L1_conv_cg1_b": _L1_conv_in["cg1_b"],
        "L1_conv_cgbn_g": _L1_conv_in["cgbn_g"],
        "L1_conv_cgbn_b": _L1_conv_in["cgbn_b"],
        "L1_conv_cgbn_m": _L1_conv_in["cgbn_m"],
        "L1_conv_cgbn_v": _L1_conv_in["cgbn_v"],
        "L1_conv_cg2_w": _L1_conv_in["cg2_w"],
        "L1_conv_cg2_b": _L1_conv_in["cg2_b"],
        "L1_conv_tau": _L1_conv_in["tau"],
        "L2_conv_w": _L2_conv_in["w"],
        "L2_conv_b_conv": _L2_conv_in["b_conv"],
        "L2_conv_bias": _L2_conv_in["bias"],
        "L2_conv_up_filter": _L2_conv_in["up_filter"],
        "L2_conv_down_filter": _L2_conv_in["down_filter"],
        "L3_conv_qkv_w": _L3_conv_in["qkv_w"],
        "L3_conv_o1_w": _L3_conv_in["o1_w"],
        "L3_conv_o2_w": _L3_conv_in["o2_w"],
        "L3_conv_kln_w": _L3_conv_in["kln_w"],
        "L3_conv_kln_b": _L3_conv_in["kln_b"],
        "L3_conv_vln_w": _L3_conv_in["vln_w"],
        "L3_conv_vln_b": _L3_conv_in["vln_b"],
    }

def reference(x, L0_conv_w_theta, L0_conv_w_phi, L0_conv_w_g, L0_conv_w_last, L1_conv_conv_w, L1_conv_bn1_g, L1_conv_bn1_b, L1_conv_bn1_m, L1_conv_bn1_v, L1_conv_cg1_w, L1_conv_cg1_b, L1_conv_cgbn_g, L1_conv_cgbn_b, L1_conv_cgbn_m, L1_conv_cgbn_v, L1_conv_cg2_w, L1_conv_cg2_b, L1_conv_tau, L2_conv_w, L2_conv_b_conv, L2_conv_bias, L2_conv_up_filter, L2_conv_down_filter, L3_conv_qkv_w, L3_conv_o1_w, L3_conv_o2_w, L3_conv_kln_w, L3_conv_kln_b, L3_conv_vln_w, L3_conv_vln_b):
    import jax
    import jax.numpy as jnp
    def _L0_conv_ref(x, w_theta, w_phi, w_g, w_last):
        import jax, jax.numpy as jnp
        import numpy as np
        B, C, H, W = x.shape
        xf = x.reshape(B, C, H * W)
        theta = jnp.einsum('kc,bcn->bkn', w_theta, xf)
        phi = jnp.einsum('kc,bcn->bkn', w_phi, xf)
        g = jnp.einsum('kc,bcn->bkn', w_g, xf)
        attn = jax.nn.softmax(jnp.einsum('bkn,bkm->bnm', theta, phi), axis=-1)
        y = jnp.einsum('bnm,bkm->bkn', attn, g)
        out = jnp.einsum('ck,bkn->bcn', w_last, y).reshape(B, C, H, W)
        return out + x

    def _L1_conv_ref(x, conv_w, bn1_g, bn1_b, bn1_m, bn1_v, cg1_w, cg1_b, cgbn_g, cgbn_b, cgbn_m, cgbn_v, cg2_w, cg2_b, tau):
        import jax, jax.numpy as jnp
        import numpy as np
        from functools import partial
        IN_DIM = 128
        NUM_HEADS = 8
        DOWN_DIM = IN_DIM // 2
        HEAD_DIM = DOWN_DIM // NUM_HEADS
        MID = max(1, DOWN_DIM // 16)
        DIL = 3
        BN_EPS = 1e-05

        def conv2d(x, w, padding=0, dilation=1):
            return jax.lax.conv_general_dilated(x, w, window_strides=(1, 1), padding=[(padding, padding), (padding, padding)], rhs_dilation=(dilation, dilation), dimension_numbers=('NCHW', 'OIHW', 'NCHW'))

        def batchnorm(x, gamma, beta, mean, var):
            scale = (gamma / jnp.sqrt(var + BN_EPS))[None, :, None, None]
            shift = (beta - mean * gamma / jnp.sqrt(var + BN_EPS))[None, :, None, None]
            return x * scale + shift

        def complex_l2_norm(z, eps=1e-06):
            denom = jnp.sqrt(jnp.sum(z.real ** 2 + z.imag ** 2, axis=-1, keepdims=True) + eps)
            return z / denom

        def complex_softmax(z):
            return jax.lax.complex(jax.nn.softmax(z.real, axis=-1), jax.nn.softmax(z.imag, axis=-1))
        B, C, H, W = x.shape
        feat = conv2d(x, conv_w, padding=DIL, dilation=DIL)
        feat = batchnorm(feat, bn1_g, bn1_b, bn1_m, bn1_v)
        feat = jax.nn.gelu(feat, approximate=False)
        F2 = jnp.fft.fft2(feat.astype(jnp.float32), axes=(-2, -1))
        N = H * W
        qkv = F2.reshape(B, NUM_HEADS, HEAD_DIM, N)
        q = complex_l2_norm(qkv)
        k = complex_l2_norm(qkv)
        v = qkv
        attn = jnp.einsum('bhdn,bhen->bhde', q, jnp.conj(k)) * tau
        attn = complex_softmax(attn)
        out_f = jnp.einsum('bhde,bhen->bhdn', attn, v)
        out_f = out_f.reshape(B, DOWN_DIM, H, W)
        out_f = jnp.abs(jnp.fft.ifft2(out_f, axes=(-2, -1)))
        gr = F2.real
        cg = conv2d(gr, cg1_w) + cg1_b[None, :, None, None]
        cg = batchnorm(cg, cgbn_g, cgbn_b, cgbn_m, cgbn_v)
        cg = jax.nn.gelu(cg, approximate=False)
        cg = conv2d(cg, cg2_w) + cg2_b[None, :, None, None]
        cg = jax.nn.sigmoid(cg)
        gate = cg * F2
        gate = jnp.abs(jnp.fft.ifft2(gate, axes=(-2, -1)))
        y = jnp.concatenate([out_f, gate], axis=1)
        return y + x

    def _L2_conv_ref(x, w, b_conv, bias, up_filter, down_filter):
        import jax, jax.numpy as jnp
        import numpy as np
        UP = 2
        DOWN = 2
        SLOPE = 0.2
        GAIN = float(np.sqrt(2.0))
        PAD = [9, 8, 9, 8]
        DN = ('NCHW', 'OIHW', 'NCHW')

        def _kaiser_beta(a):
            if a > 50.0:
                return 0.1102 * (a - 8.7)
            if a > 21.0:
                return 0.5842 * (a - 21.0) ** 0.4 + 0.07886 * (a - 21.0)
            return 0.0

        def design_lowpass_filter(numtaps, cutoff, width, fs):
            nyq = fs / 2.0
            atten = 2.285 * (numtaps - 1) * np.pi * (width / nyq) + 7.95
            beta = _kaiser_beta(atten)
            m = np.arange(numtaps) - (numtaps - 1) / 2.0
            c = cutoff / nyq
            h = c * np.sinc(c * m)
            h *= np.kaiser(numtaps, beta)
            h /= h.sum()
            return h.astype(np.float32)

        def _sep_pass(x, f1d, axis, up=1, down=1, pad=(0, 0), gain=1.0):
            C = x.shape[1]
            f = (f1d * gain)[::-1]
            taps = f.shape[0]
            if axis == 2:
                k = jnp.broadcast_to(f.reshape(1, 1, taps, 1), (C, 1, taps, 1))
                strides, ld = ((down, 1), (up, 1))
                padding = ((pad[0], pad[1] + up - 1), (0, 0))
            else:
                k = jnp.broadcast_to(f.reshape(1, 1, 1, taps), (C, 1, 1, taps))
                strides, ld = ((1, down), (1, up))
                padding = ((0, 0), (pad[0], pad[1] + up - 1))
            return jax.lax.conv_general_dilated(x, k, strides, padding, lhs_dilation=ld, dimension_numbers=DN, feature_group_count=C)
        K = w.shape[-1]
        p = K - 1
        x = jax.lax.conv_general_dilated(x, w, (1, 1), ((p, p), (p, p)), dimension_numbers=DN)
        x = x + b_conv[None, :, None, None]
        x = x + bias[None, :, None, None]
        g = float(UP)
        x = _sep_pass(x, up_filter, axis=2, up=UP, pad=(PAD[2], PAD[3]), gain=g)
        x = _sep_pass(x, up_filter, axis=3, up=UP, pad=(PAD[0], PAD[1]), gain=g)
        x = jnp.where(x >= 0, x, SLOPE * x) * GAIN
        x = _sep_pass(x, down_filter, axis=2, down=DOWN)
        x = _sep_pass(x, down_filter, axis=3, down=DOWN)
        return x

    def _L3_conv_ref(x, qkv_w, o1_w, o2_w, kln_w, kln_b, vln_w, vln_b):
        import jax, jax.numpy as jnp
        import numpy as np
        MIDC = 128
        HEADS = 8
        HEADC = MIDC // HEADS
        EPS = 1e-05

        def _ln(t, w, b):
            m = t.mean(-1, keepdims=True)
            s = jnp.std(t, axis=-1, ddof=1, keepdims=True)
            return w * ((t - m) / (s + EPS)) + b
        B, C, H, W = x.shape
        hc = C // HEADS
        N = H * W
        qkv = jnp.einsum('oc,bchw->bhwo', qkv_w, x)
        qkv = qkv.reshape(B, N, HEADS, 3 * hc).transpose(0, 2, 1, 3)
        q, k, v = jnp.split(qkv, 3, axis=-1)
        k = _ln(k, kln_w, kln_b)
        v = _ln(v, vln_w, vln_b)
        kv = jnp.einsum('bhnd,bhne->bhde', k, v) / N
        o = jnp.einsum('bhnd,bhde->bhne', q, kv)
        o = o.transpose(0, 2, 1, 3).reshape(B, H, W, C).transpose(0, 3, 1, 2)
        ret = o + x
        u = jnp.einsum('oc,bchw->bohw', o1_w, ret)
        u = jax.nn.gelu(u, approximate=False)
        u = jnp.einsum('oc,bchw->bohw', o2_w, u) + x
        return jax.nn.gelu(u, approximate=False)

    def _gn(v, G=32, eps=1e-5):
        B_, C_, H_, W_ = v.shape
        g = v.reshape(B_, G, C_ // G, H_, W_)
        m = jnp.mean(g, axis=(2, 3, 4), keepdims=True)
        s = jnp.var(g, axis=(2, 3, 4), keepdims=True)
        return ((g - m) / jnp.sqrt(s + eps)).reshape(v.shape)

    def _ln_c(v, eps=1e-6):
        m = jnp.mean(v, axis=1, keepdims=True)
        s = jnp.var(v, axis=1, keepdims=True)
        return (v - m) / jnp.sqrt(s + eps)

    def _ln_t(v, eps=1e-5):
        m = jnp.mean(v, axis=-1, keepdims=True)
        s = jnp.var(v, axis=-1, keepdims=True)
        return (v - m) / jnp.sqrt(s + eps)

    def _to_tokens(v):
        B_, C_, H_, W_ = v.shape
        return v.reshape(B_, C_, H_ * W_).transpose(0, 2, 1)
    def _from_tokens(t, like):
        B_, C_, H_, W_ = like.shape
        return t.transpose(0, 2, 1).reshape(B_, C_, H_, W_)

    x = _L0_conv_ref(x, L0_conv_w_theta, L0_conv_w_phi, L0_conv_w_g, L0_conv_w_last)
    x = _L1_conv_ref(x, L1_conv_conv_w, L1_conv_bn1_g, L1_conv_bn1_b, L1_conv_bn1_m, L1_conv_bn1_v, L1_conv_cg1_w, L1_conv_cg1_b, L1_conv_cgbn_g, L1_conv_cgbn_b, L1_conv_cgbn_m, L1_conv_cgbn_v, L1_conv_cg2_w, L1_conv_cg2_b, L1_conv_tau)
    x = _L2_conv_ref(x, L2_conv_w, L2_conv_b_conv, L2_conv_bias, L2_conv_up_filter, L2_conv_down_filter)
    x = _L3_conv_ref(x, L3_conv_qkv_w, L3_conv_o1_w, L3_conv_o2_w, L3_conv_kln_w, L3_conv_kln_b, L3_conv_vln_w, L3_conv_vln_b)
    return x


_drawn_inputs = setup_inputs


def setup_inputs(seed=0):
    import zlib

    import numpy as np

    out = dict(_drawn_inputs(seed))
    spreads = {'L1_conv_bn1_g': (1.0, 0.2),
     'L1_conv_bn1_b': (0.0, 0.1),
     'L1_conv_bn1_m': (0.0, 0.1),
     'L1_conv_bn1_v': (1.0, 0.2),
     'L1_conv_cg1_b': (0.0, 2.0),
     'L1_conv_cgbn_g': (1.0, 0.6),
     'L1_conv_cgbn_b': (0.0, 2.0),
     'L1_conv_cgbn_m': (0.0, 2.0),
     'L1_conv_cgbn_v': (1.0, 0.6),
     'L1_conv_cg2_b': (0.0, 2.0),
     'L1_conv_tau': (0.3535533845424652, 0.6)}
    factors = {}
    for name, (base, spread) in spreads.items():
        noise = np.random.default_rng([zlib.crc32(name.encode()), seed]).standard_normal(out[name].shape)
        drawn = base * np.exp(spread * noise) if base else spread * noise
        out[name] = jnp.asarray(drawn.astype(out[name].dtype))
    for name, factor in factors.items():
        out[name] = (out[name] * factor).astype(out[name].dtype)
    return out
```

```python
import concourse.bass as bass
from concourse import mybir
from contextlib import ExitStack
import numpy as np

B, C, H, W = 8, 128, 64, 64
N = H * W
CB = 64
BW = 512
NB = N // BW
MC = N // 128
TAPS = 9
MID = 4
KH = W // 2 + 1
DIL = 3
HP1 = H + 2 * DIL
HP2 = H + 4
HC = H + 2
HU = 2 * HC + 6
HK = HU // 2
CROWS = 6
NR2 = HC // CROWS
HEADS, HD = 8, 16
EPS_BN = 1e-5
GAIN = float(np.sqrt(2.0))
NG3 = N // 256
NGR = C // 2
GS = 13
SETUP = 12
START = 1


def rep(ap, dim, n):
    shape = list(ap.unsqueeze(dim).shape)
    shape[dim] = n
    return ap.unsqueeze(dim).broadcast_to(shape)


def build(nc, T, out):
    f32, f32r = mybir.dt.float32, mybir.dt.float32r
    ALU, ACT, AX = mybir.AluOpType, mybir.ActivationFunctionType, mybir.AxisListType
    ctx = ExitStack()
    with ctx:
        def sb(name, shape, dt=f32):
            return ctx.enter_context(nc.sbuf_tensor(name + "_sb", shape, dt))

        def sem(name):
            return ctx.enter_context(nc.semaphore(name))

        x_v = T["x"].rearrange("b c h w -> b c (h w)")
        out_v = out.rearrange("b c h w -> b c (h w)")

        X = sb("X", [C, N])
        ident = sb("ident", [128, 128])
        wth2 = sb("wth2", [C, 128])
        wph2 = sb("wph2", [C, 128])
        wg = sb("wg", [C, CB])
        wlast = sb("wlast", [CB, C])
        sumsel = sb("sumsel", [CB + 1, 128])
        RA = sb("RA", [128, 3 * N], f32r)
        ThH = RA[:, 0:N]
        PhS = RA[:, N:2 * N]
        ThL = RA[0:CB + 2, 2 * N:3 * N]
        PhA = sb("PhA", [CB + 2, N], f32r)
        TA = sb("TA", [CB, 2, BW], f32r)
        FA = sb("FA", [128, 23208])
        at = [0]

        def fa(n, reset=False):
            if reset:
                at[0] = 0
            at[0] += n
            return FA[:, at[0] - n:at[0]]

        gT = fa(MC * (CB + 1), True).rearrange("p (m k) -> p m k", m=MC)
        P = fa(4 * BW).rearrange("p (s n) -> p s n", s=4)
        Y = fa(BW)
        rec = fa(BW)
        upd = fa(BW)
        mx8 = fa(32).rearrange("p (t k) -> p t k", t=4)
        mxn = fa(4)
        mxHL = fa(8).rearrange("p (t k) -> p t k", t=4)
        mxr = sb("mxr", [128, 4], f32r)

        PH1, PL1 = [RA[:, i * HP1 * HP1:(i + 1) * HP1 * HP1].rearrange("p (h w) -> p h w", h=HP1) for i in range(2)]
        Xi = X[:, :].rearrange("p (h w) -> p h w", h=H)
        w1 = sb("w1", [C, TAPS, CB])
        w1s = sb("w1s", [C, TAPS, 2 * CB], f32r)
        bn = sb("bn", [CB, 4])
        bn1s, bn1b = sb("bn1s", [CB, 1]), sb("bn1b", [CB, 1])
        cgp = sb("cgp", [MID, 5])
        cgs, cgb = sb("cgs", [MID, 1]), sb("cgb", [MID, 1])
        eps5, eps6 = sb("eps5", [128, 1]), sb("eps6", [128, 1])
        cg2b = sb("cg2b", [CB, 1])
        tauc = sb("tauc", [CB, 1])
        eyecg = sb("eyecg", [CB, CB + MID])
        w2t = sb("w2t", [MID, CB])
        headneg = sb("headneg", [CB, CB])
        att = sb("att", [CB, 2 * CB])
        pairsum = sb("pairsum", [128, CB])
        hdft = sb("hdft", [H, 2 * KH])
        wdft = sb("wdft", [128, 128])
        iwdft = sb("iwdft", [128, 128])
        ihdft = sb("ihdft", [KH, 2 * H])
        c1t = fa(2 * BW, True).rearrange("p (s n) -> p s n", s=2)[0:CB]
        c1s = fa(2 * BW).rearrange("p (s n) -> p s n", s=2)[0:CB]
        Fc = fa(N)[0:CB]
        CR = CB + MID
        F1 = fa(W * CR).rearrange("p (w c) -> p w c", w=W)[0:H]
        T1 = fa(KH * CR).rearrange("p (k c) -> p k c", k=KH)
        FF = fa(KH * CR).rearrange("p (k c) -> p k c", k=KH)
        SG = fa(KH * 2 * W)[0:CB]
        RG = FA[0:MID, 4 * BW + N:4 * BW + N + KH * W]
        GT = fa(KH * CB).rearrange("p (k c) -> p k c", k=KH)
        U = FA[:, 4 * BW:4 * BW + CB * 128].rearrange("p (c w) -> p c w", c=CB)[0:KH]
        sqv = FA[:, 0:2 * BW].rearrange("p (s n) -> p s n", s=2)
        rtv = SG[:, 0:2 * BW].rearrange("p (s n) -> p s n", s=2)
        absv = FA[:, 2 * BW:4 * BW].rearrange("p (s n) -> p s n", s=2)[CB:128]
        gram, gdiag, den, rden, dmat, alog, amax, aexp, asum = [sb(n, [CB, k]) for n, k in (
            ("gram", CB), ("gdiag", CB), ("den", 4), ("rden", 4), ("dmat", CB), ("alog", CB), ("amax", 4), ("aexp", CB), ("asum", 4))]

        PH2, PL2 = [RA[:, i * HP2 * HP2:(i + 1) * HP2 * HP2].rearrange("p (h w) -> p h w", h=HP2) for i in range(2)]
        w3 = FA[:, 0:TAPS * C].rearrange("p (t c) -> p t c", t=TAPS)
        w3H, w3L = sb("w3H", [C, TAPS, C], f32r), sb("w3L", [C, TAPS, C], f32r)
        b3 = sb("b3", [C, 3])
        upm = sb("upm", [HC, HU])
        dnm = sb("dnm", [HK, 2, H])
        Z = fa(2 * W * C, True).rearrange("p (q w c) -> p q w c", q=2, w=W)[0:HK]
        Xc = FA[:, 0:HC * HC]
        XhA = X[0:HC, :].rearrange("p (w c) -> p w c", w=N // C)
        XhB = fa((HC - N // C) * C).rearrange("p (w c) -> p w c", c=C)[0:HC]

        def xh(w0, w1):
            return XhA[:, w0:w1, :] if w1 <= N // C else XhB[:, w0 - N // C:w1 - N // C, :]
        Xg = fa(2 * 2 * HC).rearrange("p (s c w) -> p s c w", s=2, c=2)[0:HC]
        S1 = fa(2 * 2 * HU).rearrange("p (s n) -> p s n", s=2)[0:HC]
        Rl = fa(4 * HU).rearrange("p (q n) -> p q n", q=2)[0:HK]
        Yt = fa(2 * 4 * HU).rearrange("p (s q n) -> p s q n", s=2, q=2)[0:HK]

        wkv, wkvc = sb("wkv", [C, 2 * C]), sb("wkvc", [C, 2 * C])
        wkm = sb("wkm", [C, 2 * HEADS])
        wq, o1t, o2t = sb("wq", [C, C]), sb("o1t", [C, C]), sb("o2t", [C, C])
        lnw, lnb = sb("lnw", [128, 2 * C]), sb("lnb", [128, 2 * C])
        headm = sb("headm", [C, C])
        KVm, MI, GTm = sb("KVm", [C, C]), sb("MI", [C, C]), sb("GTm", [C, C])
        fa(8000, True)
        sq3 = fa(2 * BW).rearrange("p (s n) -> p s n", s=2)
        kvn = fa(2 * BW).rearrange("p (s n) -> p s n", s=2)
        kvf = fa(2 * BW).rearrange("p (s n) -> p s n", s=2)
        ss3 = fa(64).rearrange("p (s n) -> p s n", s=2)
        sd3 = fa(64).rearrange("p (s n) -> p s n", s=2)
        rs3 = fa(64).rearrange("p (s n) -> p s n", s=2)
        uu = fa(2 * BW).rearrange("p (s n) -> p s n", s=2)
        tt = fa(2 * BW).rearrange("p (s n) -> p s n", s=2)
        oo = fa(2 * BW).rearrange("p (s n) -> p s n", s=2)

        bank = [ctx.enter_context(nc.psum_tensor(f"bank{i}", [128, BW], f32)) for i in range(8)]
        psS, psA, psY, psZ, psQ = bank[0:2], bank[2:4], bank[4:6], bank[6], bank[7]

        x_in = [sem(f"x_in{k}") for k in range(NB)]
        w_in = sem("w_in")
        stored = sem("stored")
        consts = sem("consts")
        th_ready, ph_ready, g_ready = sem("th_ready"), sem("ph_ready"), sem("g_ready")
        thH_done, phH_done, thL_done, phL_done, phA_done, g_done = [sem(n) for n in ("thH_done", "phH_done", "thL_done", "phL_done", "phA_done", "g_done")]
        ta_ready, a_ready, a_used, mx_ready, row_ready, row_written = [sem(n) for n in ("ta_ready", "a_ready", "a_used", "mx_ready", "row_ready", "row_written")]
        s_ready, p_ready, pv_done, y_saved, z_ready, upd_ready, x1_done = [sem(n) for n in ("s_ready", "p_ready", "pv_done", "y_saved", "z_ready", "upd_ready", "x1_done")]
        mx_step, rec_ready = sem("mx_step"), sem("rec_ready")
        names = """setup zero1 p1H_done p1L_done c1_ready c1_moved c1_summed f_done tr_ready tr_act tr_dve
            gram_ready gram_step ht_ready ht_act ht_dve wt_ready wt_act r_ready r_done sg_ready sg_done cg_ready cg_used
            of_ready sq_done sqs_ready root_done xa_done il_ready il_act il_dve ik_ready abs_done xb_done
            zero2 p2H_done p2L_done c2_ready c2_done xt_ready xt_act xt_dve xg_done s1_ready s1_done s2_ready relu_done
            y_done s3_ready z_done s4_ready s4_act s4_dve
            tok_ready sq3_done ss_done sd_done rs_step kvn_done kv_scaled kvf_done kv_ready kvm_done m_ready mi_done gt_ready gt_done
            u_ready u_done o2_ready t_done o_done""".split()
        (setup, zero1, p1H_done, p1L_done, c1_ready, c1_moved, c1_summed, f_done, tr_ready, tr_act, tr_dve,
         gram_ready, gram_step, ht_ready, ht_act, ht_dve, wt_ready, wt_act, r_ready, r_done, sg_ready, sg_done, cg_ready, cg_used,
         of_ready, sq_done, sqs_ready, root_done, xa_done, il_ready, il_act, il_dve, ik_ready, abs_done, xb_done,
         zero2, p2H_done, p2L_done, c2_ready, c2_done, xt_ready, xt_act, xt_dve, xg_done, s1_ready, s1_done, s2_ready, relu_done,
         y_done, s3_ready, z_done, s4_ready, s4_act, s4_dve,
         tok_ready, sq3_done, ss_done, sd_done, rs_step, kvn_done, kv_scaled, kvf_done, kv_ready, kvm_done, m_ready, mi_done, gt_ready, gt_done,
         u_ready, u_done, o2_ready, t_done, o_done) = [sem(n) for n in names]
        out_sem = [sem("out0"), sem("out1")]
        started = [pv_done, z_ready, x1_done, a_ready, upd_ready, s1_done, y_done, z_done, s3_ready, s1_ready, o_done, *out_sem]
        block = ctx.enter_context(nc.Block())

        def plain(engine):
            engine.nop(nofuse=True)

        weights = [(ident, "ident"), (wth2, "wth2"), (wph2, "wph2"), (wg, "wg"), (wlast, "wlast"), (sumsel, "sumsel"),
                   (w1, "w1"), (bn, "bn"), (cgp, "cgp"), (cg2b, "cg2b"), (tauc, "tauc"), (eyecg, "eyecg"), (w2t, "w2t"),
                   (headneg, "headneg"), (att, "att"), (pairsum, "pairsum"), (hdft, "hdft"), (wdft, "wdft"), (iwdft, "iwdft"),
                   (ihdft, "ihdft"), (w3, "w3"), (b3, "b3"), (upm, "upm"), (dnm, "dnm"), (wkv, "wkv"), (wq, "wq"), (o1t, "o1t"),
                   (o2t, "o2t"), (lnw, "lnw"), (lnb, "lnb"), (headm, "headm")]

        @block.sync
        def _(sp):
            for dst, name in weights:
                sp.dma_start(dst[tuple([slice(None)] * len(T[name].shape))], T[name]).then_inc(w_in, 16)
            for k in range(NB):
                sp.dma_start(X[:, k * BW:(k + 1) * BW], x_v[0, :, k * BW:(k + 1) * BW]).then_inc(x_in[k], 16)
            def finish(b, more):
                for k in range(NB):
                    ck = slice(k * BW, (k + 1) * BW)
                    sp.wait_ge(o_done, b * NB + (k + 1) + START)
                    sp.dma_start(out_v[b, :, ck], oo[:, k % 2, :]).then_inc(out_sem[k % 2], 16)
                    if more:
                        sp.wait_ge(t_done, b * NB + (k + 1))
                        sp.dma_start(X[:, ck], x_v[b + 1, :, ck]).then_inc(x_in[k], 16)

            if B > 1:
                with sp.Fori(0, B - 1) as b:
                    finish(b, True)
            finish(B - 1, False)
            for q in range(2):
                sp.wait_ge(out_sem[q], B * (NB // 2) * 16 + START)

        def max_steps(i):
            lo, hi = 4, 28
            return range((i - lo) * 4 // 3, (i - lo + 1) * 4 // 3) if lo <= i < hi else range(0)

        @block.tensor
        def _(pe):
            def prep(b):
                for k in range(NB):
                    xk = X[:, k * BW:(k + 1) * BW]
                    pe.wait_ge(x_in[k], (b + 1) * 16)
                    if k >= 2:
                        pe.wait_ge(thL_done, b * NB + (k - 1))
                    pe.matmul(psS[k % 2][:, :], wth2[:, :], xk, start=True, stop=True).then_inc(th_ready, 1)
                    if k >= 2:
                        pe.wait_ge(phL_done, b * NB + (k - 1))
                    pe.matmul(psA[k % 2][:, :], wph2[:, :], xk, start=True, stop=True).then_inc(ph_ready, 1)
                    if k >= 2:
                        pe.wait_ge(g_done, b * NB + (k - 1))
                    for s in range(4):
                        last = pe.matmul(psY[k % 2][:, s * CB:(s + 1) * CB], X[:, k * BW + s * 128:k * BW + (s + 1) * 128],
                                         wg[:, :], start=True, stop=True)
                    last.then_inc(g_ready, 1)

            def maxpass(g, par, s):
                if s >= 2:
                    pe.wait_ge(a_used, g * MC + (s - 1))
                t, k = divmod(s, NB)
                pe.matmul(psA[s % 2][:, :], TA[:, par, t * 128:(t + 1) * 128], PhS[0:CB, k * BW:(k + 1) * BW],
                          start=True, stop=True).then_inc(a_ready, 1)

            def rows(g):
                pe.wait_ge(mx_ready, g + 1)
                for t in range(4):
                    last = pe.matmul(psQ[CB:CB + 2, t * 128:(t + 1) * 128], mxHL[:, t, :], ident[:, :], start=True, stop=True)
                last.then_inc(row_ready, 1)

            def scores(i, blk):
                pe.matmul(psS[i % 2][:, :], PhS[:, i * 128:(i + 1) * 128], ThH[:, blk], start=True, stop=False)
                pe.matmul(psS[i % 2][:, :], PhA[:, i * 128:(i + 1) * 128], ThL[:, blk], start=False, stop=True).then_inc(s_ready, 1)

            def pair(b, j2, last_pair):
                for par in range(2):
                    g = b * NB + j2 * 2 + par
                    nxt = not (last_pair and par == 1)
                    blk = bass.ds((j2 * 2 + par) * BW, BW)
                    nblk = bass.ds((j2 * 2 + (par + 1)) * BW, BW)
                    for i in range(MC):
                        if 1 <= i < MC - 1:
                            pe.wait_ge(p_ready, g * MC + i)
                            scores(i + 1, blk)
                        if nxt:
                            if i == 4:
                                pe.wait_ge(ta_ready, g + 2)
                                pe.wait_ge(a_used, (g + 1) * MC)
                            for s in max_steps(i):
                                maxpass(g + 1, 1 - par, s)
                            if i == MC - 2:
                                pe.wait_ge(upd_ready, g + START)
                                rows(g + 1)
                        pe.wait_ge(p_ready, g * MC + (i + 1))
                        pe.matmul(psY[par][0:CB + 1, :], gT[:, i, :], P[:, i % 4, :], start=i == 0, stop=i == MC - 1).then_inc(pv_done, 1)
                    if nxt:
                        pe.wait_ge(row_written, g + 2)
                        scores(0, nblk)
                        scores(1, nblk)
                    pe.wait_ge(y_saved, g + 1)
                    pe.wait_ge(upd_ready, g + START)
                    pe.matmul(psQ[:, :], sumsel[:, :], Y[0:CB + 1, :], start=True, stop=True)
                    pe.matmul(psZ[:, :], wlast[:, :], Y[0:CB, :], start=True, stop=True).then_inc(z_ready, 1)

            def conv1(b):
                for r in range(NB):
                    pe.wait_ge(p1H_done, b * NB + min(r + 2, NB))
                    pe.wait_ge(p1L_done, b * NB + min(r + 2, NB))
                    if r >= 2:
                        pe.wait_ge(c1_summed, b * NB + (r - 1))
                    n = 0
                    for t in range(TAPS):
                        ky, kx = divmod(t, 3)
                        for part in (PH1, PL1):
                            last = pe.matmul(bank[r % 2][:, :], w1s[:, t, :], part[:, 8 * r + DIL * ky:8 * r + DIL * ky + 8, DIL * kx:DIL * kx + W],
                                             start=n == 0, stop=n == 2 * TAPS - 1)
                            n += 1
                    last.then_inc(c1_ready, 1)

            def spectra(b):
                pe.wait_ge(f_done, (b + 1) * NB)
                for q in range(W // 4):
                    if q >= 2:
                        pe.wait_ge((tr_act, tr_dve)[q % 2], b * 8 + q // 2)
                    plain(pe)
                    for s in range(4):
                        last = pe.matmul(bank[2 + q % 2][0:H, s * CR:(s + 1) * CR], Fc[:, 4 * q + s::W], eyecg[:, :], start=True, stop=True)
                    last.then_inc(tr_ready, 1)
                pe.wait_ge(tr_act, (b + 1) * 8)
                pe.wait_ge(tr_dve, (b + 1) * 8)
                plain(pe)
                for w in range(W):
                    last = pe.matmul(bank[4][0:CB, 0:CB], F1[:, w, 0:CB], F1[:, w, 0:CB], start=w == 0, stop=w == W - 1)
                last.then_inc(gram_ready, 1)
                for q in range(CR // 4):
                    if q >= 2:
                        if q % 2:
                            pe.wait_ge(ht_dve, b * 8 + q // 2)
                        else:
                            pe.wait_ge(ht_act, b * 9 + q // 2)
                    plain(pe)
                    for s in range(4):
                        last = pe.matmul(bank[5 + q % 2][0:W, s * 2 * KH:(s + 1) * 2 * KH], F1[:, :, 4 * q + s], hdft[:, :], start=True, stop=True)
                    last.then_inc(ht_ready, 1)
                pe.wait_ge(gram_step, b * GS + 5)
                plain(pe)
                pe.matmul(bank[4][0:CB, CB:2 * CB], gram[:, :], dmat[:, :], start=True, stop=True).then_inc(gram_step, 1)
                pe.wait_ge(ht_act, (b + 1) * 9)
                pe.wait_ge(ht_dve, (b + 1) * 8)
                for q in range(5):
                    k0, k1 = 7 * q, min(7 * q + 7, KH)
                    if q >= 2:
                        pe.wait_ge(wt_act, b * 5 + (q - 1))
                    pe.matmul(bank[q % 2][:, 0:(k1 - k0) * CR], wdft[:, :], T1[:, k0:k1, :], start=True, stop=True).then_inc(wt_ready, 1)
                pe.wait_ge(wt_act, (b + 1) * 5)
                for q in range(5):
                    k0, k1 = 8 * q, min(8 * q + 8, KH)
                    if q >= 2:
                        pe.wait_ge(r_done, b * 5 + (q - 1))
                    plain(pe)
                    for k in range(k0, k1):
                        last = pe.matmul(bank[2 + q % 2][0:MID, (k - k0) * W:(k - k0 + 1) * W], FF[0:W, k, CB:CR], ident[0:W, 0:W], start=True, stop=True)
                    last.then_inc(r_ready, 1)
                pe.wait_ge(gram_step, b * GS + 11)
                plain(pe)
                pe.matmul(bank[4][0:CB, 2 * CB:3 * CB], aexp[:, :], ident[0:CB, 0:CB], start=True, stop=True).then_inc(gram_step, 1)
                for q in range(5):
                    k0, k1 = 8 * q, min(8 * q + 8, KH)
                    pe.wait_ge(r_done, b * 5 + (q + 1))
                    if q >= 2:
                        pe.wait_ge(sg_done, b * 5 + (q - 1))
                    pe.matmul(bank[5 + q % 2][0:CB, 0:(k1 - k0) * W], w2t[:, :], RG[:, k0 * W:k1 * W], start=True, stop=True).then_inc(sg_ready, 1)
                for q in range(5):
                    k0, k1 = 8 * q, min(8 * q + 8, KH)
                    pe.wait_ge(sg_done, b * 5 + (q + 1))
                    if q >= 2:
                        pe.wait_ge(cg_used, b * 5 + (q - 1))
                    plain(pe)
                    for k in range(k0, k1):
                        gate = SG[:, k * 2 * W:(k + 1) * 2 * W]
                        last = pe.matmul(bank[q % 2][:, (k - k0) * CB:(k - k0 + 1) * CB], gate, ident[0:CB, 0:CB], start=True, stop=True)
                    last.then_inc(cg_ready, 1)

            def channel_attention(b):
                pe.wait_ge(gram_step, b * GS + 13)
                for r in range(NB):
                    if r >= 2:
                        pe.wait_ge(sq_done, b * NB + (r - 1))
                    pe.matmul(bank[2 + r % 2][:, :], att[:, :], Fc[:, r * BW:(r + 1) * BW], start=True, stop=True).then_inc(of_ready, 1)
                    if r >= 1:
                        squares(b, r - 1)
                squares(b, NB - 1)

            def squares(b, r):
                pe.wait_ge(sq_done, b * NB + (r + 1))
                if r >= 2:
                    pe.wait_ge(root_done, b * NB + (r - 1))
                pe.matmul(bank[5 + r % 2][0:CB, :], pairsum[:, :], sqv[:, r % 2, :], start=True, stop=True).then_inc(sqs_ready, 1)

            def inverse(b):
                pe.wait_ge(cg_used, (b + 1) * 5)
                for q in range(16):
                    if q >= 2:
                        pe.wait_ge((il_act, il_dve)[q % 2], b * 8 + q // 2)
                    for s in range(4):
                        last = pe.matmul(bank[q % 2][0:KH, s * 128:(s + 1) * 128], GT[:, :, 4 * q + s], iwdft[:, :], start=True, stop=True)
                    last.then_inc(il_ready, 1)
                pe.wait_ge(il_act, (b + 1) * 8)
                pe.wait_ge(il_dve, (b + 1) * 8)
                for q in range(8):
                    if q >= 2:
                        pe.wait_ge(abs_done, b * 8 + (q - 1))
                    plain(pe)
                    for s in range(8):
                        o = bank[2 + q % 2][CB:128, s * H:(s + 1) * H]
                        pe.matmul(o, U[:, :, 8 * q + s], ihdft[:, 0:H], start=True, stop=False)
                        last = pe.matmul(o, U[:, :, W + 8 * q + s], ihdft[:, H:2 * H], start=False, stop=True)
                    last.then_inc(ik_ready, 1)

            def conv2(b):
                for r in range(NR2):
                    need = min((CROWS * r + CROWS + 1) // 8 + 1, NB)
                    pe.wait_ge(p2H_done, b * NB + need)
                    pe.wait_ge(p2L_done, b * NB + need)
                    if r >= 2:
                        pe.wait_ge(c2_done, b * NR2 + (r - 1))
                    n = 0
                    for t in range(TAPS):
                        ky, kx = divmod(t, 3)
                        for wt, part in ((w3H, PH2), (w3H, PL2), (w3L, PH2)):
                            last = pe.matmul(bank[r % 2][:, 0:CROWS * HC], wt[:, t, :], part[:, CROWS * r + ky:CROWS * r + ky + CROWS, kx:kx + HC],
                                             start=n == 0, stop=n == 3 * TAPS - 1)
                            n += 1
                    last.then_inc(c2_ready, 1)

            def rows_first(b):
                pe.wait_ge(c2_done, (b + 1) * NR2)
                for q in range(17):
                    if q >= 2:
                        if q % 2:
                            pe.wait_ge(xt_dve, b * 8 + q // 2)
                        else:
                            pe.wait_ge(xt_act, b * 9 + q // 2)
                    for s in range(min(4, HC - 4 * q)):
                        last = pe.transpose(bank[2 + q % 2][0:HC, s * C:(s + 1) * C], Xc[:, 4 * q + s::HC], ident[:, :])
                    last.then_inc(xt_ready, 1)

            def resample(b):
                def up_rows(G, s):
                    pe.wait_ge(xg_done, 2 * G + 2)
                    pe.wait_ge(s1_done, G + START)
                    for c in range(2):
                        last = pe.matmul(bank[s][0:HC, c * HU:(c + 1) * HU], Xg[:, s, c, :], upm[:, :], start=True, stop=True)
                    last.then_inc(s1_ready, 1)

                def up_columns(G, s):
                    pe.wait_ge(s1_done, G + 1 + START)
                    pe.wait_ge(y_done, 2 * G + START)
                    for q in range(2):
                        pe.matmul(bank[2 + 2 * s + q][0:HK, 0:2 * HU], upm[:, q * HK:(q + 1) * HK], S1[:, s, :], start=True, stop=True).then_inc(s2_ready, 1)

                def down_columns(G, s):
                    pe.wait_ge(y_done, 2 * G + 2 + START)
                    pe.wait_ge(z_done, G + START)
                    for c in range(2):
                        for h in range(2):
                            for q in range(2):
                                last = pe.matmul(bank[6 + s][0:HK, (c * 2 + h) * W:(c * 2 + h + 1) * W],
                                                 Yt[:, s, q, c * HU + h * HK:c * HU + (h + 1) * HK], dnm[:, q, :], start=q == 0, stop=q == 1)
                    last.then_inc(s3_ready, 1)

                G0 = b * NGR
                pe.wait_ge(xt_act, (b + 1) * 9)
                pe.wait_ge(xt_dve, (b + 1) * 8)
                up_rows(G0, 0)
                up_columns(G0, 0)
                up_rows(G0 + 1, 1)
                with pe.Fori(0, NGR // 2 - 1) as j:
                    for s in range(2):
                        G = b * NGR + j * 2 + s
                        up_columns(G + 1, 1 - s)
                        up_rows(G + 2, s)
                        down_columns(G, s)
                up_columns(G0 + (NGR - 1), 1)
                down_columns(G0 + (NGR - 2), 0)
                down_columns(G0 + (NGR - 1), 1)
                pe.wait_ge(z_done, (b + 1) * NGR + START)
                for q in range(8):
                    if q >= 2:
                        pe.wait_ge((s4_act, s4_dve)[q % 2], b * 4 + q // 2)
                    for s in range(8):
                        for h in range(2):
                            last = pe.matmul(bank[q % 2][:, s * H:(s + 1) * H], Z[:, h, 8 * q + s, :], dnm[:, h, :], start=h == 0, stop=h == 1)
                    last.then_inc(s4_ready, 1)

            def keys_values(b):
                def product(b, q):
                    pe.wait_ge(kvf_done, b * NG3 + (q + 1))
                    for s in range(2):
                        last = pe.matmul(bank[4][:, 0:C], kvf[:, q % 2, s * 2 * C:s * 2 * C + C], kvf[:, q % 2, s * 2 * C + C:(s + 1) * 2 * C],
                                         start=q == 0 and s == 0, stop=q == NG3 - 1 and s == 1)
                    last.then_inc(kv_ready, 1)

                pe.wait_ge(s4_act, (b + 1) * 4)
                pe.wait_ge(s4_dve, (b + 1) * 4)
                for q in range(NG3):
                    if q >= 2:
                        pe.wait_ge(kvn_done, b * NG3 + (q - 1))
                    for s in range(2):
                        last = pe.matmul(bank[2 + q % 2][:, s * 2 * C:(s + 1) * 2 * C], X[:, (2 * q + s) * 128:(2 * q + s + 1) * 128], wkvc[:, :],
                                         start=True, stop=True)
                    last.then_inc(tok_ready, 1)
                    if q >= 2:
                        product(b, q - 2)
                product(b, NG3 - 2)
                product(b, NG3 - 1)
                pe.wait_ge(kvm_done, b + 1)
                pe.matmul(bank[5][:, 0:C], KVm[:, :], wq[:, :], start=True, stop=True).then_inc(m_ready, 1)
                pe.wait_ge(mi_done, b + 1)
                pe.matmul(bank[5][:, C:2 * C], MI[:, :], o1t[:, :], start=True, stop=True).then_inc(gt_ready, 1)

            def mlp(b):
                def second(k):
                    pe.wait_ge(u_done, b * NB + (k + 1))
                    if k >= 2:
                        pe.wait_ge(t_done, b * NB + (k - 1))
                    pe.matmul(bank[6 + k % 2][:, :], o2t[:, :], uu[:, k % 2, :], start=True, stop=True).then_inc(o2_ready, 1)

                pe.wait_ge(gt_done, b + 1)
                for k in range(NB):
                    if k >= 2:
                        pe.wait_ge(u_done, b * NB + (k - 1))
                    pe.matmul(bank[k % 2][:, :], GTm[:, :], X[:, k * BW:(k + 1) * BW], start=True, stop=True).then_inc(u_ready, 1)
                    if k >= 1:
                        second(k - 1)
                second(NB - 1)
                pe.wait_ge(t_done, (b + 1) * NB)

            def layers(b):
                conv1(b)
                spectra(b)
                channel_attention(b)
                inverse(b)
                conv2(b)
                rows_first(b)
                resample(b)
                keys_values(b)
                mlp(b)

            pe.wait_ge(w_in, 16 * len(weights))
            pe.wait_ge(consts, 1)
            pe.wait_ge(setup, SETUP)
            with pe.Fori(0, B) as b:
                prep(b)
                pe.wait_ge(ta_ready, b * NB + 1)
                pe.wait_ge(phL_done, (b + 1) * NB)
                pe.wait_ge(phH_done, (b + 1) * NB)
                for s in range(MC):
                    maxpass(b * NB, 0, s)
                pe.wait_ge(g_done, (b + 1) * NB)
                rows(b * NB)
                pe.wait_ge(thL_done, (b + 1) * NB)
                pe.wait_ge(phA_done, (b + 1) * NB)
                pe.wait_ge(row_written, b * NB + 1)
                scores(0, slice(0, BW))
                scores(1, slice(0, BW))
                with pe.Fori(0, NB // 2 - 1) as j2:
                    pair(b, j2, False)
                pair(b, NB // 2 - 1, True)
                layers(b)

        @block.scalar
        def _(act):
            def prep(b):
                for k in range(NB):
                    ck = slice(k * BW, (k + 1) * BW)
                    act.wait_ge(th_ready, b * NB + (k + 1))
                    act.activation(ThH[:, ck], psS[k % 2][:, :], ACT.Copy).then_inc(thH_done, 1)
                    act.wait_ge(ph_ready, b * NB + (k + 1))
                    act.activation(PhS[:, ck], psA[k % 2][:, :], ACT.Copy).then_inc(phH_done, 1)

            def row(g, blk):
                act.wait_ge(row_ready, g + 1)
                act.activation(ThL[CB:CB + 2, blk], psQ[CB:CB + 2, :], ACT.Copy).then_inc(row_written, 1)

            def pair(b, j2, last_pair):
                for par in range(2):
                    g = b * NB + j2 * 2 + par
                    for i in range(MC):
                        if i == MC - 1 and not (last_pair and par == 1):
                            row(g + 1, bass.ds((j2 * 2 + (par + 1)) * BW, BW))
                        act.wait_ge(pv_done, g * MC + max(i - 3, 0) + START)
                        act.wait_ge(s_ready, g * MC + (i + 1))
                        act.activation(P[:, i % 4, :], psS[i % 2][:, :], ACT.Exp).then_inc(p_ready, 1)
                    act.wait_ge(pv_done, (g + 1) * MC + START)
                    act.wait_ge(z_ready, g + START)
                    act.activation(Y[0:CB + 1, :], psY[par][0:CB + 1, :], ACT.Copy).then_inc(y_saved, 1)

            def layer1(b):
                for k in range(NB):
                    act.wait_ge(zero1, 2 * (b + 1))
                    act.wait_ge(x1_done, b * NB + (k + 1) + START)
                    act.activation(PH1[:, DIL + 8 * k:DIL + 8 * k + 8, DIL:DIL + W], Xi[:, 8 * k:8 * k + 8, :], ACT.Copy).then_inc(p1H_done, 1)

                def feature(r):
                    act.wait_ge(c1_summed, b * NB + (r + 1))
                    act.activation(Fc[:, r * BW:(r + 1) * BW], c1s[:, r % 2, :], ACT.Gelu, bias=bn1b[:, :], scale=bn1s[:, :]).then_inc(f_done, 1)

                for r in range(NB):
                    act.wait_ge(c1_ready, b * NB + (r + 1))
                    act.activation(c1t[:, r % 2, :], bank[r % 2][CB:128, :], ACT.Copy).then_inc(c1_moved, 1)
                    if r >= 1:
                        feature(r - 1)
                feature(NB - 1)
                for q in range(0, W // 4, 2):
                    act.wait_ge(tr_ready, b * 16 + (q + 1))
                    act.activation(F1[:, 4 * q:4 * q + 4, :], bank[2 + q % 2][0:H, 0:4 * CR].rearrange("p (w c) -> p w c", w=4), ACT.Copy).then_inc(tr_act, 1)
                act.wait_ge(gram_step, b * GS + 2)
                act.activation(den[:, 0:1], gdiag[:, 0:1], ACT.Sqrt, scale=float(N), bias=eps6[0:CB, :]).then_inc(gram_step, 1)
                for q in range(0, CR // 4, 2):
                    act.wait_ge(ht_ready, b * 17 + (q + 1))
                    for s in range(2):
                        last = act.activation(T1[s * W:(s + 1) * W, :, 4 * q:4 * q + 4], bank[5 + q % 2][0:W, 0:8 * KH].rearrange("p (c s k) -> p s k c", c=4, s=2)[:, s], ACT.Copy)
                    last.then_inc(ht_act, 1)
                act.wait_ge(gram_step, b * GS + 8)
                act.activation(aexp[:, :], alog[:, :], ACT.Exp, bias=amax[:, 0:1], accum_out=asum[:, 0:1]).then_inc(gram_step, 1)
                for q in range(5):
                    k0, k1 = 7 * q, min(7 * q + 7, KH)
                    act.wait_ge(wt_ready, b * 5 + (q + 1))
                    act.activation(FF[:, k0:k1, :], bank[q % 2][:, 0:(k1 - k0) * CR].rearrange("p (k c) -> p k c", c=CR), ACT.Copy).then_inc(wt_act, 1)
                for q in range(5):
                    k0, k1 = 8 * q, min(8 * q + 8, KH)
                    act.wait_ge(r_ready, b * 5 + (q + 1))
                    act.activation(RG[:, k0 * W:k1 * W], bank[2 + q % 2][0:MID, 0:(k1 - k0) * W], ACT.Gelu, bias=cgb[:, :], scale=cgs[:, :]).then_inc(r_done, 1)
                for q in range(5):
                    k0, k1 = 8 * q, min(8 * q + 8, KH)
                    act.wait_ge(sg_ready, b * 5 + (q + 1))
                    act.activation(SG[:, k0 * 2 * W:k1 * 2 * W].rearrange("p (k s l) -> p k s l", s=2, l=W), rep(bank[5 + q % 2][0:CB, 0:(k1 - k0) * W].rearrange("p (k l) -> p k l", l=W), 2, 2), ACT.Sigmoid, bias=cg2b[:, :]).then_inc(sg_done, 1)

                def root(r):
                    act.wait_ge(sqs_ready, b * NB + (r + 1))
                    if r >= 2:
                        act.wait_ge(xa_done, b * NB + (r - 1))
                    act.activation(rtv[:, r % 2, :], bank[5 + r % 2][0:CB, :], ACT.Sqrt).then_inc(root_done, 1)

                for r in range(NB):
                    act.wait_ge(of_ready, b * NB + (r + 1))
                    if r >= 2:
                        act.wait_ge(sqs_ready, b * NB + (r - 1))
                    act.activation(sqv[:, r % 2, :], bank[2 + r % 2][:, :], ACT.Square).then_inc(sq_done, 1)
                    if r >= 1:
                        root(r - 1)
                root(NB - 1)
                for q in range(0, 16, 2):
                    act.wait_ge(il_ready, b * 16 + (q + 1))
                    act.activation(U[:, 4 * q:4 * q + 4, :], bank[q % 2][0:KH, :].rearrange("p (c w) -> p c w", c=4), ACT.Copy).then_inc(il_act, 1)
                for q in range(8):
                    act.wait_ge(ik_ready, b * 8 + (q + 1))
                    if q >= 2:
                        act.wait_ge(xb_done, b * 8 + (q - 1))
                    act.activation(absv[:, q % 2, :], bank[2 + q % 2][CB:128, :], ACT.Abs).then_inc(abs_done, 1)

            def layer2(b):
                act.wait_ge(zero2, 2 * (b + 1))
                act.wait_ge(xa_done, (b + 1) * 8)
                act.wait_ge(xb_done, (b + 1) * 8)
                for k in range(NB):
                    act.activation(PH2[:, 2 + 8 * k:10 + 8 * k, 2:2 + W], Xi[:, 8 * k:8 * k + 8, :], ACT.Copy).then_inc(p2H_done, 1)
                for r in range(NR2):
                    act.wait_ge(c2_ready, b * NR2 + (r + 1))
                    act.activation(Xc[:, r * CROWS * HC:(r + 1) * CROWS * HC], bank[r % 2][:, 0:CROWS * HC], ACT.Identity, bias=b3[:, 2:3]).then_inc(c2_done, 1)
                for q in range(0, 17, 2):
                    n = min(4, HC - 4 * q)
                    act.wait_ge(xt_ready, b * 17 + (q + 1))
                    act.activation(xh(4 * q, 4 * q + n), bank[2 + q % 2][0:HC, 0:n * C].rearrange("p (w c) -> p w c", w=n), ACT.Copy).then_inc(xt_act, 1)

                def saved(G, s):
                    act.wait_ge(s1_ready, G + 1 + START)
                    act.activation(S1[:, s, :], bank[s][0:HC, 0:2 * HU], ACT.Copy).then_inc(s1_done, 1)

                def relus(G, s):
                    for q in range(2):
                        act.wait_ge(s2_ready, 2 * G + (q + 1))
                        act.wait_ge(y_done, (2 * G + (q - 1) if q else 2 * G) + START)
                        act.activation(Rl[:, q, :], bank[2 + 2 * s + q][0:HK, 0:2 * HU], ACT.Relu, scale=0.8 * GAIN).then_inc(relu_done, 1)

                G0 = b * NGR
                saved(G0, 0)
                with act.Fori(0, NGR // 2 - 1) as j:
                    for s in range(2):
                        G = b * NGR + j * 2 + s
                        saved(G + 1, 1 - s)
                        relus(G, s)
                saved(G0 + (NGR - 1), 1)
                relus(G0 + (NGR - 2), 0)
                relus(G0 + (NGR - 1), 1)
                for q in range(0, 8, 2):
                    act.wait_ge(s4_ready, b * 8 + (q + 1))
                    act.activation(Xi[:, :, 8 * q:8 * q + 8], bank[q % 2][:, :].rearrange("p (w h) -> p h w", w=8), ACT.Copy).then_inc(s4_act, 1)

            def layer3(b):
                def deviations(q):
                    act.wait_ge(ss_done, b * NG3 + (q + 1))
                    act.activation(sd3[:, q % 2, :], ss3[:, q % 2, :], ACT.Sqrt, scale=1.0 / (HD - 1)).then_inc(sd_done, 1)

                for q in range(NG3):
                    act.wait_ge(tok_ready, b * NG3 + (q + 1))
                    if q >= 2:
                        act.wait_ge(ss_done, b * NG3 + (q - 1))
                    act.activation(sq3[:, q % 2, :], bank[2 + q % 2][:, :], ACT.Square).then_inc(sq3_done, 1)
                    if q >= 1:
                        deviations(q - 1)
                deviations(NG3 - 1)

                def final(k):
                    act.wait_ge(t_done, b * NB + (k + 1))
                    act.wait_ge(out_sem[k % 2], (b * (NB // 2) + k // 2) * 16 + START)
                    act.activation(oo[:, k % 2, :], tt[:, k % 2, :], ACT.Gelu).then_inc(o_done, 1)

                for k in range(NB):
                    act.wait_ge(u_ready, b * NB + (k + 1))
                    if k >= 2:
                        act.wait_ge(o2_ready, b * NB + (k - 1))
                    act.activation(uu[:, k % 2, :], bank[k % 2][:, :], ACT.Gelu).then_inc(u_done, 1)
                    if k >= 1:
                        final(k - 1)
                final(NB - 1)

            act.wait_ge(w_in, 16 * len(weights))
            act.wait_ge(setup, 2)
            act.activation(bn1s[:, :], bn[:, 3:4], ACT.Sqrt, bias=eps5[0:CB, :]).then_inc(setup, 1)
            act.activation(cgs[:, :], cgp[:, 4:5], ACT.Sqrt, bias=eps5[0:MID, :]).then_inc(setup, 1)
            act.wait_ge(setup, 4)

            with act.Fori(0, B) as b:
                prep(b)
                row(b * NB, slice(0, BW))
                with act.Fori(0, NB // 2 - 1) as j2:
                    pair(b, j2, False)
                pair(b, NB // 2 - 1, True)
                layer1(b)
                layer2(b)
                layer3(b)

        @block.vector
        def _(v):
            def prep(b):
                v.memset(gT[:, :, CB:CB + 1], 1.0)
                v.memset(PhA[CB:CB + 2, :].bitcast(f32), -1.0)
                for k in range(NB):
                    ck = slice(k * BW, (k + 1) * BW)
                    v.wait_ge(thH_done, b * NB + (k + 1))
                    v.tensor_tensor(ThL[0:CB, ck], psS[k % 2][0:CB, :], ThH[0:CB, ck].bitcast(f32), ALU.subtract).then_inc(thL_done, 1)
                    v.wait_ge(phH_done, b * NB + (k + 1))
                    v.tensor_tensor(PhS[CB:128, ck], psA[k % 2][CB:128, :], PhS[CB:128, ck].bitcast(f32), ALU.subtract).then_inc(phL_done, 1)
                    v.wait_ge(g_ready, b * NB + (k + 1))
                    v.tensor_copy(gT[:, 4 * k:4 * k + 4, 0:CB], psY[k % 2][:, 0:4 * CB].rearrange("p (s k) -> p s k", s=4)).then_inc(g_done, 1)

            def maxes(g):
                for s in range(MC):
                    v.wait_ge(a_ready, g * MC + (s + 1) + START)
                    v.reduce_max(mx8[:, s // NB, s % NB:s % NB + 1], psA[s % 2][:, :], AX.X).then_inc(a_used, 1)
                v.wait_ge(a_used, (g + 1) * MC)
                v.reduce_max(mxn[:, :], mx8[:, :, :], AX.X).then_inc(mx_step, 1)
                v.wait_ge(mx_step, g * 2 + 1)
                v.tensor_copy(mxr[:, :], mxn[:, :]).then_inc(mx_step, 1)
                v.wait_ge(mx_step, g * 2 + 2)
                v.tensor_copy(mxHL[:, :, 0], mxr[:, :].bitcast(f32))
                v.tensor_tensor(mxHL[:, :, 1], mxn[:, :], mxr[:, :].bitcast(f32), ALU.subtract).then_inc(mx_ready, 1)
                v.wait_ge(mx_ready, g + 1)

            def update(g):
                v.wait_ge(z_ready, g + 1 + START)
                v.reciprocal(rec[:, :], psQ[:, :]).then_inc(rec_ready, 1)
                v.wait_ge(x1_done, g + START)
                v.wait_ge(rec_ready, g + 1)
                v.tensor_tensor(upd[:, :], psZ[:, :], rec[:, :], ALU.mult).then_inc(upd_ready, 1)

            def pair(b, j2, last_pair):
                for par in range(2):
                    g = b * NB + j2 * 2 + par
                    if not (last_pair and par == 1):
                        maxes(g + 1)
                    update(g)

            def layer1(b):
                for k in range(NB):
                    v.wait_ge(p1H_done, b * NB + (k + 1))
                    r = slice(DIL + 8 * k, DIL + 8 * k + 8)
                    v.tensor_tensor(PL1[:, r, DIL:DIL + W], Xi[:, 8 * k:8 * k + 8, :], PH1[:, r, DIL:DIL + W].bitcast(f32), ALU.subtract).then_inc(p1L_done, 1)
                for r in range(NB):
                    v.wait_ge(c1_moved, b * NB + (r + 1))
                    if r >= 2:
                        v.wait_ge(f_done, b * NB + (r - 1))
                    v.tensor_tensor(c1s[:, r % 2, :], bank[r % 2][0:CB, :], c1t[:, r % 2, :], ALU.add).then_inc(c1_summed, 1)
                for q in range(1, W // 4, 2):
                    v.wait_ge(tr_ready, b * 16 + (q + 1))
                    v.tensor_copy(F1[:, 4 * q:4 * q + 4, :], bank[2 + q % 2][0:H, 0:4 * CR].rearrange("p (w c) -> p w c", w=4)).then_inc(tr_dve, 1)
                v.wait_ge(gram_ready, b + 1)
                v.tensor_copy(gram[:, :], bank[4][0:CB, 0:CB]).then_inc(gram_step, 1)
                v.wait_ge(gram_step, b * GS + 1)
                v.tensor_tensor_reduce(out=dmat[:, :], in0=gram[:, :], in1=ident[0:CB, 0:CB], scale=1.0, scalar=0.0, op0=ALU.mult, op1=ALU.add,
                                       accum_out=gdiag[:, 0:1]).then_inc(gram_step, 1)
                v.wait_ge(gram_step, b * GS + 3)
                v.reciprocal(rden[:, 0:1], den[:, 0:1]).then_inc(gram_step, 1)
                v.wait_ge(gram_step, b * GS + 4)
                v.tensor_scalar(dmat[:, :], ident[0:CB, 0:CB], rden[:, 0:1], None, ALU.mult)
                v.tensor_scalar(rden[:, 1:2], rden[:, 0:1], tauc[:, 0:1], float(N), ALU.mult, ALU.mult).then_inc(gram_step, 1)
                for q in range(1, CR // 4, 2):
                    v.wait_ge(ht_ready, b * 17 + (q + 1))
                    for s in range(2):
                        last = v.tensor_copy(T1[s * W:(s + 1) * W, :, 4 * q:4 * q + 4], bank[5 + q % 2][0:W, 0:8 * KH].rearrange("p (c s k) -> p s k c", c=4, s=2)[:, s])
                    last.then_inc(ht_dve, 1)
                v.wait_ge(gram_step, b * GS + 6)
                v.scalar_tensor_tensor(out=alog[:, :], in0=bank[4][0:CB, CB:2 * CB], scalar=rden[:, 1:2], in1=headneg[:, :], op0=ALU.mult, op1=ALU.add).then_inc(gram_step, 1)
                v.wait_ge(gram_step, b * GS + 7)
                v.tensor_reduce(amax[:, 0:1], alog[:, :], AX.X, ALU.max, negate=True).then_inc(gram_step, 1)
                v.wait_ge(gram_step, b * GS + 9)
                v.reciprocal(asum[:, 1:2], asum[:, 0:1]).then_inc(gram_step, 1)
                v.wait_ge(gram_step, b * GS + 10)
                v.tensor_scalar(aexp[:, :], aexp[:, :], asum[:, 1:2], None, ALU.mult).then_inc(gram_step, 1)
                v.wait_ge(gram_step, b * GS + 12)
                v.tensor_copy(att[:, 0:CB], bank[4][0:CB, 2 * CB:3 * CB]).then_inc(gram_step, 1)
                v.wait_ge(wt_act, (b + 1) * 5)
                for q in range(5):
                    k0, k1 = 8 * q, min(8 * q + 8, KH)
                    v.wait_ge(cg_ready, b * 5 + (q + 1))
                    v.tensor_tensor(GT[:, k0:k1, :], FF[:, k0:k1, 0:CB], bank[q % 2][:, 0:(k1 - k0) * CB].rearrange("p (k c) -> p k c", c=CB), ALU.mult).then_inc(cg_used, 1)
                for r in range(NB):
                    v.wait_ge(root_done, b * NB + (r + 1))
                    ck = slice(r * BW, (r + 1) * BW)
                    v.tensor_tensor(X[0:CB, ck], X[0:CB, ck], rtv[:, r % 2, :], ALU.add).then_inc(xa_done, 1)
                for q in range(1, 16, 2):
                    v.wait_ge(il_ready, b * 16 + (q + 1))
                    v.tensor_copy(U[:, 4 * q:4 * q + 4, :], bank[q % 2][0:KH, :].rearrange("p (c w) -> p c w", c=4)).then_inc(il_dve, 1)
                for q in range(8):
                    v.wait_ge(abs_done, b * 8 + (q + 1))
                    xs = Xi[CB:128, :, 8 * q:8 * q + 8]
                    v.tensor_tensor(xs, xs, absv[:, q % 2, :].rearrange("p (w h) -> p h w", w=8), ALU.add).then_inc(xb_done, 1)

            def layer2(b):
                v.wait_ge(xa_done, (b + 1) * 8)
                v.wait_ge(xb_done, (b + 1) * 8)
                for k in range(NB):
                    v.wait_ge(p2H_done, b * NB + (k + 1))
                    r = slice(2 + 8 * k, 10 + 8 * k)
                    v.tensor_tensor(PL2[:, r, 2:2 + W], Xi[:, 8 * k:8 * k + 8, :], PH2[:, r, 2:2 + W].bitcast(f32), ALU.subtract).then_inc(p2L_done, 1)
                for q in range(1, 17, 2):
                    v.wait_ge(xt_ready, b * 17 + (q + 1))
                    v.tensor_copy(xh(4 * q, 4 * q + 4), bank[2 + q % 2][0:HC, :].rearrange("p (w c) -> p w c", w=4)).then_inc(xt_dve, 1)

                def leaky(G, s):
                    for q in range(2):
                        v.wait_ge(relu_done, 2 * G + (q + 1))
                        v.wait_ge(s3_ready, G + START)
                        v.scalar_tensor_tensor(out=Yt[:, s, q, :], in0=bank[2 + 2 * s + q][0:HK, 0:2 * HU], scalar=0.2 * GAIN, in1=Rl[:, q, :],
                                               op0=ALU.mult, op1=ALU.add).then_inc(y_done, 1)

                def keep(G, s, c):
                    v.wait_ge(s3_ready, G + 1 + START)
                    v.tensor_copy(Z[:, :, :, c], bank[6 + s][0:HK, 0:4 * W].rearrange("p (c q w) -> p q w c", c=2, q=2)).then_inc(z_done, 1)

                G0 = b * NGR
                leaky(G0, 0)
                with v.Fori(0, NGR // 2 - 1) as j:
                    for s in range(2):
                        G = b * NGR + j * 2 + s
                        leaky(G + 1, 1 - s)
                        keep(G, s, bass.ds((j * 2 + s) * 2, 2))
                leaky(G0 + (NGR - 1), 1)
                keep(G0 + (NGR - 2), 0, slice(C - 4, C - 2))
                keep(G0 + (NGR - 1), 1, slice(C - 2, C))
                for q in range(1, 8, 2):
                    v.wait_ge(s4_ready, b * 8 + (q + 1))
                    v.tensor_copy(Xi[:, :, 8 * q:8 * q + 8], bank[q % 2][:, :].rearrange("p (w h) -> p h w", w=8)).then_inc(s4_dve, 1)

            def layer3(b):
                def normalise(q):
                    s = q % 2
                    v.wait_ge(sd_done, b * NG3 + (q + 1))
                    v.tensor_scalar_add(sd3[:, s, :], sd3[:, s, :], EPS_BN).then_inc(rs_step, 1)
                    v.wait_ge(rs_step, b * 2 * NG3 + (2 * q + 1))
                    v.reciprocal(rs3[:, s, :], sd3[:, s, :]).then_inc(rs_step, 1)
                    v.wait_ge(rs_step, b * 2 * NG3 + (2 * q + 2))
                    if q >= 2:
                        v.wait_ge(kv_scaled, b * NG3 + (q - 1))
                    v.tensor_tensor(kvn[:, s, :].rearrange("p (g d) -> p g d", d=HD), bank[2 + s][:, :].rearrange("p (g d) -> p g d", d=HD),
                                    rep(rs3[:, s, :], 2, HD), ALU.mult).then_inc(kvn_done, 1)

                for q in range(NG3):
                    v.wait_ge(sq3_done, b * NG3 + (q + 1))
                    v.reduce_sum(ss3[:, q % 2, :], sq3[:, q % 2, :].rearrange("p (g d) -> p g d", d=HD), AX.X).then_inc(ss_done, 1)
                    if q >= 1:
                        normalise(q - 1)
                normalise(NG3 - 1)
                v.wait_ge(kv_ready, (b + 1) * NG3)
                v.tensor_tensor(KVm[:, :], bank[4][:, 0:C], headm[:, :], ALU.mult).then_inc(kvm_done, 1)
                v.wait_ge(m_ready, b + 1)
                v.tensor_tensor(MI[:, :], bank[5][:, 0:C], ident[:, :], ALU.add).then_inc(mi_done, 1)
                v.wait_ge(gt_ready, b + 1)
                v.tensor_copy(GTm[:, :], bank[5][:, C:2 * C]).then_inc(gt_done, 1)
                for k in range(NB):
                    v.wait_ge(o2_ready, b * NB + (k + 1))
                    v.wait_ge(o_done, b * NB + max(k - 1, 0) + START)
                    v.tensor_tensor(tt[:, k % 2, :], bank[6 + k % 2][:, :], X[:, k * BW:(k + 1) * BW], ALU.add).then_inc(t_done, 1)

            v.memset(eps5[:, :], EPS_BN).then_inc(setup, 1)
            v.memset(eps6[:, :], 1e-6).then_inc(setup, 1)
            v.wait_ge(w_in, 16 * len(weights))
            v.wait_ge(setup, 4)
            v.reciprocal(den[:, 0:1], bn1s[:, :])
            v.reciprocal(den[0:MID, 1:2], cgs[:, :]).then_inc(setup, 1)
            v.wait_ge(setup, 5)
            v.tensor_scalar(bn1s[:, :], den[:, 0:1], bn[:, 0:1], None, ALU.mult)
            v.tensor_scalar(cgs[:, :], den[0:MID, 1:2], cgp[:, 1:2], None, ALU.mult)
            v.tensor_tensor(rden[0:MID, 0:1], cgp[:, 0:1], cgp[:, 3:4], ALU.subtract).then_inc(setup, 1)
            v.wait_ge(setup, 6)
            v.tensor_tensor(amax[:, 0:1], bn[:, 2:3], bn1s[:, :], ALU.mult)
            v.tensor_tensor(amax[0:MID, 1:2], rden[0:MID, 0:1], cgs[:, :], ALU.mult).then_inc(setup, 1)
            v.wait_ge(setup, 7)
            v.tensor_tensor(bn1b[:, :], bn[:, 1:2], amax[:, 0:1], ALU.subtract)
            v.tensor_tensor(cgb[:, :], cgp[:, 2:3], amax[0:MID, 1:2], ALU.add)
            v.tensor_tensor(b3[:, 2:3], b3[:, 0:1], b3[:, 1:2], ALU.add)
            v.tensor_scalar_mul(upm[:, :], upm[:, :], 2.0)
            v.tensor_copy(w1s[:, :, 0:CB], w1[:, :, :])
            v.tensor_copy(w3H[:, :, :], w3[:, :, :])
            v.reduce_sum(wkm[:, :], wkv[:, :].rearrange("p (g d) -> p g d", d=HD), AX.X).then_inc(setup, 1)
            v.wait_ge(setup, 8)
            v.tensor_tensor(w1s[:, :, CB:2 * CB], w1[:, :, :], w1s[:, :, 0:CB].bitcast(f32), ALU.subtract)
            v.tensor_tensor(w3L[:, :, :], w3[:, :, :], w3H[:, :, :].bitcast(f32), ALU.subtract)
            v.tensor_scalar_mul(wkm[:, :], wkm[:, :], 1.0 / HD).then_inc(setup, 1)
            v.wait_ge(setup, 9)
            v.tensor_tensor(wkvc[:, :].rearrange("p (g d) -> p g d", d=HD), wkv[:, :].rearrange("p (g d) -> p g d", d=HD),
                            rep(wkm[:, :], 2, HD), ALU.subtract).then_inc(setup, 3)

            with v.Fori(0, B) as b:
                prep(b)
                maxes(b * NB)
                plain(v)
                with v.Fori(0, NB // 2 - 1) as j2:
                    pair(b, j2, False)
                pair(b, NB // 2 - 1, True)
                layer1(b)
                layer2(b)
                layer3(b)

        @block.gpsimd
        def _(pool):
            for s in started:
                pool.nop().then_inc(s, START)
            pool.nop().then_inc(consts, 1)

            def pair(b, j2, last_pair):
                for par in range(2):
                    g = b * NB + j2 * 2 + par
                    if not (last_pair and par == 1):
                        pool.wait_ge(a_ready, g * MC + START)
                        plain(pool)
                        pool.tensor_copy(TA[:, 1 - par, :], ThH[0:CB, bass.ds((j2 * 2 + (par + 1)) * BW, BW)]).then_inc(ta_ready, 1)
                    blk = bass.ds((j2 * 2 + par) * BW, BW)
                    pool.wait_ge(upd_ready, g + 1 + START)
                    pool.tensor_tensor(X[:, blk], X[:, blk], upd[:, :], ALU.add).then_inc(x1_done, 1)

            with pool.Fori(0, B) as b:
                pool.wait_ge(thH_done, b * NB + 1)
                plain(pool)
                pool.tensor_copy(TA[:, 0, :], ThH[0:CB, 0:BW]).then_inc(ta_ready, 1)
                for k in range(NB):
                    ck = slice(k * BW, (k + 1) * BW)
                    pool.wait_ge(phH_done, b * NB + (k + 1))
                    plain(pool)
                    pool.tensor_copy(PhA[0:CB, ck], PhS[0:CB, ck]).then_inc(phA_done, 1)
                plain(pool)
                with pool.Fori(0, NB // 2 - 1) as j2:
                    pair(b, j2, False)
                pair(b, NB // 2 - 1, True)
                pool.wait_ge(upd_ready, (b + 1) * NB + START)
                for part in (PH1, PL1):
                    plain(pool)
                    pool.memset(part[:, :, :].bitcast(f32), 0.0).then_inc(zero1, 1)
                pool.wait_ge(c1_ready, (b + 1) * NB)
                for part in (PH2, PL2):
                    plain(pool)
                    pool.memset(part[:, :, :].bitcast(f32), 0.0).then_inc(zero2, 1)
                pool.wait_ge(xt_act, (b + 1) * 9)
                pool.wait_ge(xt_dve, (b + 1) * 8)
                plain(pool)
                with pool.Fori(0, NGR // 2) as j:
                    for s in range(2):
                        pool.wait_ge(s1_ready, b * NGR + j * 2 + START)
                        for part, w0 in ((XhA, 0), (XhB, N // C)):
                            plain(pool)
                            pool.tensor_copy(Xg[:, s, :, w0:w0 + part.shape[1]], part[:, :, bass.ds((j * 2 + s) * 2, 2)].rearrange("p w c -> p c w")).then_inc(xg_done, 1)
                w_, b_ = [rep(m[:, :], 1, 2) for m in (lnw, lnb)]
                for q in range(NG3):
                    s = q % 2
                    pool.wait_ge(kvn_done, b * NG3 + (q + 1))
                    if q >= 2:
                        pool.wait_ge(kv_ready, b * NG3 + (q - 1))
                    two = kvf[:, s, :].rearrange("p (s n) -> p s n", s=2)
                    pool.tensor_tensor(two, kvn[:, s, :].rearrange("p (s n) -> p s n", s=2), w_, ALU.mult).then_inc(kv_scaled, 1)
                    pool.wait_ge(kv_scaled, b * NG3 + (q + 1))
                    pool.tensor_tensor(two, two, b_, ALU.add).then_inc(kvf_done, 1)


def host(inp):
    z = {}
    z["x"] = np.asarray(inp["x"])
    t = np.asarray(inp["L0_conv_w_theta"]).T
    z["wth2"] = np.concatenate([t, t], 1)
    t = np.asarray(inp["L0_conv_w_phi"]).T
    z["wph2"] = np.concatenate([t, t], 1)
    z["wg"] = np.asarray(inp["L0_conv_w_g"]).T
    z["wlast"] = np.asarray(inp["L0_conv_w_last"]).T
    s = np.zeros((CB + 1, 128), np.float32)
    s[CB] = 1
    z["sumsel"] = s
    z["ident"] = np.eye(128, dtype=np.float32)
    g = lambda n: np.asarray(inp[n])
    z["w1"] = g("L1_conv_conv_w").reshape(CB, C, TAPS).transpose(1, 2, 0)
    z["bn"] = np.stack([g("L1_conv_bn1_" + k) for k in "gbmv"], 1)
    z["cgp"] = np.stack([g("L1_conv_cg1_b")] + [g("L1_conv_cgbn_" + k) for k in "gbmv"], 1)
    z["cg2b"] = g("L1_conv_cg2_b")[:, None]
    z["tauc"] = np.repeat(g("L1_conv_tau").reshape(8), 8)[:, None]
    z["eyecg"] = np.concatenate([np.eye(CB, dtype=np.float32), g("L1_conv_cg1_w")[:, :, 0, 0].T], 1)
    z["w2t"] = g("L1_conv_cg2_w")[:, :, 0, 0].T
    head = np.kron(np.eye(8), np.ones((8, 8)))
    z["headneg"] = np.where(head > 0, 0.0, -1e30)
    z["att"] = np.concatenate([head * 0, head / 8], 1)
    z["pairsum"] = np.concatenate([np.eye(CB), np.eye(CB)], 0)
    ang = 2 * np.pi * np.outer(np.arange(W), np.arange(W)) / W
    co, si = np.cos(ang), np.sin(ang)
    z["hdft"] = np.concatenate([co[:, :KH], si[:, :KH]], 1)
    z["wdft"] = np.block([[co, si], [-si, co]])
    z["iwdft"] = np.block([[co, -si], [si, co]])
    a = np.full(KH, 2.0); a[0] = a[-1] = 1
    z["ihdft"] = np.concatenate([co[:KH] * a[:, None], si[:KH] * a[:, None]], 1) / N
    z["w3"] = g("L2_conv_w").reshape(C, C, TAPS).transpose(1, 2, 0)
    z["b3"] = np.stack([g("L2_conv_b_conv"), g("L2_conv_bias"), np.zeros(C, np.float32)], 1)
    f = g("L2_conv_up_filter")
    up = np.zeros((HC, HU), np.float32)
    for i in range(HC):
        for t in range(12):
            if 0 <= 2 * i - 2 + t < HU:
                up[i, 2 * i - 2 + t] = f[t]
    z["upm"] = up
    f = g("L2_conv_down_filter")
    dn = np.zeros((HU, H), np.float32)
    for j in range(H):
        for t in range(12):
            dn[2 * j + t, j] = f[11 - t]
    z["dnm"] = dn.reshape(2, HK, H).transpose(1, 0, 2)
    qkv = g("L3_conv_qkv_w").reshape(HEADS, 3, HD, C)
    z["wq"] = qkv[:, 0].reshape(C, C)
    z["wkv"] = np.concatenate([qkv[:, 1].reshape(C, C), qkv[:, 2].reshape(C, C)], 0).T
    z["o1t"], z["o2t"] = g("L3_conv_o1_w").T, g("L3_conv_o2_w").T
    for k, n in (("lnw", "w"), ("lnb", "b")):
        row = np.concatenate([g("L3_conv_kln_" + n).reshape(C), g("L3_conv_vln_" + n).reshape(C)])
        z[k] = np.broadcast_to(row, (128, 2 * C))
    z["headm"] = np.kron(np.eye(HEADS), np.ones((HD, HD))) / N
    return {k: np.ascontiguousarray(v, dtype=np.float32) for k, v in z.items()}


def kernel(**inputs):
    import concourse.bacc as bacc
    from concourse import mybir as _mybir
    from concourse.bass_utils import run_bass_kernel_spmd

    nc = bacc.Bacc("TRN2", target_bir_lowering=False, num_devices=1)
    arrays = host(inputs)
    T = {k: nc.dram_tensor(k, v.shape, _mybir.dt.float32, kind="ExternalInput").ap() for k, v in arrays.items()}
    out = nc.dram_tensor("out", (B, C, H, W), _mybir.dt.float32, kind="ExternalOutput").ap()
    build(nc, T, out)
    r = run_bass_kernel_spmd(nc, [arrays], core_ids=[0])
    return r.results[0]["out"]
```

```python
import concourse.bass as bass
from concourse import mybir
from contextlib import ExitStack
import numpy as np

B, C, H, W = 8, 128, 64, 64
N = H * W
CB = 64
BW = 512
ROW_STEP = 27
MAX_LAG = 2
Z_STEP = 2
NB = N // BW
MC = N // 128
TAPS = 9
MID = 4
CR = CB + MID
KH = W // 2 + 1
DIL = 3
HP1 = H + 2 * DIL
HP2 = H + 4
HC = H + 2
HU = 2 * HC + 6
HK = HU // 2
CROWS = 6
NR2 = HC // CROWS
HEADS, HD = 8, 16
EPS_BN = 1e-5
GAIN = float(np.sqrt(2.0))
NG3 = N // 256
NGR = C // 2
GS = 13
SETUP = 12
START = 4


def rep(ap, dim, n):
    shape = list(ap.unsqueeze(dim).shape)
    shape[dim] = n
    return ap.unsqueeze(dim).broadcast_to(shape)


def build(nc, T, out):
    f32, f32r = mybir.dt.float32, mybir.dt.float32r
    ALU, ACT, AX = mybir.AluOpType, mybir.ActivationFunctionType, mybir.AxisListType
    ctx = ExitStack()
    with ctx:
        def sb(name, shape, dt=f32):
            return ctx.enter_context(nc.sbuf_tensor(name + "_sb", shape, dt))

        def sem(name):
            return ctx.enter_context(nc.semaphore(name))

        x_v = T["x"].rearrange("b c h w -> b c (h w)")
        out_v = out.rearrange("b c h w -> b c (h w)")

        X = sb("X", [C, N])
        Xi = X[:, :].rearrange("p (h w) -> p h w", h=H)
        ident = sb("ident", [128, 128])
        wth2, wph2, wg = sb("wth2", [C, 128]), sb("wph2", [C, 128]), sb("wg", [C, CB])
        wlast, sumsel = sb("wlast", [CB, C]), sb("sumsel", [CB + 1, 128])
        w1s = sb("w1s", [C, TAPS, 2 * CB], f32r)
        bn, bn1s, bn1b = sb("bn", [CB, 4]), sb("bn1s", [CB, 1]), sb("bn1b", [CB, 1])
        cgp, cgs, cgb = sb("cgp", [MID, 5]), sb("cgs", [MID, 1]), sb("cgb", [MID, 1])
        eps5, eps6 = sb("eps5", [128, 1]), sb("eps6", [128, 1])
        cg2b, tauc = sb("cg2b", [CB, 1]), sb("tauc", [CB, 1])
        eyecg, w2t = sb("eyecg", [CB, CR]), sb("w2t", [MID, CB])
        headneg, att, pairsum = sb("headneg", [CB, CB]), sb("att", [CB, 2 * CB]), sb("pairsum", [128, CB])
        hdft, wdft, iwdft, ihdft = sb("hdft", [H, 2 * KH]), sb("wdft", [128, 128]), sb("iwdft", [128, 128]), sb("ihdft", [KH, 2 * H])
        gram, gdiag, den, rden, dmat, alog, amax, aexp, asum = [sb(n, [CB, k]) for n, k in (
            ("gram", CB), ("gdiag", CB), ("den", 4), ("rden", 4), ("dmat", CB), ("alog", CB), ("amax", 4), ("aexp", CB), ("asum", 4))]
        w3H, w3L = sb("w3H", [C, TAPS, C], f32r), sb("w3L", [C, TAPS, C], f32r)
        b3, upm, dnm = sb("b3", [C, 3]), sb("upm", [HC, HU]), sb("dnm", [HK, 2, H])
        upH, upL = sb("upH", [HC, HU], f32r), sb("upL", [HC, HU], f32r)
        wkvc, wkm = sb("wkvc", [C, 2 * C]), sb("wkm", [C, 2 * HEADS])
        wq, o1t, o2t = sb("wq", [C, C]), sb("o1t", [C, C]), sb("o2t", [C, C])
        lncol, lnrow, headm = sb("lncol", [C, 3]), sb("lnrow", [128, 2, C]), sb("headm", [C, C])
        KVm, MI, GTm, kvt = sb("KVm", [C, C]), sb("MI", [C, C]), sb("GTm", [C, C]), sb("kvt", [C, 2, C])
        kvn = sb("kvn", [128, 2, 2, 2 * C + 1])
        onesq = sb("onesq", [128, 128])

        ARENA = 168 * 1024
        arena_at = -(-nc.sbuf_base // 64) * 64

        def place(name, at, shape, dt=f32):
            size = -(-int(np.prod(shape[1:])) * 4 // 64) * 64
            assert at + size <= ARENA, name
            return nc.alloc_sbuf_tensor_at(name, shape, dt, offset=arena_at + at), at + size

        ThH, at = place("ThH", 0, [128, N], f32r)
        PhS, at = place("PhS", at, [128, N], f32r)
        ThL, at = place("ThL", at, [CB + 2, N], f32r)
        PhA, at = place("PhA", at, [CB + 2, N], f32r)
        TA, at = place("TA", at, [CB, 2, BW], f32r)
        gH, at = place("gH", at, [128, MC, CB + 1], f32r)
        gL, at = place("gL", at, [128, MC, CB + 1], f32r)
        P, at = place("P", at, [128, 4, BW])
        PH, at = place("PH", at, [128, 4, BW], f32r)
        PL, at = place("PL", at, [128, 4, BW], f32r)
        Y, at = place("Y", at, [128, BW])
        rec, at = place("rec", at, [128, BW])
        upd, at = place("upd", at, [128, BW])
        mx8, at = place("mx8", at, [128, 4, NB])
        mxn, at = place("mxn", at, [128, 4])
        mxr, at = place("mxr", at, [128, 4], f32r)
        mxHL, at = place("mxHL", at, [128, 4, 2])

        PH1, at = place("PH1", 0, [128, HP1, HP1], f32r)
        PL1, at = place("PL1", at, [128, HP1, HP1], f32r)
        c1_at = at
        c1t, at = place("c1t", at, [CB, 2, BW])
        c1s, at = place("c1s", at, [CB, 2, BW])
        Fc, at = place("Fc", at, [CB, N])
        F1, at = place("F1", at, [H, W, CR])
        T1, at = place("T1", at, [128, KH, CR])
        FF, at = place("FF", at, [128, KH, CR])
        SG, at = place("SG", at, [CB, KH, 2, W])
        RG, at = place("RG", at, [MID, KH * W])
        GT, at = place("GT", at, [128, KH, CB])
        U, _ = place("U", c1_at, [KH, CB, 128])
        sqv, at = place("sqv", at, [128, 2, BW])
        rtv, at = place("rtv", at, [CB, 2, BW])
        absv, at = place("absv", at, [128, 2, BW])

        PH2, at = place("PH2", 0, [128, HP2, HP2], f32r)
        PL2, at = place("PL2", at, [128, HP2, HP2], f32r)
        Xh, at = place("Xh", at, [HC, HC, C])
        Xc, _ = place("Xc", at, [128, HC * HC])
        Z, at = place("Z", at, [HK, 2, W, C])
        Xg, at = place("Xg", at, [HC, 2, 2, HC])
        S1H, at = place("S1H", at, [HC, 2, 2 * HU], f32r)
        S1L, at = place("S1L", at, [HC, 2, 2 * HU], f32r)
        Rl, at = place("Rl", at, [HK, 2, 2 * HU])
        Yt, at = place("Yt", at, [HK, 2, 2, 2 * HU])

        sq3, at = place("sq3", 112 * 1024, [128, 2, BW])
        ss3, at = place("ss3", at, [128, 2, 32])
        sd3, at = place("sd3", at, [128, 2, 32])
        rs3, at = place("rs3", at, [128, 2, 32])
        uu, at = place("uu", at, [128, 2, BW])
        tt, at = place("tt", at, [128, 2, BW])
        oo, at = place("oo", at, [128, 2, BW])

        w1, at = place("w1", 0, [C, TAPS, CB])
        w3, at = place("w3", at, [C, TAPS, C])
        wkv, at = place("wkv", at, [C, 2 * C])

        bank = [ctx.enter_context(nc.psum_tensor(f"bank{i}", [128, BW], f32)) for i in range(8)]
        psS, psA, psY, psZ, psQ = bank[0:2], bank[3:5], (bank[2], bank[5]), bank[6], bank[7]

        x_in = [sem(f"x_in{k}") for k in range(NB)]
        w_in = sem("w_in")
        ups = sem("ups")
        consts = sem("consts")
        th_ready, ph_ready, g_ready = sem("th_ready"), sem("ph_ready"), sem("g_ready")
        thH_done, phH_done, thL_done, phL_done, phA_done, g_done = [sem(n) for n in ("thH_done", "phH_done", "thL_done", "phL_done", "phA_done", "g_done")]
        ta_ready, a_ready, a_used, mx_ready, row_ready, row_written = [sem(n) for n in ("ta_ready", "a_ready", "a_used", "mx_ready", "row_ready", "row_written")]
        s_ready, exp_done, ph_done, pl_even, pl_odd, pv_done, y_saved, z_ready, upd_ready, x1_done = [sem(n) for n in ("s_ready", "exp_done", "ph_done", "pl_even", "pl_odd", "pv_done", "y_saved", "z_ready", "upd_ready", "x1_done")]
        mx_step, rec_ready, gh_done = sem("mx_step"), sem("rec_ready"), sem("gh_done")
        names = """setup zero1 p1H_done p1L_done c1_ready c1_moved c1_summed f_done tr_ready tr_act tr_dve
            gram_ready gram_step ht_ready ht_act ht_dve wt_ready wt_act r_ready r_done sg_ready sg_done cg_ready cg_used
            of_ready sq_done sqs_ready root_done xa_done il_ready il_act il_dve ik_ready abs_done xb_done
            zero2 p2H_done p2L_done c2_ready c2_done xt_ready xt_act xt_dve xg_done s1_ready s1h_done s1_done s2_ready relu_done
            y_done s3_ready z_done s4_ready s4_act s4_dve
            tok_ready sq3_done ss_done sd_done rs_step kvn_done kv_step kv_ready kvm_done m_ready mi_done gt_ready gt_done
            u_ready u_done o2_ready t_done o_done""".split()
        (setup, zero1, p1H_done, p1L_done, c1_ready, c1_moved, c1_summed, f_done, tr_ready, tr_act, tr_dve,
         gram_ready, gram_step, ht_ready, ht_act, ht_dve, wt_ready, wt_act, r_ready, r_done, sg_ready, sg_done, cg_ready, cg_used,
         of_ready, sq_done, sqs_ready, root_done, xa_done, il_ready, il_act, il_dve, ik_ready, abs_done, xb_done,
         zero2, p2H_done, p2L_done, c2_ready, c2_done, xt_ready, xt_act, xt_dve, xg_done, s1_ready, s1h_done, s1_done, s2_ready, relu_done,
         y_done, s3_ready, z_done, s4_ready, s4_act, s4_dve,
         tok_ready, sq3_done, ss_done, sd_done, rs_step, kvn_done, kv_step, kv_ready, kvm_done, m_ready, mi_done, gt_ready, gt_done,
         u_ready, u_done, o2_ready, t_done, o_done) = [sem(n) for n in names]
        out_sem = [sem("out0"), sem("out1")]
        started = [pv_done, pl_even, pl_odd, z_ready, x1_done, a_ready, upd_ready, s1_done, y_done, z_done, s3_ready, s1_ready, o_done, *out_sem]
        block = ctx.enter_context(nc.Block())

        def plain(engine):
            engine.nop(nofuse=True)

        weights = [(ident, "ident"), (wth2, "wth2"), (wph2, "wph2"), (wg, "wg"), (wlast, "wlast"), (sumsel, "sumsel"),
                   (w1, "w1"), (bn, "bn"), (cgp, "cgp"), (cg2b, "cg2b"), (tauc, "tauc"), (eyecg, "eyecg"), (w2t, "w2t"),
                   (headneg, "headneg"), (att, "att"), (pairsum, "pairsum"), (hdft, "hdft"), (wdft, "wdft"), (iwdft, "iwdft"),
                   (ihdft, "ihdft"), (w3, "w3"), (b3, "b3"), (upm, "upm"), (dnm, "dnm"), (wkv, "wkv"), (wq, "wq"), (o1t, "o1t"),
                   (o2t, "o2t"), (lncol, "lncol"), (lnrow, "lnrow"), (headm, "headm")]

        @block.sync
        def _(sp):
            for dst, name in weights:
                sp.dma_start(dst[tuple([slice(None)] * len(T[name].shape))], T[name]).then_inc(w_in, 16)
            for k in range(NB):
                sp.dma_start(X[:, k * BW:(k + 1) * BW], x_v[0, :, k * BW:(k + 1) * BW]).then_inc(x_in[k], 16)
            def finish(b, more):
                for k in range(NB):
                    ck = slice(k * BW, (k + 1) * BW)
                    sp.wait_ge(o_done, b * NB + (k + 1) + START)
                    sp.dma_start(out_v[b, :, ck], oo[:, k % 2, :]).then_inc(out_sem[k % 2], 16)
                    if more:
                        sp.wait_ge(t_done, b * NB + (k + 1))
                        sp.dma_start(X[:, ck], x_v[b + 1, :, ck]).then_inc(x_in[k], 16)

            if B > 1:
                with sp.Fori(0, B - 1) as b:
                    finish(b, True)
            finish(B - 1, False)
            for q in range(2):
                sp.wait_ge(out_sem[q], B * (NB // 2) * 16 + START)

        def max_steps(i):
            lo, hi = 1, ROW_STEP - MAX_LAG
            return range((i - lo) * MC // (hi - lo), (i - lo + 1) * MC // (hi - lo)) if lo <= i < hi else range(0)

        def blocks(engine, b, one):
            one(b, 0, 0)
            plain(engine)
            with engine.Fori(0, NB // 2 - 1) as j2:
                one(b, j2 * 2 + 1, 1)
                one(b, j2 * 2 + 2, 0)
            one(b, NB - 1, 1)

        def is_first(j):
            return isinstance(j, int) and j == 0

        def is_last(j):
            return isinstance(j, int) and j == NB - 1

        def columns(j):
            return slice(j * BW, (j + 1) * BW) if isinstance(j, int) else bass.ds(j * BW, BW)

        @block.tensor
        def _(pe):
            def prep(b):
                for k in range(NB):
                    xk = X[:, k * BW:(k + 1) * BW]
                    pe.wait_ge(x_in[k], (b + 1) * 16)
                    if k >= 2:
                        pe.wait_ge(thL_done, b * NB + (k - 1))
                    pe.matmul(bank[k % 2][:, :], wth2[:, :], xk, start=True, stop=True).then_inc(th_ready, 1)
                    if k >= 2:
                        pe.wait_ge(phL_done, b * NB + (k - 1))
                    pe.matmul(bank[(2, 5)[k % 2]][:, :], wph2[:, :], xk, start=True, stop=True).then_inc(ph_ready, 1)
                    if k >= 2:
                        pe.wait_ge(g_done, b * NB + (k - 1))
                    for s in range(4):
                        last = pe.matmul(bank[6 + k % 2][:, s * CB:(s + 1) * CB], X[:, k * BW + s * 128:k * BW + (s + 1) * 128],
                                         wg[:, :], start=True, stop=True)
                    last.then_inc(g_ready, 1)
                    if k == 1:
                        pe.wait_ge(ta_ready, b * NB + 1)
                    if k >= 1:
                        pe.wait_ge(phH_done, b * NB + k)
                        for s in range(4 * k - 4, 4 * k):
                            maxpass(b * NB, 0, s)
                pe.wait_ge(phH_done, (b + 1) * NB)
                for s in range(MC - 4, MC):
                    maxpass(b * NB, 0, s)

            def maxpass(g, par, s):
                if s >= 2:
                    pe.wait_ge(a_used, g * MC + (s - 1))
                k, t = divmod(s, 4)
                pe.matmul(psA[s % 2][:, :], TA[:, par, t * 128:(t + 1) * 128], PhS[0:CB, k * BW:(k + 1) * BW],
                          start=True, stop=True).then_inc(a_ready, 1)

            def rows(g):
                pe.wait_ge(mx_ready, g + 1)
                for t in range(4):
                    last = pe.matmul(psQ[CB:CB + 2, t * 128:(t + 1) * 128], mxHL[:, t, :], ident[:, :], start=True, stop=True)
                last.then_inc(row_ready, 1)

            def scores(i, blk):
                pe.matmul(psS[i % 2][:, :], PhS[:, i * 128:(i + 1) * 128], ThH[:, blk], start=True, stop=False)
                pe.matmul(psS[i % 2][:, :], PhA[:, i * 128:(i + 1) * 128], ThL[:, blk], start=False, stop=True).then_inc(s_ready, 1)

            def finish(g):
                pe.wait_ge(y_saved, g + 1)
                pe.wait_ge(upd_ready, g + START)
                pe.matmul(psQ[:, :], sumsel[:, :], Y[0:CB + 1, :], start=True, stop=True)
                pe.matmul(psZ[:, :], wlast[:, :], Y[0:CB, :], start=True, stop=True).then_inc(z_ready, 1)

            def one(b, j, par):
                g = b * NB + j
                for i in range(MC):
                    if i + 3 < MC:
                        pe.wait_ge(exp_done, g * MC + (i + 2))
                        scores(i + 3, columns(j))
                    elif not is_last(j):
                        if i + 3 == MC:
                            pe.wait_ge(row_written, g + 2)
                        pe.wait_ge(exp_done, g * MC + (i + 2))
                        scores(i + 3 - MC, columns(j + 1))
                    if i == Z_STEP and not is_first(j):
                        finish(g - 1)
                    if not is_last(j):
                        if i == 1:
                            pe.wait_ge(ta_ready, g + 2)
                            pe.wait_ge(a_used, (g + 1) * MC)
                        for s in max_steps(i):
                            maxpass(g + 1, 1 - par, s)
                        if i == ROW_STEP:
                            pe.wait_ge(upd_ready, g + START)
                            rows(g + 1)
                    pe.wait_ge(ph_done, g * MC + (i + 1))
                    pe.wait_ge((pl_even, pl_odd)[i % 2], g * (MC // 2) + (i // 2 + 1) + START)
                    pe.matmul(psY[par][0:CB + 1, :], gH[:, i, :], PH[:, i % 4, :], start=i == 0, stop=False)
                    pe.matmul(psY[par][0:CB + 1, :], gL[:, i, :], PH[:, i % 4, :], start=False, stop=False)
                    pe.matmul(psY[par][0:CB + 1, :], gH[:, i, :], PL[:, i % 4, :], start=False, stop=i == MC - 1).then_inc(pv_done, 1)
                if is_last(j):
                    finish(g)

            def conv1(b):
                for r in range(NB):
                    pe.wait_ge(p1H_done, b * NB + min(r + 2, NB))
                    pe.wait_ge(p1L_done, b * NB + min(r + 2, NB))
                    if r >= 2:
                        pe.wait_ge(c1_summed, b * NB + (r - 1))
                    n = 0
                    for t in range(TAPS):
                        ky, kx = divmod(t, 3)
                        for part in (PH1, PL1):
                            last = pe.matmul(bank[r % 2][:, :], w1s[:, t, :], part[:, 8 * r + DIL * ky:8 * r + DIL * ky + 8, DIL * kx:DIL * kx + W],
                                             start=n == 0, stop=n == 2 * TAPS - 1)
                            n += 1
                    last.then_inc(c1_ready, 1)

            def spectra(b):
                pe.wait_ge(f_done, (b + 1) * NB)
                for q in range(W // 4):
                    if q >= 2:
                        pe.wait_ge((tr_act, tr_dve)[q % 2], b * 8 + q // 2)
                    plain(pe)
                    for s in range(4):
                        last = pe.matmul(bank[2 + q % 2][0:H, s * CR:(s + 1) * CR], Fc[:, 4 * q + s::W], eyecg[:, :], start=True, stop=True)
                    last.then_inc(tr_ready, 1)
                pe.wait_ge(tr_act, (b + 1) * 8)
                pe.wait_ge(tr_dve, (b + 1) * 8)
                plain(pe)
                for w in range(W):
                    last = pe.matmul(bank[4][0:CB, 0:CB], F1[:, w, 0:CB], F1[:, w, 0:CB], start=w == 0, stop=w == W - 1)
                last.then_inc(gram_ready, 1)
                for q in range(CR // 4):
                    if q >= 2:
                        if q % 2:
                            pe.wait_ge(ht_dve, b * 8 + q // 2)
                        else:
                            pe.wait_ge(ht_act, b * 9 + q // 2)
                    plain(pe)
                    for s in range(4):
                        last = pe.matmul(bank[5 + q % 2][0:W, s * 2 * KH:(s + 1) * 2 * KH], F1[:, :, 4 * q + s], hdft[:, :], start=True, stop=True)
                    last.then_inc(ht_ready, 1)
                pe.wait_ge(gram_step, b * GS + 5)
                plain(pe)
                pe.matmul(bank[4][0:CB, CB:2 * CB], gram[:, :], dmat[:, :], start=True, stop=True).then_inc(gram_step, 1)
                pe.wait_ge(ht_act, (b + 1) * 9)
                pe.wait_ge(ht_dve, (b + 1) * 8)
                for q in range(5):
                    k0, k1 = 7 * q, min(7 * q + 7, KH)
                    if q >= 2:
                        pe.wait_ge(wt_act, b * 5 + (q - 1))
                    pe.matmul(bank[q % 2][:, 0:(k1 - k0) * CR], wdft[:, :], T1[:, k0:k1, :], start=True, stop=True).then_inc(wt_ready, 1)
                pe.wait_ge(wt_act, (b + 1) * 5)
                for q in range(5):
                    k0, k1 = 8 * q, min(8 * q + 8, KH)
                    if q >= 2:
                        pe.wait_ge(r_done, b * 5 + (q - 1))
                    plain(pe)
                    for k in range(k0, k1):
                        last = pe.matmul(bank[2 + q % 2][0:MID, (k - k0) * W:(k - k0 + 1) * W], FF[0:W, k, CB:CR], ident[0:W, 0:W], start=True, stop=True)
                    last.then_inc(r_ready, 1)
                pe.wait_ge(gram_step, b * GS + 11)
                plain(pe)
                pe.matmul(bank[4][0:CB, 2 * CB:3 * CB], aexp[:, :], ident[0:CB, 0:CB], start=True, stop=True).then_inc(gram_step, 1)
                for q in range(5):
                    k0, k1 = 8 * q, min(8 * q + 8, KH)
                    pe.wait_ge(r_done, b * 5 + (q + 1))
                    if q >= 2:
                        pe.wait_ge(sg_done, b * 5 + (q - 1))
                    pe.matmul(bank[5 + q % 2][0:CB, 0:(k1 - k0) * W], w2t[:, :], RG[:, k0 * W:k1 * W], start=True, stop=True).then_inc(sg_ready, 1)
                for q in range(5):
                    k0, k1 = 8 * q, min(8 * q + 8, KH)
                    pe.wait_ge(sg_done, b * 5 + (q + 1))
                    if q >= 2:
                        pe.wait_ge(cg_used, b * 5 + (q - 1))
                    plain(pe)
                    for k in range(k0, k1):
                        gate = SG[:, k, :, :].rearrange("p s l -> p (s l)")
                        last = pe.matmul(bank[q % 2][:, (k - k0) * CB:(k - k0 + 1) * CB], gate, ident[0:CB, 0:CB], start=True, stop=True)
                    last.then_inc(cg_ready, 1)

            def channel_attention(b):
                pe.wait_ge(gram_step, b * GS + 13)
                for r in range(NB):
                    if r >= 2:
                        pe.wait_ge(sq_done, b * NB + (r - 1))
                    pe.matmul(bank[2 + r % 2][:, :], att[:, :], Fc[:, r * BW:(r + 1) * BW], start=True, stop=True).then_inc(of_ready, 1)
                    if r >= 1:
                        squares(b, r - 1)
                squares(b, NB - 1)

            def squares(b, r):
                pe.wait_ge(sq_done, b * NB + (r + 1))
                if r >= 2:
                    pe.wait_ge(root_done, b * NB + (r - 1))
                pe.matmul(bank[5 + r % 2][0:CB, :], pairsum[:, :], sqv[:, r % 2, :], start=True, stop=True).then_inc(sqs_ready, 1)

            def inverse(b):
                pe.wait_ge(cg_used, (b + 1) * 5)
                for q in range(16):
                    if q >= 2:
                        pe.wait_ge((il_act, il_dve)[q % 2], b * 8 + q // 2)
                    for s in range(4):
                        last = pe.matmul(bank[q % 2][0:KH, s * 128:(s + 1) * 128], GT[:, :, 4 * q + s], iwdft[:, :], start=True, stop=True)
                    last.then_inc(il_ready, 1)
                pe.wait_ge(il_act, (b + 1) * 8)
                pe.wait_ge(il_dve, (b + 1) * 8)
                for q in range(8):
                    if q >= 2:
                        pe.wait_ge(abs_done, b * 8 + (q - 1))
                    plain(pe)
                    for s in range(8):
                        o = bank[2 + q % 2][CB:128, s * H:(s + 1) * H]
                        pe.matmul(o, U[:, :, 8 * q + s], ihdft[:, 0:H], start=True, stop=False)
                        last = pe.matmul(o, U[:, :, W + 8 * q + s], ihdft[:, H:2 * H], start=False, stop=True)
                    last.then_inc(ik_ready, 1)

            def conv2(b):
                for r in range(NR2):
                    need = min((CROWS * r + CROWS + 1) // 8 + 1, NB)
                    pe.wait_ge(p2H_done, b * NB + need)
                    pe.wait_ge(p2L_done, b * NB + need)
                    if r >= 2:
                        pe.wait_ge(c2_done, b * NR2 + (r - 1))
                    n = 0
                    for t in range(TAPS):
                        ky, kx = divmod(t, 3)
                        for wt, part in ((w3H, PH2), (w3H, PL2), (w3L, PH2)):
                            last = pe.matmul(bank[r % 2][:, 0:CROWS * HC], wt[:, t, :], part[:, CROWS * r + ky:CROWS * r + ky + CROWS, kx:kx + HC],
                                             start=n == 0, stop=n == 3 * TAPS - 1)
                            n += 1
                    last.then_inc(c2_ready, 1)

            def rows_first(b):
                pe.wait_ge(c2_done, (b + 1) * NR2)
                for q in range(17):
                    if q >= 2:
                        if q % 2:
                            pe.wait_ge(xt_dve, b * 8 + q // 2)
                        else:
                            pe.wait_ge(xt_act, b * 9 + q // 2)
                    for s in range(min(4, HC - 4 * q)):
                        last = pe.transpose(bank[2 + q % 2][0:HC, s * C:(s + 1) * C], Xc[:, 4 * q + s::HC], ident[:, :])
                    last.then_inc(xt_ready, 1)

            def resample(b):
                def up_rows(G, s):
                    pe.wait_ge(xg_done, G + 1)
                    pe.wait_ge(s1_done, G - 1 + START)
                    for c in range(2):
                        last = pe.matmul(bank[s][0:HC, c * HU:(c + 1) * HU], Xg[:, s, c, :], upm[:, :], start=True, stop=True)
                    last.then_inc(s1_ready, 1)

                def up_columns(G, s):
                    pe.wait_ge(s1_done, G + 1 + START)
                    pe.wait_ge(y_done, 2 * (G - 1) + START)
                    for q in range(2):
                        half = slice(q * HK, (q + 1) * HK)
                        ps = bank[2 + 2 * s + q][0:HK, 0:2 * HU]
                        pe.matmul(ps, upH[:, half], S1H[:, s, :], start=True, stop=False)
                        pe.matmul(ps, upH[:, half], S1L[:, s, :], start=False, stop=False)
                        pe.matmul(ps, upL[:, half], S1H[:, s, :], start=False, stop=True).then_inc(s2_ready, 1)

                def down_columns(G, s):
                    pe.wait_ge(y_done, 2 * G + 2 + START)
                    pe.wait_ge(z_done, G - 1 + START)
                    for c in range(2):
                        for h in range(2):
                            for q in range(2):
                                last = pe.matmul(bank[6 + s][0:HK, (c * 2 + h) * W:(c * 2 + h + 1) * W],
                                                 Yt[:, s, q, c * HU + h * HK:c * HU + (h + 1) * HK], dnm[:, q, :], start=q == 0, stop=q == 1)
                    last.then_inc(s3_ready, 1)

                G0 = b * NGR
                pe.wait_ge(xt_act, (b + 1) * 9)
                pe.wait_ge(xt_dve, (b + 1) * 8)
                up_rows(G0, 0)
                up_columns(G0, 0)
                up_rows(G0 + 1, 1)
                with pe.Fori(0, NGR // 2 - 1) as j:
                    for s in range(2):
                        G = b * NGR + j * 2 + s
                        up_columns(G + 1, 1 - s)
                        up_rows(G + 2, s)
                        down_columns(G, s)
                up_columns(G0 + (NGR - 1), 1)
                down_columns(G0 + (NGR - 2), 0)
                down_columns(G0 + (NGR - 1), 1)
                pe.wait_ge(z_done, (b + 1) * NGR + START)
                for q in range(8):
                    if q >= 2:
                        pe.wait_ge((s4_act, s4_dve)[q % 2], b * 4 + q // 2)
                    for s in range(8):
                        for h in range(2):
                            last = pe.matmul(bank[q % 2][:, s * H:(s + 1) * H], Z[:, h, 8 * q + s, :], dnm[:, h, :], start=h == 0, stop=h == 1)
                    last.then_inc(s4_ready, 1)

            def keys_values(b):
                def product(b, q):
                    pe.wait_ge(kvn_done, b * NG3 + (q + 1))
                    for s in range(2):
                        first, final = q == 0 and s == 0, q == NG3 - 1 and s == 1
                        pe.matmul(bank[4][:, 0:C + 1], kvn[:, q % 2, s, 0:C], kvn[:, q % 2, s, C:2 * C + 1], start=first, stop=final)
                        last = pe.matmul(bank[5][:, 0:C], onesq[:, :], kvn[:, q % 2, s, C:2 * C], start=first, stop=final)
                    last.then_inc(kv_ready, 1)

                pe.wait_ge(s4_act, (b + 1) * 4)
                pe.wait_ge(s4_dve, (b + 1) * 4)
                for q in range(NG3):
                    if q >= 2:
                        pe.wait_ge(kvn_done, b * NG3 + (q - 1))
                    for s in range(2):
                        last = pe.matmul(bank[2 + q % 2][:, s * 2 * C:(s + 1) * 2 * C], X[:, (2 * q + s) * 128:(2 * q + s + 1) * 128], wkvc[:, :],
                                         start=True, stop=True)
                    last.then_inc(tok_ready, 1)
                    if q >= 2:
                        product(b, q - 2)
                product(b, NG3 - 2)
                product(b, NG3 - 1)
                pe.wait_ge(kvm_done, b + 1)
                pe.matmul(bank[0][:, 0:C], KVm[:, :], wq[:, :], start=True, stop=True).then_inc(m_ready, 1)
                pe.wait_ge(mi_done, b + 1)
                pe.matmul(bank[0][:, C:2 * C], MI[:, :], o1t[:, :], start=True, stop=True).then_inc(gt_ready, 1)

            def mlp(b):
                def second(k):
                    pe.wait_ge(u_done, b * NB + (k + 1))
                    if k >= 2:
                        pe.wait_ge(t_done, b * NB + (k - 1))
                    pe.matmul(bank[6 + k % 2][:, :], o2t[:, :], uu[:, k % 2, :], start=True, stop=True).then_inc(o2_ready, 1)

                pe.wait_ge(gt_done, b + 1)
                for k in range(NB):
                    if k >= 2:
                        pe.wait_ge(u_done, b * NB + (k - 1))
                    pe.matmul(bank[k % 2][:, :], GTm[:, :], X[:, k * BW:(k + 1) * BW], start=True, stop=True).then_inc(u_ready, 1)
                    if k >= 1:
                        second(k - 1)
                second(NB - 1)
                pe.wait_ge(t_done, (b + 1) * NB)

            def layers(b):
                conv1(b)
                spectra(b)
                channel_attention(b)
                inverse(b)
                conv2(b)
                rows_first(b)
                resample(b)
                keys_values(b)
                mlp(b)

            pe.wait_ge(w_in, 16 * len(weights))
            pe.wait_ge(consts, 1)
            pe.wait_ge(setup, SETUP)
            with pe.Fori(0, B) as b:
                prep(b)
                pe.wait_ge(g_done, (b + 1) * NB)
                rows(b * NB)
                pe.wait_ge(thL_done, (b + 1) * NB)
                pe.wait_ge(phA_done, (b + 1) * NB)
                pe.wait_ge(row_written, b * NB + 1)
                scores(0, columns(0))
                scores(1, columns(0))
                pe.wait_ge(exp_done, b * NB * MC + 1)
                scores(2, columns(0))
                blocks(pe, b, one)
                layers(b)

        @block.scalar
        def _(act):
            def prep(b):
                for k in range(NB):
                    ck = slice(k * BW, (k + 1) * BW)
                    act.wait_ge(th_ready, b * NB + (k + 1))
                    act.activation(ThH[:, ck], psS[k % 2][:, :], ACT.Copy).then_inc(thH_done, 1)
                    act.wait_ge(ph_ready, b * NB + (k + 1))
                    act.activation(PhS[:, ck], bank[(2, 5)[k % 2]][:, :], ACT.Copy).then_inc(phH_done, 1)

            def row(g, blk):
                act.wait_ge(row_ready, g + 1)
                act.activation(ThL[CB:CB + 2, blk], psQ[CB:CB + 2, :], ACT.Copy).then_inc(row_written, 1)

            def save(g, par):
                act.wait_ge(pv_done, (g + 1) * MC + START)
                act.wait_ge(z_ready, g + START)
                act.activation(Y[0:CB + 1, :], psY[par][0:CB + 1, :], ACT.Copy).then_inc(y_saved, 1)

            def one(b, j, par):
                g = b * NB + j
                for i in range(MC):
                    act.wait_ge(s_ready, g * MC + (i + 1))
                    act.wait_ge((pl_even, pl_odd)[i % 2], g * (MC // 2) + ((i - 4) // 2 + 1) + START)
                    act.activation(P[:, i % 4, :], psS[i % 2][:, :], ACT.Exp).then_inc(exp_done, 1)
                    if i == 1 and not is_first(j):
                        save(g - 1, 1 - par)
                    if i == ROW_STEP + 3 and not is_last(j):
                        row(g + 1, columns(j + 1))
                    act.wait_ge(exp_done, g * MC + (i + 1))
                    act.wait_ge(pv_done, g * MC + (i - 3) + START)
                    act.activation(PH[:, i % 4, :], P[:, i % 4, :], ACT.Copy).then_inc(ph_done, 1)
                if is_last(j):
                    save(g, par)

            def layer1(b):
                for k in range(NB):
                    act.wait_ge(zero1, 2 * (b + 1))
                    act.wait_ge(x1_done, b * NB + (k + 1) + START)
                    act.activation(PH1[:, DIL + 8 * k:DIL + 8 * k + 8, DIL:DIL + W], Xi[:, 8 * k:8 * k + 8, :], ACT.Copy).then_inc(p1H_done, 1)

                def feature(r):
                    act.wait_ge(c1_summed, b * NB + (r + 1))
                    act.activation(Fc[:, r * BW:(r + 1) * BW], c1s[:, r % 2, :], ACT.Gelu, bias=bn1b[:, :], scale=bn1s[:, :]).then_inc(f_done, 1)

                for r in range(NB):
                    act.wait_ge(c1_ready, b * NB + (r + 1))
                    act.activation(c1t[:, r % 2, :], bank[r % 2][CB:128, :], ACT.Copy).then_inc(c1_moved, 1)
                    if r >= 1:
                        feature(r - 1)
                feature(NB - 1)
                for q in range(0, W // 4, 2):
                    act.wait_ge(tr_ready, b * 16 + (q + 1))
                    act.activation(F1[:, 4 * q:4 * q + 4, :], bank[2 + q % 2][0:H, 0:4 * CR].rearrange("p (w c) -> p w c", w=4), ACT.Copy).then_inc(tr_act, 1)
                act.wait_ge(gram_step, b * GS + 2)
                act.activation(den[:, 0:1], gdiag[:, 0:1], ACT.Sqrt, scale=float(N), bias=eps6[0:CB, :]).then_inc(gram_step, 1)
                for q in range(0, CR // 4, 2):
                    act.wait_ge(ht_ready, b * 17 + (q + 1))
                    for s in range(2):
                        last = act.activation(T1[s * W:(s + 1) * W, :, 4 * q:4 * q + 4], bank[5 + q % 2][0:W, 0:8 * KH].rearrange("p (c s k) -> p s k c", c=4, s=2)[:, s], ACT.Copy)
                    last.then_inc(ht_act, 1)
                act.wait_ge(gram_step, b * GS + 8)
                act.activation(aexp[:, :], alog[:, :], ACT.Exp, bias=amax[:, 0:1], accum_out=asum[:, 0:1]).then_inc(gram_step, 1)
                for q in range(5):
                    k0, k1 = 7 * q, min(7 * q + 7, KH)
                    act.wait_ge(wt_ready, b * 5 + (q + 1))
                    act.activation(FF[:, k0:k1, :], bank[q % 2][:, 0:(k1 - k0) * CR].rearrange("p (k c) -> p k c", c=CR), ACT.Copy).then_inc(wt_act, 1)
                for q in range(5):
                    k0, k1 = 8 * q, min(8 * q + 8, KH)
                    act.wait_ge(r_ready, b * 5 + (q + 1))
                    act.activation(RG[:, k0 * W:k1 * W], bank[2 + q % 2][0:MID, 0:(k1 - k0) * W], ACT.Gelu, bias=cgb[:, :], scale=cgs[:, :]).then_inc(r_done, 1)
                for q in range(5):
                    k0, k1 = 8 * q, min(8 * q + 8, KH)
                    act.wait_ge(sg_ready, b * 5 + (q + 1))
                    act.activation(SG[:, k0:k1, :, :], rep(bank[5 + q % 2][0:CB, 0:(k1 - k0) * W].rearrange("p (k l) -> p k l", l=W), 2, 2), ACT.Sigmoid, bias=cg2b[:, :]).then_inc(sg_done, 1)

                def root(r):
                    act.wait_ge(sqs_ready, b * NB + (r + 1))
                    if r >= 2:
                        act.wait_ge(xa_done, b * NB + (r - 1))
                    act.activation(rtv[:, r % 2, :], bank[5 + r % 2][0:CB, :], ACT.Sqrt).then_inc(root_done, 1)

                for r in range(NB):
                    act.wait_ge(of_ready, b * NB + (r + 1))
                    if r >= 2:
                        act.wait_ge(sqs_ready, b * NB + (r - 1))
                    act.activation(sqv[:, r % 2, :], bank[2 + r % 2][:, :], ACT.Square).then_inc(sq_done, 1)
                    if r >= 1:
                        root(r - 1)
                root(NB - 1)
                for q in range(0, 16, 2):
                    act.wait_ge(il_ready, b * 16 + (q + 1))
                    act.activation(U[:, 4 * q:4 * q + 4, :], bank[q % 2][0:KH, :].rearrange("p (c w) -> p c w", c=4), ACT.Copy).then_inc(il_act, 1)
                for q in range(8):
                    act.wait_ge(ik_ready, b * 8 + (q + 1))
                    if q >= 2:
                        act.wait_ge(xb_done, b * 8 + (q - 1))
                    act.activation(absv[CB:128, q % 2, :], bank[2 + q % 2][CB:128, :], ACT.Abs).then_inc(abs_done, 1)

            def layer2(b):
                act.wait_ge(zero2, 2 * (b + 1))
                act.wait_ge(xa_done, (b + 1) * 8)
                act.wait_ge(xb_done, (b + 1) * 8)
                for k in range(NB):
                    act.activation(PH2[:, 2 + 8 * k:10 + 8 * k, 2:2 + W], Xi[:, 8 * k:8 * k + 8, :], ACT.Copy).then_inc(p2H_done, 1)
                for r in range(NR2):
                    act.wait_ge(c2_ready, b * NR2 + (r + 1))
                    act.activation(Xc[:, r * CROWS * HC:(r + 1) * CROWS * HC], bank[r % 2][:, 0:CROWS * HC], ACT.Identity, bias=b3[:, 2:3]).then_inc(c2_done, 1)
                for q in range(0, 17, 2):
                    n = min(4, HC - 4 * q)
                    act.wait_ge(xt_ready, b * 17 + (q + 1))
                    act.activation(Xh[:, 4 * q:4 * q + n, :], bank[2 + q % 2][0:HC, 0:n * C].rearrange("p (w c) -> p w c", w=n), ACT.Copy).then_inc(xt_act, 1)

                def saved(G, s):
                    act.wait_ge(s1_ready, G + 1 + START)
                    act.activation(S1H[:, s, :], bank[s][0:HC, 0:2 * HU], ACT.Copy).then_inc(s1h_done, 1)

                def relus(G, s):
                    for q in range(2):
                        act.wait_ge(s2_ready, 2 * G + (q + 1))
                        act.wait_ge(y_done, 2 * G + (q - 1) + START)
                        act.activation(Rl[:, q, :], bank[2 + 2 * s + q][0:HK, 0:2 * HU], ACT.Relu, scale=0.8 * GAIN).then_inc(relu_done, 1)

                G0 = b * NGR
                saved(G0, 0)
                saved(G0 + 1, 1)
                relus(G0, 0)
                with act.Fori(0, NGR // 2 - 1) as j:
                    for s in range(2):
                        G = b * NGR + j * 2 + s
                        relus(G + 1, 1 - s)
                        saved(G + 2, s)
                relus(G0 + (NGR - 1), 1)
                for q in range(0, 8, 2):
                    act.wait_ge(s4_ready, b * 8 + (q + 1))
                    act.activation(Xi[:, :, 8 * q:8 * q + 8], bank[q % 2][:, :].rearrange("p (w h) -> p h w", w=8), ACT.Copy).then_inc(s4_act, 1)

            def layer3(b):
                def deviations(q):
                    act.wait_ge(ss_done, b * NG3 + (q + 1))
                    act.activation(sd3[:, q % 2, :], ss3[:, q % 2, :], ACT.Sqrt, scale=1.0 / (HD - 1)).then_inc(sd_done, 1)

                for q in range(NG3):
                    act.wait_ge(tok_ready, b * NG3 + (q + 1))
                    if q >= 2:
                        act.wait_ge(ss_done, b * NG3 + (q - 1))
                    act.activation(sq3[:, q % 2, :], bank[2 + q % 2][:, :], ACT.Square).then_inc(sq3_done, 1)
                    if q >= 1:
                        deviations(q - 1)
                deviations(NG3 - 1)

                def final(k):
                    act.wait_ge(t_done, b * NB + (k + 1))
                    act.wait_ge(out_sem[k % 2], (b * (NB // 2) + k // 2) * 16 + START)
                    act.activation(oo[:, k % 2, :], tt[:, k % 2, :], ACT.Gelu).then_inc(o_done, 1)

                for k in range(NB):
                    act.wait_ge(u_ready, b * NB + (k + 1))
                    if k >= 2:
                        act.wait_ge(o2_ready, b * NB + (k - 1))
                    act.activation(uu[:, k % 2, :], bank[k % 2][:, :], ACT.Gelu).then_inc(u_done, 1)
                    if k >= 1:
                        final(k - 1)
                final(NB - 1)

            act.wait_ge(w_in, 16 * len(weights))
            act.wait_ge(setup, 2)
            act.activation(bn1s[:, :], bn[:, 3:4], ACT.Sqrt, bias=eps5[0:CB, :]).then_inc(setup, 1)
            act.activation(cgs[:, :], cgp[:, 4:5], ACT.Sqrt, bias=eps5[0:MID, :]).then_inc(setup, 1)
            act.wait_ge(setup, 4)

            with act.Fori(0, B) as b:
                prep(b)
                row(b * NB, slice(0, BW))
                blocks(act, b, one)
                layer1(b)
                layer2(b)
                layer3(b)

        @block.vector
        def _(v):
            def prep(b):
                v.memset(gH[:, :, CB:CB + 1].bitcast(f32), 1.0)
                v.memset(gL[:, :, CB:CB + 1].bitcast(f32), 0.0)
                v.memset(PhA[CB:CB + 2, :].bitcast(f32), -1.0)
                for k in range(NB):
                    ck = slice(k * BW, (k + 1) * BW)
                    v.wait_ge(thH_done, b * NB + (k + 1))
                    v.tensor_tensor(ThL[0:CB, ck], bank[k % 2][0:CB, :], ThH[0:CB, ck].bitcast(f32), ALU.subtract).then_inc(thL_done, 1)
                    v.wait_ge(phH_done, b * NB + (k + 1))
                    v.tensor_tensor(PhS[CB:128, ck], bank[(2, 5)[k % 2]][CB:128, :], PhS[CB:128, ck].bitcast(f32), ALU.subtract).then_inc(phL_done, 1)
                    v.wait_ge(g_ready, b * NB + (k + 1))
                    gk = bank[6 + k % 2][:, 0:4 * CB].rearrange("p (s k) -> p s k", s=4)
                    v.tensor_copy(gH[:, 4 * k:4 * k + 4, 0:CB], gk).then_inc(gh_done, 1)
                    v.wait_ge(gh_done, b * NB + (k + 1))
                    v.tensor_tensor(gL[:, 4 * k:4 * k + 4, 0:CB], gk, gH[:, 4 * k:4 * k + 4, 0:CB].bitcast(f32), ALU.subtract).then_inc(g_done, 1)
                    if k >= 1:
                        for s in range(4 * k - 4, 4 * k):
                            maximum(b * NB, s)
                for s in range(MC - 4, MC):
                    maximum(b * NB, s)

            def maximum(g, s):
                k, t = divmod(s, 4)
                v.wait_ge(a_ready, g * MC + (s + 1) + START)
                v.reduce_max(mx8[:, t, k:k + 1], psA[s % 2][:, :], AX.X).then_inc(a_used, 1)

            def maxima(g):
                v.wait_ge(a_used, (g + 1) * MC)
                v.reduce_max(mxn[:, :], mx8[:, :, :], AX.X).then_inc(mx_step, 1)
                v.wait_ge(mx_step, g * 2 + 1)
                v.tensor_copy(mxr[:, :], mxn[:, :]).then_inc(mx_step, 1)
                v.wait_ge(mx_step, g * 2 + 2)
                v.tensor_copy(mxHL[:, :, 0], mxr[:, :].bitcast(f32))
                v.tensor_tensor(mxHL[:, :, 1], mxn[:, :], mxr[:, :].bitcast(f32), ALU.subtract).then_inc(mx_ready, 1)
                v.wait_ge(mx_ready, g + 1)

            def quarter(g, q):
                v.wait_ge(z_ready, g + 1 + START)
                v.reciprocal(rec[:, q * 128:(q + 1) * 128], psQ[:, q * 128:(q + 1) * 128]).then_inc(rec_ready, 1)

            def update(g):
                v.wait_ge(rec_ready, 4 * (g + 1))
                v.wait_ge(x1_done, g + START)
                v.tensor_tensor(upd[:, :], psZ[:, :], rec[:, :], ALU.mult).then_inc(upd_ready, 1)

            def one(b, j, par):
                g = b * NB + j
                for i in range(MC):
                    if i == 0 and not is_last(j):
                        v.tensor_copy(TA[:, 1 - par, :], ThH[0:CB, columns(j + 1)]).then_inc(ta_ready, 1)
                    if i % 2 == 0:
                        v.wait_ge(ph_done, g * MC + (i + 1))
                        v.tensor_tensor(PL[:, i % 4, :], P[:, i % 4, :], PH[:, i % 4, :].bitcast(f32), ALU.subtract).then_inc(pl_even, 1)
                    if not is_last(j):
                        for s in max_steps(i - MAX_LAG):
                            maximum(g + 1, s)
                        if i == ROW_STEP:
                            maxima(g + 1)
                    if not is_first(j) and i % 2 == 1 and 5 <= i < 13:
                        quarter(g - 1, (i - 5) // 2)
                    if i == 13 and not is_first(j):
                        update(g - 1)
                if is_last(j):
                    for q in range(4):
                        quarter(g, q)
                    update(g)

            def layer1(b):
                for k in range(NB):
                    v.wait_ge(p1H_done, b * NB + (k + 1))
                    r = slice(DIL + 8 * k, DIL + 8 * k + 8)
                    v.tensor_tensor(PL1[:, r, DIL:DIL + W], Xi[:, 8 * k:8 * k + 8, :], PH1[:, r, DIL:DIL + W].bitcast(f32), ALU.subtract).then_inc(p1L_done, 1)
                for r in range(NB):
                    v.wait_ge(c1_moved, b * NB + (r + 1))
                    if r >= 2:
                        v.wait_ge(f_done, b * NB + (r - 1))
                    v.tensor_tensor(c1s[:, r % 2, :], bank[r % 2][0:CB, :], c1t[:, r % 2, :], ALU.add).then_inc(c1_summed, 1)
                for q in range(1, W // 4, 2):
                    v.wait_ge(tr_ready, b * 16 + (q + 1))
                    v.tensor_copy(F1[:, 4 * q:4 * q + 4, :], bank[2 + q % 2][0:H, 0:4 * CR].rearrange("p (w c) -> p w c", w=4)).then_inc(tr_dve, 1)
                v.wait_ge(gram_ready, b + 1)
                v.tensor_copy(gram[:, :], bank[4][0:CB, 0:CB]).then_inc(gram_step, 1)
                v.wait_ge(gram_step, b * GS + 1)
                v.tensor_tensor_reduce(out=dmat[:, :], in0=gram[:, :], in1=ident[0:CB, 0:CB], scale=1.0, scalar=0.0, op0=ALU.mult, op1=ALU.add,
                                       accum_out=gdiag[:, 0:1]).then_inc(gram_step, 1)
                v.wait_ge(gram_step, b * GS + 3)
                v.reciprocal(rden[:, 0:1], den[:, 0:1]).then_inc(gram_step, 1)
                v.wait_ge(gram_step, b * GS + 4)
                v.tensor_scalar(dmat[:, :], ident[0:CB, 0:CB], rden[:, 0:1], None, ALU.mult)
                v.tensor_scalar(rden[:, 1:2], rden[:, 0:1], tauc[:, 0:1], float(N), ALU.mult, ALU.mult).then_inc(gram_step, 1)
                for q in range(1, CR // 4, 2):
                    v.wait_ge(ht_ready, b * 17 + (q + 1))
                    for s in range(2):
                        last = v.tensor_copy(T1[s * W:(s + 1) * W, :, 4 * q:4 * q + 4], bank[5 + q % 2][0:W, 0:8 * KH].rearrange("p (c s k) -> p s k c", c=4, s=2)[:, s])
                    last.then_inc(ht_dve, 1)
                v.wait_ge(gram_step, b * GS + 6)
                v.scalar_tensor_tensor(out=alog[:, :], in0=bank[4][0:CB, CB:2 * CB], scalar=rden[:, 1:2], in1=headneg[:, :], op0=ALU.mult, op1=ALU.add).then_inc(gram_step, 1)
                v.wait_ge(gram_step, b * GS + 7)
                v.tensor_reduce(amax[:, 0:1], alog[:, :], AX.X, ALU.max, negate=True).then_inc(gram_step, 1)
                v.wait_ge(gram_step, b * GS + 9)
                v.reciprocal(asum[:, 1:2], asum[:, 0:1]).then_inc(gram_step, 1)
                v.wait_ge(gram_step, b * GS + 10)
                v.tensor_scalar(aexp[:, :], aexp[:, :], asum[:, 1:2], None, ALU.mult).then_inc(gram_step, 1)
                v.wait_ge(gram_step, b * GS + 12)
                v.tensor_copy(att[:, 0:CB], bank[4][0:CB, 2 * CB:3 * CB]).then_inc(gram_step, 1)
                v.wait_ge(wt_act, (b + 1) * 5)
                for q in range(5):
                    k0, k1 = 8 * q, min(8 * q + 8, KH)
                    v.wait_ge(cg_ready, b * 5 + (q + 1))
                    v.tensor_tensor(GT[:, k0:k1, :], FF[:, k0:k1, 0:CB], bank[q % 2][:, 0:(k1 - k0) * CB].rearrange("p (k c) -> p k c", c=CB), ALU.mult).then_inc(cg_used, 1)
                for r in range(NB):
                    v.wait_ge(root_done, b * NB + (r + 1))
                    ck = slice(r * BW, (r + 1) * BW)
                    v.tensor_tensor(X[0:CB, ck], X[0:CB, ck], rtv[:, r % 2, :], ALU.add).then_inc(xa_done, 1)
                for q in range(1, 16, 2):
                    v.wait_ge(il_ready, b * 16 + (q + 1))
                    v.tensor_copy(U[:, 4 * q:4 * q + 4, :], bank[q % 2][0:KH, :].rearrange("p (c w) -> p c w", c=4)).then_inc(il_dve, 1)
                for q in range(8):
                    v.wait_ge(abs_done, b * 8 + (q + 1))
                    xs = Xi[CB:128, :, 8 * q:8 * q + 8]
                    v.tensor_tensor(xs, xs, absv[CB:128, q % 2, :].rearrange("p (w h) -> p h w", w=8), ALU.add).then_inc(xb_done, 1)

            def layer2(b):
                v.wait_ge(xa_done, (b + 1) * 8)
                v.wait_ge(xb_done, (b + 1) * 8)
                for k in range(NB):
                    v.wait_ge(p2H_done, b * NB + (k + 1))
                    r = slice(2 + 8 * k, 10 + 8 * k)
                    v.tensor_tensor(PL2[:, r, 2:2 + W], Xi[:, 8 * k:8 * k + 8, :], PH2[:, r, 2:2 + W].bitcast(f32), ALU.subtract).then_inc(p2L_done, 1)
                for q in range(1, 17, 2):
                    v.wait_ge(xt_ready, b * 17 + (q + 1))
                    v.tensor_copy(Xh[:, 4 * q:4 * q + 4, :], bank[2 + q % 2][0:HC, :].rearrange("p (w c) -> p w c", w=4)).then_inc(xt_dve, 1)

                def leaky(G, s):
                    for q in range(2):
                        v.wait_ge(relu_done, 2 * G + (q + 1))
                        v.wait_ge(s3_ready, G - 1 + START)
                        v.scalar_tensor_tensor(out=Yt[:, s, q, :], in0=bank[2 + 2 * s + q][0:HK, 0:2 * HU], scalar=0.2 * GAIN, in1=Rl[:, q, :],
                                               op0=ALU.mult, op1=ALU.add).then_inc(y_done, 1)

                def keep(G, s, c):
                    v.wait_ge(s3_ready, G + 1 + START)
                    v.tensor_copy(Z[:, :, :, c], bank[6 + s][0:HK, 0:4 * W].rearrange("p (c q w) -> p q w c", c=2, q=2)).then_inc(z_done, 1)

                def rest(G, s):
                    v.wait_ge(s1h_done, G + 1)
                    v.tensor_tensor(S1L[:, s, :], bank[s][0:HC, 0:2 * HU], S1H[:, s, :].bitcast(f32), ALU.subtract).then_inc(s1_done, 1)

                G0 = b * NGR
                rest(G0, 0)
                rest(G0 + 1, 1)
                leaky(G0, 0)
                with v.Fori(0, NGR // 2 - 1) as j:
                    for s in range(2):
                        G = b * NGR + j * 2 + s
                        leaky(G + 1, 1 - s)
                        rest(G + 2, s)
                        keep(G, s, bass.ds((j * 2 + s) * 2, 2))
                leaky(G0 + (NGR - 1), 1)
                keep(G0 + (NGR - 2), 0, slice(C - 4, C - 2))
                keep(G0 + (NGR - 1), 1, slice(C - 2, C))
                for q in range(1, 8, 2):
                    v.wait_ge(s4_ready, b * 8 + (q + 1))
                    v.tensor_copy(Xi[:, :, 8 * q:8 * q + 8], bank[q % 2][:, :].rearrange("p (w h) -> p h w", w=8)).then_inc(s4_dve, 1)

            def layer3(b):
                def normalise(q):
                    s = q % 2
                    v.wait_ge(sd_done, b * NG3 + (q + 1))
                    v.tensor_scalar_add(sd3[:, s, :], sd3[:, s, :], EPS_BN).then_inc(rs_step, 1)
                    v.wait_ge(rs_step, b * 2 * NG3 + (2 * q + 1))
                    v.reciprocal(rs3[:, s, :], sd3[:, s, :]).then_inc(rs_step, 1)
                    v.wait_ge(rs_step, b * 2 * NG3 + (2 * q + 2))
                    if q >= 2:
                        v.wait_ge(kv_ready, b * NG3 + (q - 1))
                    for h in range(2):
                        last = v.tensor_tensor(kvn[:, s, h, 0:2 * C].rearrange("p (g d) -> p g d", d=HD),
                                               bank[2 + s][:, h * 2 * C:(h + 1) * 2 * C].rearrange("p (g d) -> p g d", d=HD),
                                               rep(rs3[:, s, h * 2 * HEADS:(h + 1) * 2 * HEADS], 2, HD), ALU.mult)
                    last.then_inc(kvn_done, 1)

                for q in range(NG3):
                    v.wait_ge(sq3_done, b * NG3 + (q + 1))
                    v.reduce_sum(ss3[:, q % 2, :], sq3[:, q % 2, :].rearrange("p (g d) -> p g d", d=HD), AX.X).then_inc(ss_done, 1)
                    if q >= 1:
                        normalise(q - 1)
                normalise(NG3 - 1)
                v.wait_ge(kv_ready, (b + 1) * NG3)
                v.scalar_tensor_tensor(out=kvt[:, 0, :], in0=bank[4][:, 0:C], scalar=lncol[:, 0:1], in1=lnrow[:, 0, :], op0=ALU.mult, op1=ALU.mult)
                v.scalar_tensor_tensor(out=kvt[:, 1, :], in0=bank[5][:, 0:C], scalar=lncol[:, 1:2], in1=lnrow[:, 0, :], op0=ALU.mult, op1=ALU.mult)
                v.scalar_tensor_tensor(out=wkm[:, 0:1], in0=bank[4][:, C:C + 1], scalar=lncol[:, 0:1], in1=lncol[:, 2:3], op0=ALU.mult, op1=ALU.add).then_inc(kv_step, 1)
                v.wait_ge(kv_step, 4 * b + 1)
                v.tensor_tensor(kvt[:, 0, :], kvt[:, 0, :], kvt[:, 1, :], ALU.add).then_inc(kv_step, 1)
                v.wait_ge(kv_step, 4 * b + 2)
                v.tensor_scalar(kvt[:, 1, :], lnrow[:, 1, :], wkm[:, 0:1], None, ALU.mult).then_inc(kv_step, 1)
                v.wait_ge(kv_step, 4 * b + 3)
                v.tensor_tensor(kvt[:, 0, :], kvt[:, 0, :], kvt[:, 1, :], ALU.add).then_inc(kv_step, 1)
                v.wait_ge(kv_step, 4 * b + 4)
                v.tensor_tensor(KVm[:, :], kvt[:, 0, :], headm[:, :], ALU.mult).then_inc(kvm_done, 1)
                v.wait_ge(m_ready, b + 1)
                v.tensor_tensor(MI[:, :], bank[0][:, 0:C], ident[:, :], ALU.add).then_inc(mi_done, 1)
                v.wait_ge(gt_ready, b + 1)
                v.tensor_copy(GTm[:, :], bank[0][:, C:2 * C]).then_inc(gt_done, 1)
                for k in range(NB):
                    v.wait_ge(o2_ready, b * NB + (k + 1))
                    v.wait_ge(o_done, b * NB + max(k - 1, 0) + START)
                    v.tensor_tensor(tt[:, k % 2, :], bank[6 + k % 2][:, :], X[:, k * BW:(k + 1) * BW], ALU.add).then_inc(t_done, 1)

            v.memset(eps5[:, :], EPS_BN).then_inc(setup, 1)
            v.memset(eps6[:, :], 1e-6).then_inc(setup, 1)
            v.wait_ge(w_in, 16 * len(weights))
            v.wait_ge(setup, 4)
            v.reciprocal(den[:, 0:1], bn1s[:, :])
            v.reciprocal(den[0:MID, 1:2], cgs[:, :]).then_inc(setup, 1)
            v.wait_ge(setup, 5)
            v.tensor_scalar(bn1s[:, :], den[:, 0:1], bn[:, 0:1], None, ALU.mult)
            v.tensor_scalar(cgs[:, :], den[0:MID, 1:2], cgp[:, 1:2], None, ALU.mult)
            v.tensor_tensor(rden[0:MID, 0:1], cgp[:, 0:1], cgp[:, 3:4], ALU.subtract).then_inc(setup, 1)
            v.wait_ge(setup, 6)
            v.tensor_tensor(amax[:, 0:1], bn[:, 2:3], bn1s[:, :], ALU.mult)
            v.tensor_tensor(amax[0:MID, 1:2], rden[0:MID, 0:1], cgs[:, :], ALU.mult).then_inc(setup, 1)
            v.wait_ge(setup, 7)
            v.tensor_tensor(bn1b[:, :], bn[:, 1:2], amax[:, 0:1], ALU.subtract)
            v.tensor_tensor(cgb[:, :], cgp[:, 2:3], amax[0:MID, 1:2], ALU.add)
            v.tensor_tensor(b3[:, 2:3], b3[:, 0:1], b3[:, 1:2], ALU.add)
            v.tensor_scalar_mul(upm[:, :], upm[:, :], 2.0).then_inc(ups, 1)
            v.wait_ge(ups, 1)
            v.tensor_copy(upH[:, :], upm[:, :]).then_inc(ups, 1)
            v.wait_ge(ups, 2)
            v.tensor_tensor(upL[:, :], upm[:, :], upH[:, :].bitcast(f32), ALU.subtract)
            v.tensor_scalar_mul(lncol[:, 2:3], lncol[:, 1:2], float(N))
            v.memset(onesq[:, :], 1.0)
            v.memset(kvn[:, :, :, 2 * C:2 * C + 1], 1.0)
            v.tensor_copy(w1s[:, :, 0:CB], w1[:, :, :])
            v.tensor_copy(w3H[:, :, :], w3[:, :, :])
            v.reduce_sum(wkm[:, :], wkv[:, :].rearrange("p (g d) -> p g d", d=HD), AX.X).then_inc(setup, 1)
            v.wait_ge(setup, 8)
            v.tensor_tensor(w1s[:, :, CB:2 * CB], w1[:, :, :], w1s[:, :, 0:CB].bitcast(f32), ALU.subtract)
            v.tensor_tensor(w3L[:, :, :], w3[:, :, :], w3H[:, :, :].bitcast(f32), ALU.subtract)
            v.tensor_scalar_mul(wkm[:, :], wkm[:, :], 1.0 / HD).then_inc(setup, 1)
            v.wait_ge(setup, 9)
            v.tensor_tensor(wkvc[:, :].rearrange("p (g d) -> p g d", d=HD), wkv[:, :].rearrange("p (g d) -> p g d", d=HD),
                            rep(wkm[:, :], 2, HD), ALU.subtract).then_inc(setup, 3)

            with v.Fori(0, B) as b:
                prep(b)
                maxima(b * NB)
                blocks(v, b, one)
                layer1(b)
                layer2(b)
                layer3(b)

        @block.gpsimd
        def _(pool):
            for s in started:
                pool.nop().then_inc(s, START)
            pool.nop().then_inc(consts, 1)

            def add(j, g):
                pool.wait_ge(upd_ready, g + 1 + START)
                pool.tensor_tensor(X[:, columns(j)], X[:, columns(j)], upd[:, :], ALU.add).then_inc(x1_done, 1)

            def one(b, j, par):
                g = b * NB + j
                for i in range(1, MC, 2):
                    pool.wait_ge(ph_done, g * MC + (i + 1))
                    pool.tensor_tensor(PL[:, i % 4, :], P[:, i % 4, :], PH[:, i % 4, :].bitcast(f32), ALU.subtract).then_inc(pl_odd, 1)
                    if i == 17 and not is_first(j):
                        add(j - 1, g - 1)
                if is_last(j):
                    add(j, g)

            with pool.Fori(0, B) as b:
                pool.wait_ge(thH_done, b * NB + 1)
                plain(pool)
                pool.tensor_copy(TA[:, 0, :], ThH[0:CB, 0:BW]).then_inc(ta_ready, 1)
                for k in range(NB):
                    ck = slice(k * BW, (k + 1) * BW)
                    pool.wait_ge(phH_done, b * NB + (k + 1))
                    plain(pool)
                    pool.tensor_copy(PhA[0:CB, ck], PhS[0:CB, ck]).then_inc(phA_done, 1)
                plain(pool)
                blocks(pool, b, one)
                pool.wait_ge(upd_ready, (b + 1) * NB + START)
                for part in (PH1, PL1):
                    plain(pool)
                    pool.memset(part[:, :, :].bitcast(f32), 0.0).then_inc(zero1, 1)
                pool.wait_ge(c1_ready, (b + 1) * NB)
                for part in (PH2, PL2):
                    plain(pool)
                    pool.memset(part[:, :, :].bitcast(f32), 0.0).then_inc(zero2, 1)
                pool.wait_ge(xt_act, (b + 1) * 9)
                pool.wait_ge(xt_dve, (b + 1) * 8)
                plain(pool)
                with pool.Fori(0, NGR // 2) as j:
                    for s in range(2):
                        pool.wait_ge(s1_ready, b * NGR + j * 2 + (s - 1) + START)
                        plain(pool)
                        pool.tensor_copy(Xg[:, s, :, :], Xh[:, :, bass.ds((j * 2 + s) * 2, 2)].rearrange("p w c -> p c w")).then_inc(xg_done, 1)


def host(inp):
    z = {}
    z["x"] = np.asarray(inp["x"])
    t = np.asarray(inp["L0_conv_w_theta"]).T
    z["wth2"] = np.concatenate([t, t], 1)
    t = np.asarray(inp["L0_conv_w_phi"]).T
    z["wph2"] = np.concatenate([t, t], 1)
    z["wg"] = np.asarray(inp["L0_conv_w_g"]).T
    z["wlast"] = np.asarray(inp["L0_conv_w_last"]).T
    s = np.zeros((CB + 1, 128), np.float32)
    s[CB] = 1
    z["sumsel"] = s
    z["ident"] = np.eye(128, dtype=np.float32)
    g = lambda n: np.asarray(inp[n])
    z["w1"] = g("L1_conv_conv_w").reshape(CB, C, TAPS).transpose(1, 2, 0)
    z["bn"] = np.stack([g("L1_conv_bn1_" + k) for k in "gbmv"], 1)
    z["cgp"] = np.stack([g("L1_conv_cg1_b")] + [g("L1_conv_cgbn_" + k) for k in "gbmv"], 1)
    z["cg2b"] = g("L1_conv_cg2_b")[:, None]
    z["tauc"] = np.repeat(g("L1_conv_tau").reshape(8), 8)[:, None]
    z["eyecg"] = np.concatenate([np.eye(CB, dtype=np.float32), g("L1_conv_cg1_w")[:, :, 0, 0].T], 1)
    z["w2t"] = g("L1_conv_cg2_w")[:, :, 0, 0].T
    head = np.kron(np.eye(8), np.ones((8, 8)))
    z["headneg"] = np.where(head > 0, 0.0, -1e30)
    z["att"] = np.concatenate([head * 0, head / 8], 1)
    z["pairsum"] = np.concatenate([np.eye(CB), np.eye(CB)], 0)
    ang = 2 * np.pi * np.outer(np.arange(W), np.arange(W)) / W
    co, si = np.cos(ang), np.sin(ang)
    z["hdft"] = np.concatenate([co[:, :KH], si[:, :KH]], 1)
    z["wdft"] = np.block([[co, si], [-si, co]])
    z["iwdft"] = np.block([[co, -si], [si, co]])
    a = np.full(KH, 2.0); a[0] = a[-1] = 1
    z["ihdft"] = np.concatenate([co[:KH] * a[:, None], si[:KH] * a[:, None]], 1) / N
    z["w3"] = g("L2_conv_w").reshape(C, C, TAPS).transpose(1, 2, 0)
    z["b3"] = np.stack([g("L2_conv_b_conv"), g("L2_conv_bias"), np.zeros(C, np.float32)], 1)
    f = g("L2_conv_up_filter")
    up = np.zeros((HC, HU), np.float32)
    for i in range(HC):
        for t in range(12):
            if 0 <= 2 * i - 2 + t < HU:
                up[i, 2 * i - 2 + t] = f[t]
    z["upm"] = up
    f = g("L2_conv_down_filter")
    dn = np.zeros((HU, H), np.float32)
    for j in range(H):
        for t in range(12):
            dn[2 * j + t, j] = f[11 - t]
    z["dnm"] = dn.reshape(2, HK, H).transpose(1, 0, 2)
    qkv = g("L3_conv_qkv_w").reshape(HEADS, 3, HD, C)
    z["wq"] = qkv[:, 0].reshape(C, C)
    z["wkv"] = np.concatenate([qkv[:, 1].reshape(C, C), qkv[:, 2].reshape(C, C)], 0).T
    z["o1t"], z["o2t"] = g("L3_conv_o1_w").T, g("L3_conv_o2_w").T
    z["lncol"] = np.stack([g("L3_conv_kln_w").reshape(C), g("L3_conv_kln_b").reshape(C), np.zeros(C, np.float32)], 1)
    z["lnrow"] = np.broadcast_to(np.stack([g("L3_conv_vln_w").reshape(C), g("L3_conv_vln_b").reshape(C)]), (128, 2, C))
    z["headm"] = np.kron(np.eye(HEADS), np.ones((HD, HD))) / N
    return {k: np.ascontiguousarray(v, dtype=np.float32) for k, v in z.items()}


def kernel(**inputs):
    import concourse.bacc as bacc
    from concourse import mybir as _mybir
    from concourse.bass_utils import run_bass_kernel_spmd

    nc = bacc.Bacc("TRN2", target_bir_lowering=False, num_devices=1)
    arrays = host(inputs)
    T = {k: nc.dram_tensor(k, v.shape, _mybir.dt.float32, kind="ExternalInput").ap() for k, v in arrays.items()}
    out = nc.dram_tensor("out", (B, C, H, W), _mybir.dt.float32, kind="ExternalOutput").ap()
    build(nc, T, out)
    r = run_bass_kernel_spmd(nc, [arrays], core_ids=[0])
    return r.results[0]["out"]
```

```python
import concourse.bass as bass
from concourse import mybir
from contextlib import ExitStack
import numpy as np

B, C, H, W = 8, 128, 64, 64
N = H * W
CB = 64
BW = 512
ROW_STEP = 27
MAX_LAG = 1
PAD_STEPS = (5, 8, 11, 14, 17, 20, 25)
Z_STEP = 2
NB = N // BW
MC = N // 128
TAPS = 9
MID = 4
CR = CB + MID
KH = W // 2 + 1
DIL = 3
XT = 20
FIR = 36
HP1 = H + 2 * DIL
HP2 = H + 4
HC = H + 2
HU = 2 * HC + 6
HK = HU // 2
NR = HU - 128
WR = (128 - 12) // 2 + 1
RC = 8
NRG = C // RC
CROWS = 6
NR2 = HC // CROWS
HEADS, HD = 8, 16
EPS_BN = 1e-5
GAIN = float(np.sqrt(2.0))
NG3 = N // 256
ORDER = [0, 4, 1, 5, 2, 6, 3, 7]
NGR = C // 2
GS = 13
SETUP = 12
START = 4


def rep(ap, dim, n):
    shape = list(ap.unsqueeze(dim).shape)
    shape[dim] = n
    return ap.unsqueeze(dim).broadcast_to(shape)


def build(nc, T, out):
    f32, f32r = mybir.dt.float32, mybir.dt.float32r
    ALU, ACT, AX = mybir.AluOpType, mybir.ActivationFunctionType, mybir.AxisListType
    ctx = ExitStack()
    with ctx:
        def sb(name, shape, dt=f32):
            return ctx.enter_context(nc.sbuf_tensor(name + "_sb", shape, dt))

        def sem(name):
            return ctx.enter_context(nc.semaphore(name))

        x_v = T["x"].rearrange("b c h w -> b c (h w)")
        out_v = out.rearrange("b c h w -> b c (h w)")

        X = sb("X", [C, N])
        Xi = X[:, :].rearrange("p (h w) -> p h w", h=H)
        ident = sb("ident", [128, 128])
        wth2, wph2, wg = sb("wth2", [C, 128]), sb("wph2", [C, 128]), sb("wg", [C, CB])
        wlast, sumsel = sb("wlast", [CB, C]), sb("sumsel", [CB + 1, 128])
        w1s = sb("w1s", [C, TAPS, 2 * CB], f32r)
        bn, bn1s, bn1b = sb("bn", [CB, 4]), sb("bn1s", [CB, 1]), sb("bn1b", [CB, 1])
        cgp, cgs, cgb = sb("cgp", [MID, 5]), sb("cgs", [MID, 1]), sb("cgb", [MID, 1])
        eps5, eps6 = sb("eps5", [128, 1]), sb("eps6", [128, 1])
        cg2b, tauc = sb("cg2b", [CB, 1]), sb("tauc", [CB, 1])
        eyecg, w2t = sb("eyecg", [CB, CR]), sb("w2t", [MID, CB])
        headneg, att, pairsum = sb("headneg", [CB, CB]), sb("att", [CB, 2 * CB]), sb("pairsum", [128, CB])
        hdft, wdft, iwdft, ihdft = sb("hdft", [H, 2 * KH]), sb("wdft", [128, 128]), sb("iwdft", [128, 128]), sb("ihdft", [KH, 2 * H])
        gram, gdiag, den, rden, dmat, alog, amax, aexp, asum = [sb(n, [CB, k]) for n, k in (
            ("gram", CB), ("gdiag", CB), ("den", 4), ("rden", 4), ("dmat", CB), ("alog", CB), ("amax", 4), ("aexp", CB), ("asum", 4))]
        w3H, w3L = sb("w3H", [C, TAPS, C], f32r), sb("w3L", [C, TAPS, C], f32r)
        b3, upm, dnm = sb("b3", [C, 3]), sb("upm", [HC, HU]), sb("dnm", [HK, 2, H])
        upH, upL = sb("upH", [HC, HU], f32r), sb("upL", [HC, HU], f32r)
        upf = sb("upf", [C, 12])
        dnw = sb("dnw", [128, W])
        dnr = sb("dnr", [RC * NR, RC, W - WR])
        wkvc, wkm = sb("wkvc", [C, 2 * C]), sb("wkm", [C, 2 * HEADS])
        wq, o1t, o2t = sb("wq", [C, C]), sb("o1t", [C, C]), sb("o2t", [C, C])
        lncol, lnrow, headm = sb("lncol", [C, 3]), sb("lnrow", [128, 2, C]), sb("headm", [C, C])
        KVm, MI, GTm, kvt = sb("KVm", [C, C]), sb("MI", [C, C]), sb("GTm", [C, C]), sb("kvt", [C, 2, C])
        kvn = sb("kvn", [128, 2, 2, 2 * C + 1])
        onesq = sb("onesq", [128, 128])

        arena_at = -(-nc.sbuf_base // 64) * 64
        ARENA = (nc.sbuf_usable_end - arena_at) // 64 * 64

        def place(name, at, shape, dt=f32):
            size = -(-int(np.prod(shape[1:])) * 4 // 64) * 64
            assert at + size <= ARENA, name
            return nc.alloc_sbuf_tensor_at(name, shape, dt, offset=arena_at + at), at + size

        ThH, at = place("ThH", 0, [128, N], f32r)
        PhS, at = place("PhS", at, [128, N], f32r)
        ThL, at = place("ThL", at, [CB + 2, N], f32r)
        PhA, at = place("PhA", at, [CB + 2, N], f32r)
        TA, at = place("TA", at, [CB, 2, BW], f32r)
        gH, at = place("gH", at, [128, MC, CB + 1], f32r)
        gL, at = place("gL", at, [128, MC, CB + 1], f32r)
        P, at = place("P", at, [128, 4, BW])
        PH, at = place("PH", at, [128, 4, BW], f32r)
        PL, at = place("PL", at, [128, 4, BW], f32r)
        Y, at = place("Y", at, [128, BW])
        rec, at = place("rec", at, [128, BW])
        upd, at = place("upd", at, [128, BW])
        mx8, at = place("mx8", at, [128, 4, NB])
        mxn, at = place("mxn", at, [128, 4])
        mxr, at = place("mxr", at, [128, 4], f32r)
        mxHL, at = place("mxHL", at, [128, 4, 2])

        pads_at = at
        PH1, at = place("PH1", pads_at, [128, HP1, HP1], f32r)
        PL1, _ = place("PL1", at, [128, HP1, HP1], f32r)
        PH2, at = place("PH2", pads_at, [128, HP2, HP2], f32r)
        PL2, _ = place("PL2", at, [128, HP2, HP2], f32r)

        c1_at = 0
        c1t, at = place("c1t", 0, [CB, 2, BW])
        c1s, at = place("c1s", at, [CB, 2, BW])
        Fc, at = place("Fc", at, [CB, N])
        F1, at = place("F1", at, [H, W, CR])
        T1, at = place("T1", at, [128, KH, CR])
        FF, at = place("FF", at, [128, KH, CR])
        SG, at = place("SG", at, [CB, KH, 2, W])
        RG, at = place("RG", at, [MID, KH * W])
        GT, at = place("GT", at, [128, KH, CB])
        U, _ = place("U", c1_at, [KH, CB, 128])
        sqv, at = place("sqv", at, [128, 2, BW])
        rtv, at = place("rtv", at, [CB, 2, BW])
        absv, at = place("absv", at, [128, 2, BW])

        XhH, at = place("XhH", 0, [HC, HC, C], f32r)
        XhL, at = place("XhL", at, [HC, HC, C], f32r)
        Xc, ax = place("Xc", at, [128, HC * HC])
        Z, at = place("Z", at, [HK, 2, W, C])
        XrH, ax = place("XrH", ax, [HC, C, NR], f32r)
        XrL, ax = place("XrL", ax, [HC, C, NR], f32r)
        Xcr, ax = place("Xcr", ax, [C, HC, NR // 2, 2])
        RlR, ax = place("RlR", ax, [RC * NR, 2, HU])
        YtR, ax = place("YtR", ax, [RC * NR, 2, HU])
        XgH, at = place("XgH", at, [HC, 2, 2, HC], f32r)
        XgL, at = place("XgL", at, [HC, 2, 2, HC], f32r)
        S1H, at = place("S1H", at, [HC, 2, 2 * HU], f32r)
        S1L, at = place("S1L", at, [HC, 2, 2 * HU], f32r)
        Rl, at = place("Rl", at, [128, 2, 2 * HU])
        Yt, at = place("Yt", at, [128, 2, 2 * HU])
        Zr, at = place("Zr", at, [HK, 2, W - WR, C])

        sq3, at = place("sq3", 0, [128, 2, BW])
        ss3, at = place("ss3", at, [128, 4, 32])
        sd3, at = place("sd3", at, [128, 4, 32])
        rs3, at = place("rs3", at, [128, 4, 32])
        uu, at = place("uu", pads_at, [128, 2, BW])
        tt, at = place("tt", at, [128, 2, BW])
        oo, at = place("oo", at, [128, 2, BW])

        w1, at = place("w1", 0, [C, TAPS, CB])
        w3, at = place("w3", at, [C, TAPS, C])
        wkv, at = place("wkv", at, [C, 2 * C])

        bank = [ctx.enter_context(nc.psum_tensor(f"bank{i}", [128, BW], f32)) for i in range(8)]
        psT = (bank[2], bank[3], bank[6], bank[7])
        psS, psA, psY, psZ, psQ = bank[0:2], bank[3:5], (bank[2], bank[5]), bank[6], bank[7]

        x_in = [sem(f"x_in{k}") for k in range(NB)]
        w_in = sem("w_in")
        ups = sem("ups")
        consts = sem("consts")
        th_ready, ph_ready, g_ready = sem("th_ready"), sem("ph_ready"), sem("g_ready")
        thH_done, phH_done, thL_done, phL_done, phA_done, g_done = [sem(n) for n in ("thH_done", "phH_done", "thL_done", "phL_done", "phA_done", "g_done")]
        ta_ready, a_ready, a_used, mx_ready, row_ready, row_written = [sem(n) for n in ("ta_ready", "a_ready", "a_used", "mx_ready", "row_ready", "row_written")]
        s_ready, exp_done, ph_done, pl_even, pl_odd, pv_done, y_saved, z_ready, upd_ready, x1_done = [sem(n) for n in ("s_ready", "exp_done", "ph_done", "pl_even", "pl_odd", "pv_done", "y_saved", "z_ready", "upd_ready", "x1_done")]
        minus_set = sem("minus_set")
        mx_step, rec_ready, gh_done = sem("mx_step"), sem("rec_ready"), sem("gh_done")
        names = """setup zero1 p1H_done p1L_done c1_ready c1_moved c1_summed f_done tr_ready tr_act tr_dve
            gram_ready gram_step ht_ready ht_act ht_dve wt_ready wt_act r_ready r_done sg_ready sg_done cg_ready cg_used
            of_ready sq_done sqs_ready root_done xa_done il_ready il_act il_dve ik_ready abs_done xb_done
            fir_step r1_ready rr_done ry_done r3_ready zr_done z_added zero2 p2H_done p2L_done c2_ready c2_done xt_ready xt_act xt_dve xg_done s1_ready s1h_done s1_done s2_ready relu_done
            y_done s3_ready z_done s4_ready s4_act s4_dve
            tok_ready sq3_done ss_done sd_done rs_step kvn_done kv_step kv_ready kvm_done m_ready mi_done gt_ready gt_done
            u_ready u_done o2_ready t_done o_done""".split()
        (setup, zero1, p1H_done, p1L_done, c1_ready, c1_moved, c1_summed, f_done, tr_ready, tr_act, tr_dve,
         gram_ready, gram_step, ht_ready, ht_act, ht_dve, wt_ready, wt_act, r_ready, r_done, sg_ready, sg_done, cg_ready, cg_used,
         of_ready, sq_done, sqs_ready, root_done, xa_done, il_ready, il_act, il_dve, ik_ready, abs_done, xb_done,
         fir_step, r1_ready, rr_done, ry_done, r3_ready, zr_done, z_added, zero2, p2H_done, p2L_done, c2_ready, c2_done, xt_ready, xt_act, xt_dve, xg_done, s1_ready, s1h_done, s1_done, s2_ready, relu_done,
         y_done, s3_ready, z_done, s4_ready, s4_act, s4_dve,
         tok_ready, sq3_done, ss_done, sd_done, rs_step, kvn_done, kv_step, kv_ready, kvm_done, m_ready, mi_done, gt_ready, gt_done,
         u_ready, u_done, o2_ready, t_done, o_done) = [sem(n) for n in names]
        out_sem = [sem("out0"), sem("out1")]
        started = [t_done, pv_done, pl_even, pl_odd, z_ready, x1_done, a_ready, upd_ready, s1_done, y_done, z_done, s3_ready, s1_ready, o_done, *out_sem]
        block = ctx.enter_context(nc.Block())

        def plain(engine):
            engine.nop(nofuse=True)

        weights = [(ident, "ident"), (wth2, "wth2"), (wph2, "wph2"), (wg, "wg"), (wlast, "wlast"), (sumsel, "sumsel"),
                   (w1, "w1"), (bn, "bn"), (cgp, "cgp"), (cg2b, "cg2b"), (tauc, "tauc"), (eyecg, "eyecg"), (w2t, "w2t"),
                   (headneg, "headneg"), (att, "att"), (pairsum, "pairsum"), (hdft, "hdft"), (wdft, "wdft"), (iwdft, "iwdft"),
                   (ihdft, "ihdft"), (w3, "w3"), (b3, "b3"), (upm, "upm"), (dnm, "dnm"), (dnw, "dnw"), (dnr, "dnr"), (upf, "upf"), (wkv, "wkv"), (wq, "wq"), (o1t, "o1t"),
                   (o2t, "o2t"), (lncol, "lncol"), (lnrow, "lnrow"), (headm, "headm")]

        @block.sync
        def _(sp):
            for dst, name in weights:
                sp.dma_start(dst[tuple([slice(None)] * len(T[name].shape))], T[name]).then_inc(w_in, 16)
            for k in range(NB):
                sp.dma_start(X[:, k * BW:(k + 1) * BW], x_v[0, :, k * BW:(k + 1) * BW]).then_inc(x_in[k], 16)

            def finish(b, more):
                for k in range(NB):
                    ck = slice(k * BW, (k + 1) * BW)
                    sp.wait_ge(o_done, b * NB + (k + 1) + START)
                    sp.dma_start(out_v[b, :, ck], oo[:, k % 2, :]).then_inc(out_sem[k % 2], 16)
                    if more:
                        sp.wait_ge(t_done, b * NB + (k + 1) + START)
                        sp.dma_start(X[:, ck], x_v[b + 1, :, ck]).then_inc(x_in[k], 16)

            if B > 1:
                with sp.Fori(0, B - 1) as b:
                    finish(b, True)
            finish(B - 1, False)
            for q in range(2):
                sp.wait_ge(out_sem[q], B * (NB // 2) * 16 + START)

        def max_steps(i):
            lo, hi = 1, ROW_STEP - MAX_LAG
            return range((i - lo) * MC // (hi - lo), (i - lo + 1) * MC // (hi - lo)) if lo <= i < hi else range(0)

        def blocks(engine, b, one):
            one(b, 0, 0)
            plain(engine)
            with engine.Fori(0, NB // 2 - 1) as j2:
                one(b, j2 * 2 + 1, 1)
                one(b, j2 * 2 + 2, 0)
            one(b, NB - 1, 1)

        def is_first(j):
            return isinstance(j, int) and j == 0

        def is_last(j):
            return isinstance(j, int) and j == NB - 1

        def columns(j):
            return slice(j * BW, (j + 1) * BW) if isinstance(j, int) else bass.ds(j * BW, BW)

        @block.tensor
        def _(pe):
            def prep(b):
                for k in range(NB):
                    xk = X[:, k * BW:(k + 1) * BW]
                    pe.wait_ge(x_in[k], (b + 1) * 16)
                    if k >= 2:
                        pe.wait_ge(thL_done, b * NB + (k - 1))
                    pe.matmul(bank[k % 2][:, :], wth2[:, :], xk, start=True, stop=True).then_inc(th_ready, 1)
                    if k == 1:
                        pe.wait_ge(ta_ready, b * NB + 1)
                    if k >= 1:
                        pe.wait_ge(phH_done, b * NB + k)
                        maxpass(b * NB, 0, 4 * k - 4)
                        maxpass(b * NB, 0, 4 * k - 3)
                    if k >= 2:
                        pe.wait_ge(phL_done, b * NB + (k - 1))
                    pe.matmul(bank[(2, 5)[k % 2]][:, :], wph2[:, :], xk, start=True, stop=True).then_inc(ph_ready, 1)
                    if k >= 1:
                        maxpass(b * NB, 0, 4 * k - 2)
                        maxpass(b * NB, 0, 4 * k - 1)
                    if k >= 2:
                        pe.wait_ge(g_done, b * NB + (k - 1))
                    else:
                        pe.wait_ge(t_done, b * NB + START)
                    for s in range(4):
                        last = pe.matmul(bank[6 + k % 2][:, s * CB:(s + 1) * CB], X[:, k * BW + s * 128:k * BW + (s + 1) * 128],
                                         wg[:, :], start=True, stop=True)
                    last.then_inc(g_ready, 1)
                pe.wait_ge(phH_done, (b + 1) * NB)
                for s in range(MC - 4, MC):
                    maxpass(b * NB, 0, s)

            def maxpass(g, par, s):
                if s >= 2:
                    pe.wait_ge(a_used, g * MC + (s - 1))
                k, t = divmod(s, 4)
                pe.matmul(psA[s % 2][:, :], TA[:, par, t * 128:(t + 1) * 128], PhS[0:CB, k * BW:(k + 1) * BW],
                          start=True, stop=True).then_inc(a_ready, 1)

            def rows(g):
                pe.wait_ge(mx_ready, g + 1)
                for t in range(4):
                    last = pe.matmul(psQ[CB:CB + 2, t * 128:(t + 1) * 128], mxHL[:, t, :], ident[:, :], start=True, stop=True)
                last.then_inc(row_ready, 1)

            def scores(i, blk):
                pe.matmul(psS[i % 2][:, :], PhS[:, i * 128:(i + 1) * 128], ThH[:, blk], start=True, stop=False)
                pe.matmul(psS[i % 2][:, :], PhA[:, i * 128:(i + 1) * 128], ThL[:, blk], start=False, stop=True).then_inc(s_ready, 1)

            def finish(g):
                pe.wait_ge(y_saved, g + 1)
                pe.wait_ge(upd_ready, g + START)
                pe.matmul(psQ[:, :], sumsel[:, :], Y[0:CB + 1, :], start=True, stop=True)
                pe.matmul(psZ[:, :], wlast[:, :], Y[0:CB, :], start=True, stop=True).then_inc(z_ready, 1)

            def one(b, j, par):
                g = b * NB + j
                for i in range(MC):
                    if i + 3 < MC:
                        pe.wait_ge(exp_done, g * MC + (i + 2))
                        scores(i + 3, columns(j))
                    elif not is_last(j):
                        if i + 3 == MC:
                            pe.wait_ge(row_written, g + 2)
                        pe.wait_ge(exp_done, g * MC + (i + 2))
                        scores(i + 3 - MC, columns(j + 1))
                    if i == Z_STEP and not is_first(j):
                        finish(g - 1)
                    if not is_last(j):
                        if i == 1:
                            pe.wait_ge(ta_ready, g + 2)
                            pe.wait_ge(a_used, (g + 1) * MC)
                        for s in max_steps(i):
                            maxpass(g + 1, 1 - par, s)
                        if i == ROW_STEP:
                            pe.wait_ge(upd_ready, g + START)
                            rows(g + 1)
                    pe.wait_ge(ph_done, g * MC + (i + 1))
                    pe.wait_ge((pl_even, pl_odd)[i % 2], g * (MC // 2) + (i // 2 + 1) + START)
                    pe.matmul(psY[par][0:CB + 1, :], gH[:, i, :], PH[:, i % 4, :], start=i == 0, stop=False)
                    pe.matmul(psY[par][0:CB + 1, :], gL[:, i, :], PH[:, i % 4, :], start=False, stop=False)
                    pe.matmul(psY[par][0:CB + 1, :], gH[:, i, :], PL[:, i % 4, :], start=False, stop=i == MC - 1).then_inc(pv_done, 1)

            def conv1(b):
                for r in range(NB):
                    if r == 2:
                        finish(b * NB + (NB - 1))
                    pe.wait_ge(p1H_done, b * NB + min(r + 2, NB))
                    pe.wait_ge(p1L_done, b * NB + min(r + 2, NB))
                    if r >= 2:
                        pe.wait_ge(c1_summed, b * NB + (r - 1))
                    n = 0
                    for t in range(TAPS):
                        ky, kx = divmod(t, 3)
                        for part in (PH1, PL1):
                            last = pe.matmul(bank[r % 2][:, :], w1s[:, t, :], part[:, 8 * r + DIL * ky:8 * r + DIL * ky + 8, DIL * kx:DIL * kx + W],
                                             start=n == 0, stop=n == 2 * TAPS - 1)
                            n += 1
                    last.then_inc(c1_ready, 1)

            def spectra(b):
                pe.wait_ge(f_done, (b + 1) * NB)
                for q in range(W // 4):
                    if q >= 2:
                        pe.wait_ge((tr_act, tr_dve)[q % 2], b * 8 + q // 2)
                    plain(pe)
                    for s in range(4):
                        last = pe.matmul(bank[2 + q % 2][0:H, s * CR:(s + 1) * CR], Fc[:, 4 * q + s::W], eyecg[:, :], start=True, stop=True)
                    last.then_inc(tr_ready, 1)
                pe.wait_ge(tr_act, (b + 1) * 8)
                pe.wait_ge(tr_dve, (b + 1) * 8)
                plain(pe)
                for w in range(W):
                    last = pe.matmul(bank[4][0:CB, 0:CB], F1[:, w, 0:CB], F1[:, w, 0:CB], start=w == 0, stop=w == W - 1)
                last.then_inc(gram_ready, 1)
                for q in range(CR // 4):
                    if q >= 2:
                        if q % 2:
                            pe.wait_ge(ht_dve, b * 8 + q // 2)
                        else:
                            pe.wait_ge(ht_act, b * 9 + q // 2)
                    plain(pe)
                    for s in range(4):
                        last = pe.matmul(bank[5 + q % 2][0:W, s * 2 * KH:(s + 1) * 2 * KH], F1[:, :, 4 * q + s], hdft[:, :], start=True, stop=True)
                    last.then_inc(ht_ready, 1)
                pe.wait_ge(gram_step, b * GS + 5)
                plain(pe)
                pe.matmul(bank[4][0:CB, CB:2 * CB], gram[:, :], dmat[:, :], start=True, stop=True).then_inc(gram_step, 1)
                pe.wait_ge(ht_act, (b + 1) * 9)
                pe.wait_ge(ht_dve, (b + 1) * 8)
                for q in range(5):
                    k0, k1 = 7 * q, min(7 * q + 7, KH)
                    if q >= 2:
                        pe.wait_ge(wt_act, b * 5 + (q - 1))
                    pe.matmul(bank[q % 2][:, 0:(k1 - k0) * CR], wdft[:, :], T1[:, k0:k1, :], start=True, stop=True).then_inc(wt_ready, 1)
                pe.wait_ge(wt_act, (b + 1) * 5)
                for q in range(5):
                    k0, k1 = 8 * q, min(8 * q + 8, KH)
                    if q >= 2:
                        pe.wait_ge(r_done, b * 5 + (q - 1))
                    plain(pe)
                    for k in range(k0, k1):
                        last = pe.transpose(bank[2 + q % 2][0:MID, (k - k0) * W:(k - k0 + 1) * W], FF[0:W, k, CB:CR], ident[0:W, 0:W])
                    last.then_inc(r_ready, 1)
                pe.wait_ge(gram_step, b * GS + 11)
                plain(pe)
                pe.matmul(bank[4][0:CB, 2 * CB:3 * CB], aexp[:, :], ident[0:CB, 0:CB], start=True, stop=True).then_inc(gram_step, 1)
                for q in range(5):
                    k0, k1 = 8 * q, min(8 * q + 8, KH)
                    pe.wait_ge(r_done, b * 5 + (q + 1))
                    if q >= 2:
                        pe.wait_ge(sg_done, b * 5 + (q - 1))
                    pe.matmul(bank[5 + q % 2][0:CB, 0:(k1 - k0) * W], w2t[:, :], RG[:, k0 * W:k1 * W], start=True, stop=True).then_inc(sg_ready, 1)
                for q in range(5):
                    k0, k1 = 8 * q, min(8 * q + 8, KH)
                    pe.wait_ge(sg_done, b * 5 + (q + 1))
                    if q >= 2:
                        pe.wait_ge(cg_used, b * 5 + (q - 1))
                    plain(pe)
                    for k in range(k0, k1):
                        gate = SG[:, k, :, :].rearrange("p s l -> p (s l)")
                        last = pe.transpose(bank[q % 2][:, (k - k0) * CB:(k - k0 + 1) * CB], gate, ident[0:CB, 0:CB])
                    last.then_inc(cg_ready, 1)

            def channel_attention(b):
                pe.wait_ge(gram_step, b * GS + 13)
                for r in range(NB):
                    if r >= 2:
                        pe.wait_ge(sq_done, b * NB + (r - 1))
                    pe.matmul(bank[2 + r % 2][:, :], att[:, :], Fc[:, r * BW:(r + 1) * BW], start=True, stop=True).then_inc(of_ready, 1)
                    if r >= 1:
                        squares(b, r - 1)
                squares(b, NB - 1)

            def squares(b, r):
                pe.wait_ge(sq_done, b * NB + (r + 1))
                if r >= 2:
                    pe.wait_ge(root_done, b * NB + (r - 1))
                pe.matmul(bank[5 + r % 2][0:CB, :], pairsum[:, :], sqv[:, r % 2, :], start=True, stop=True).then_inc(sqs_ready, 1)

            def inverse(b):
                pe.wait_ge(cg_used, (b + 1) * 5)
                for q in range(16):
                    if q >= 2:
                        pe.wait_ge((il_act, il_dve)[q % 2], b * 8 + q // 2)
                    for s in range(4):
                        last = pe.matmul(bank[q % 2][0:KH, s * 128:(s + 1) * 128], GT[:, :, 4 * q + s], iwdft[:, :], start=True, stop=True)
                    last.then_inc(il_ready, 1)
                pe.wait_ge(il_act, (b + 1) * 8)
                pe.wait_ge(il_dve, (b + 1) * 8)
                for q in range(8):
                    if q >= 2:
                        pe.wait_ge(abs_done, b * 8 + (q - 1))
                    plain(pe)
                    for s in range(8):
                        o = bank[2 + q % 2][CB:128, s * H:(s + 1) * H]
                        pe.matmul(o, U[:, :, 8 * q + s], ihdft[:, 0:H], start=True, stop=False)
                        last = pe.matmul(o, U[:, :, W + 8 * q + s], ihdft[:, H:2 * H], start=False, stop=True)
                    last.then_inc(ik_ready, 1)

            def conv2(b):
                pe.wait_ge(p2H_done, (b + 1) * NB)
                pe.wait_ge(p2L_done, (b + 1) * NB)
                for r in range(NR2):
                    if r >= 2:
                        pe.wait_ge(c2_done, b * NR2 + (r - 1))
                    n = 0
                    for t in range(TAPS):
                        ky, kx = divmod(t, 3)
                        for wt, part in ((w3H, PH2), (w3H, PL2), (w3L, PH2)):
                            last = pe.matmul(bank[r % 2][:, 0:CROWS * HC], wt[:, t, :], part[:, CROWS * r + ky:CROWS * r + ky + CROWS, kx:kx + HC],
                                             start=n == 0, stop=n == 3 * TAPS - 1)
                            n += 1
                    last.then_inc(c2_ready, 1)

            def rows_first(b):
                pe.wait_ge(c2_done, (b + 1) * NR2)
                for q in range(17):
                    if q >= 4:
                        pe.wait_ge(xt_dve, b * XT + (q - 3))
                    for s in range(min(4, HC - 4 * q)):
                        last = pe.transpose(bank[2 + q % 4][0:HC, s * C:(s + 1) * C], Xc[:, 4 * q + s::HC], ident[:, :])
                    last.then_inc(xt_ready, 1)
                columns_ = Xcr[:, :, :, :].rearrange("p h m k -> p (h m k)")
                pe.wait_ge(fir_step, (b + 1) * FIR)
                for q in range(17, XT):
                    pe.wait_ge(xt_dve, b * XT + (q - 3))
                    for s in range(min(4, NR - 4 * (q - 17))):
                        last = pe.transpose(bank[2 + q % 4][0:HC, s * C:(s + 1) * C], columns_[:, 4 * (q - 17) + s::NR], ident[:, :])
                    last.then_inc(xt_ready, 1)

            def past(b):
                def up(g):
                    if g >= 2:
                        pe.wait_ge(ry_done, b * NRG + (g - 1))
                    chans = slice(g * RC * NR, (g + 1) * RC * NR)
                    ps = bank[g % 2][0:RC * NR, 0:HU]
                    pe.matmul(ps, xrH[:, chans], upH[:, :], start=True, stop=False)
                    pe.matmul(ps, xrH[:, chans], upL[:, :], start=False, stop=False)
                    pe.matmul(ps, xrL[:, chans], upH[:, :], start=False, stop=True).then_inc(r1_ready, 1)

                def down(g):
                    pe.wait_ge(ry_done, b * NRG + (g + 1))
                    if g >= 2:
                        pe.wait_ge(zr_done, b * NRG + (g - 1))
                    n = RC * (W - WR)
                    for h in range(2):
                        last = pe.matmul(bank[6 + g % 2][0:HK, h * n:(h + 1) * n], YtR[:, g % 2, h * HK:(h + 1) * HK], dnr[:, :, :], start=True, stop=True)
                    last.then_inc(r3_ready, 1)

                xrH, xrL = [t[:, :, :].rearrange("p c k -> p (c k)") for t in (XrH, XrL)]
                pe.wait_ge(xt_dve, (b + 1) * XT)
                for g in range(NRG + 2):
                    if g < NRG:
                        up(g)
                    if g >= 2:
                        down(g - 2)
                pe.wait_ge(zr_done, (b + 1) * NRG)

            def resample(b):
                def up_rows(G, s):
                    pe.wait_ge(xg_done, 2 * (G + 1))
                    pe.wait_ge(s1_done, G - 1 + START)
                    for c in range(2):
                        ps = bank[s][0:HC, c * HU:(c + 1) * HU]
                        pe.matmul(ps, XgH[:, s, c, :], upH[:, :], start=True, stop=False)
                        pe.matmul(ps, XgH[:, s, c, :], upL[:, :], start=False, stop=False)
                        last = pe.matmul(ps, XgL[:, s, c, :], upH[:, :], start=False, stop=True)
                    last.then_inc(s1_ready, 1)

                def up_columns(G, s):
                    pe.wait_ge(s1_done, G + 1 + START)
                    pe.wait_ge(y_done, G - 1 + START)
                    ps = bank[2 + 2 * s][:, 0:2 * HU]
                    pe.matmul(ps, upH[:, 0:128], S1H[:, s, :], start=True, stop=False)
                    pe.matmul(ps, upH[:, 0:128], S1L[:, s, :], start=False, stop=False)
                    pe.matmul(ps, upL[:, 0:128], S1H[:, s, :], start=False, stop=True).then_inc(s2_ready, 1)

                def down_columns(G, s):
                    pe.wait_ge(y_done, G + 1 + START)
                    pe.wait_ge(z_done, G - 1 + START)
                    for c in range(2):
                        for h in range(2):
                            last = pe.matmul(bank[6 + s][0:HK, (c * 2 + h) * W:(c * 2 + h + 1) * W],
                                             Yt[:, s, c * HU + h * HK:c * HU + (h + 1) * HK], dnw[:, :], start=True, stop=True)
                    last.then_inc(s3_ready, 1)

                G0 = b * NGR
                up_rows(G0, 0)
                up_rows(G0 + 1, 1)
                up_columns(G0, 0)
                with pe.Fori(0, NGR // 2 - 1) as j:
                    for s in range(2):
                        G = b * NGR + j * 2 + s
                        up_rows(G + 2, s)
                        up_columns(G + 1, 1 - s)
                        down_columns(G, s)
                up_columns(G0 + (NGR - 1), 1)
                down_columns(G0 + (NGR - 2), 0)
                down_columns(G0 + (NGR - 1), 1)

            def down_rows(b, p):
                if p == 0:
                    pe.wait_ge(z_done, (b + 1) * NGR + START)
                if p == 7:
                    pe.wait_ge(z_added, b + 1)
                if p >= 2:
                    pe.wait_ge((s4_act, s4_dve)[p % 2], b * 4 + p // 2)
                for s in range(8):
                    for h in range(2):
                        last = pe.matmul(bank[p % 2][:, s * H:(s + 1) * H], Z[:, h, 8 * ORDER[p] + s, :], dnm[:, h, :], start=h == 0, stop=h == 1)
                last.then_inc(s4_ready, 1)

            def keys_values(b):
                def tokens(q):
                    pe.wait_ge(s4_act, b * 4 + (q // 4 + 1))
                    pe.wait_ge(s4_dve, b * 4 + (q // 4 + 1))
                    if q >= 4:
                        pe.wait_ge(kvn_done, b * NG3 + (q - 3))
                    for s in range(2):
                        last = pe.matmul(psT[q % 4][:, s * 2 * C:(s + 1) * 2 * C], X[:, 2 * q + s::W // 2], wkvc[:, :], start=True, stop=True)
                    last.then_inc(tok_ready, 1)

                def product(q):
                    pe.wait_ge(kvn_done, b * NG3 + (q + 1))
                    for s in range(2):
                        first, final = q == 0 and s == 0, q == NG3 - 1 and s == 1
                        pe.matmul(bank[4][:, 0:C + 1], kvn[:, q % 2, s, 0:C], kvn[:, q % 2, s, C:2 * C + 1], start=first, stop=final)
                        last = pe.matmul(bank[5][:, 0:C], onesq[:, :], kvn[:, q % 2, s, C:2 * C], start=first, stop=final)
                    last.then_inc(kv_ready, 1)

                down_rows(b, 0)
                down_rows(b, 1)
                for q in range(NG3 + 3):
                    if q % 2 == 0 and q // 2 + 2 < 8:
                        down_rows(b, q // 2 + 2)
                    if q < NG3:
                        tokens(q)
                    if q >= 3:
                        product(q - 3)
                pe.wait_ge(kvm_done, b + 1)
                pe.matmul(bank[0][:, 0:C], KVm[:, :], wq[:, :], start=True, stop=True).then_inc(m_ready, 1)
                pe.wait_ge(mi_done, b + 1)
                pe.matmul(bank[0][:, C:2 * C], MI[:, :], o1t[:, :], start=True, stop=True).then_inc(gt_ready, 1)

            def mlp(b):
                def second(k):
                    pe.wait_ge(u_done, b * NB + (k + 1))
                    if k >= 2:
                        pe.wait_ge(t_done, b * NB + (k - 1) + START)
                    pe.matmul(bank[6 + k % 2][:, :], o2t[:, :], uu[:, k % 2, :], start=True, stop=True).then_inc(o2_ready, 1)

                pe.wait_ge(gt_done, b + 1)
                for k in range(NB):
                    if k >= 2:
                        pe.wait_ge(u_done, b * NB + (k - 1))
                    pe.matmul(bank[k % 2][:, :], GTm[:, :], X[:, k * BW:(k + 1) * BW], start=True, stop=True).then_inc(u_ready, 1)
                    if k >= 1:
                        second(k - 1)
                second(NB - 1)

            def layers(b):
                conv1(b)
                spectra(b)
                channel_attention(b)
                inverse(b)
                conv2(b)
                rows_first(b)
                past(b)
                resample(b)
                keys_values(b)
                mlp(b)

            pe.wait_ge(w_in, 16 * len(weights))
            pe.wait_ge(consts, 1)
            pe.wait_ge(setup, SETUP)
            with pe.Fori(0, B) as b:
                prep(b)
                pe.wait_ge(g_done, (b + 1) * NB)
                rows(b * NB)
                pe.wait_ge(thL_done, (b + 1) * NB)
                pe.wait_ge(phA_done, (b + 1) * NB)
                pe.wait_ge(row_written, b * NB + 1)
                scores(0, columns(0))
                scores(1, columns(0))
                pe.wait_ge(exp_done, b * NB * MC + 1)
                scores(2, columns(0))
                blocks(pe, b, one)
                layers(b)

        @block.scalar
        def _(act):
            def prep(b):
                for k in range(NB):
                    ck = slice(k * BW, (k + 1) * BW)
                    act.wait_ge(th_ready, b * NB + (k + 1))
                    act.activation(ThH[:, ck], psS[k % 2][:, :], ACT.Copy).then_inc(thH_done, 1)
                    act.wait_ge(ph_ready, b * NB + (k + 1))
                    act.activation(PhS[:, ck], bank[(2, 5)[k % 2]][:, :], ACT.Copy).then_inc(phH_done, 1)
                    act.wait_ge(g_ready, b * NB + (k + 1))
                    act.activation(gH[:, 4 * k:4 * k + 4, 0:CB], bank[6 + k % 2][:, 0:4 * CB].rearrange("p (s k) -> p s k", s=4), ACT.Copy).then_inc(gh_done, 1)

            def row(g, blk):
                act.wait_ge(row_ready, g + 1)
                act.activation(ThL[CB:CB + 2, blk], psQ[CB:CB + 2, :], ACT.Copy).then_inc(row_written, 1)

            def padded1(b, k):
                act.wait_ge(zero1, b + 1)
                act.wait_ge(x1_done, b * NB + (k + 1) + START)
                act.activation(PH1[:, DIL + 8 * k:DIL + 8 * k + 8, DIL:DIL + W], Xi[:, 8 * k:8 * k + 8, :], ACT.Copy).then_inc(p1H_done, 1)

            def save(g, par):
                act.wait_ge(pv_done, (g + 1) * MC + START)
                act.wait_ge(z_ready, g + START)
                act.activation(Y[0:CB + 1, :], psY[par][0:CB + 1, :], ACT.Copy).then_inc(y_saved, 1)

            def one(b, j, par):
                g = b * NB + j
                for i in range(MC):
                    act.wait_ge(s_ready, g * MC + (i + 1))
                    act.wait_ge((pl_even, pl_odd)[i % 2], g * (MC // 2) + ((i - 4) // 2 + 1) + START)
                    act.activation(P[:, i % 4, :], psS[i % 2][:, :], ACT.Exp).then_inc(exp_done, 1)
                    if i == 1 and not is_first(j):
                        save(g - 1, 1 - par)
                    if i == ROW_STEP + 3 and not is_last(j):
                        row(g + 1, columns(j + 1))
                    if is_last(j) and i in PAD_STEPS:
                        padded1(b, PAD_STEPS.index(i))
                    act.wait_ge(exp_done, g * MC + (i + 1))
                    act.wait_ge(pv_done, g * MC + (i - 3) + START)
                    act.activation(PH[:, i % 4, :], P[:, i % 4, :], ACT.Copy).then_inc(ph_done, 1)
                if is_last(j):
                    save(g, par)

            def layer1(b):
                def feature(r):
                    act.wait_ge(c1_summed, b * NB + (r + 1))
                    act.activation(Fc[:, r * BW:(r + 1) * BW], c1s[:, r % 2, :], ACT.Gelu, bias=bn1b[:, :], scale=bn1s[:, :]).then_inc(f_done, 1)

                for r in range(NB):
                    act.wait_ge(c1_ready, b * NB + (r + 1))
                    act.activation(c1t[:, r % 2, :], bank[r % 2][CB:128, :], ACT.Copy).then_inc(c1_moved, 1)
                    if r >= 1:
                        feature(r - 1)
                    if r == 2:
                        padded1(b, NB - 1)
                feature(NB - 1)
                for q in range(0, W // 4, 2):
                    act.wait_ge(tr_ready, b * 16 + (q + 1))
                    act.activation(F1[:, 4 * q:4 * q + 4, :], bank[2 + q % 2][0:H, 0:4 * CR].rearrange("p (w c) -> p w c", w=4), ACT.Copy).then_inc(tr_act, 1)
                act.wait_ge(gram_step, b * GS + 2)
                act.activation(den[:, 0:1], gdiag[:, 0:1], ACT.Sqrt, scale=float(N), bias=eps6[0:CB, :]).then_inc(gram_step, 1)
                for q in range(0, CR // 4, 2):
                    act.wait_ge(ht_ready, b * 17 + (q + 1))
                    for s in range(2):
                        last = act.activation(T1[s * W:(s + 1) * W, :, 4 * q:4 * q + 4], bank[5 + q % 2][0:W, 0:8 * KH].rearrange("p (c s k) -> p s k c", c=4, s=2)[:, s], ACT.Copy)
                    last.then_inc(ht_act, 1)
                act.wait_ge(gram_step, b * GS + 8)
                act.activation(aexp[:, :], alog[:, :], ACT.Exp, bias=amax[:, 0:1], accum_out=asum[:, 0:1]).then_inc(gram_step, 1)
                for q in range(5):
                    k0, k1 = 7 * q, min(7 * q + 7, KH)
                    act.wait_ge(wt_ready, b * 5 + (q + 1))
                    act.activation(FF[:, k0:k1, :], bank[q % 2][:, 0:(k1 - k0) * CR].rearrange("p (k c) -> p k c", c=CR), ACT.Copy).then_inc(wt_act, 1)
                for q in range(5):
                    k0, k1 = 8 * q, min(8 * q + 8, KH)
                    act.wait_ge(r_ready, b * 5 + (q + 1))
                    act.activation(RG[:, k0 * W:k1 * W], bank[2 + q % 2][0:MID, 0:(k1 - k0) * W], ACT.Gelu, bias=cgb[:, :], scale=cgs[:, :]).then_inc(r_done, 1)
                for q in range(5):
                    k0, k1 = 8 * q, min(8 * q + 8, KH)
                    act.wait_ge(sg_ready, b * 5 + (q + 1))
                    act.activation(SG[:, k0:k1, :, :], rep(bank[5 + q % 2][0:CB, 0:(k1 - k0) * W].rearrange("p (k l) -> p k l", l=W), 2, 2), ACT.Sigmoid, bias=cg2b[:, :]).then_inc(sg_done, 1)

                def root(r):
                    act.wait_ge(sqs_ready, b * NB + (r + 1))
                    if r >= 2:
                        act.wait_ge(xa_done, b * NB + (r - 1))
                    act.activation(rtv[:, r % 2, :], bank[5 + r % 2][0:CB, :], ACT.Sqrt).then_inc(root_done, 1)

                for r in range(NB):
                    act.wait_ge(of_ready, b * NB + (r + 1))
                    if r >= 2:
                        act.wait_ge(sqs_ready, b * NB + (r - 1))
                    act.activation(sqv[:, r % 2, :], bank[2 + r % 2][:, :], ACT.Square).then_inc(sq_done, 1)
                    if r >= 1:
                        root(r - 1)
                root(NB - 1)
                for q in range(0, 16, 2):
                    act.wait_ge(il_ready, b * 16 + (q + 1))
                    act.activation(U[:, 4 * q:4 * q + 4, :], bank[q % 2][0:KH, :].rearrange("p (c w) -> p c w", c=4), ACT.Copy).then_inc(il_act, 1)

                def padded2(q):
                    act.wait_ge(xb_done, b * 8 + (q + 1))
                    act.activation(PH2[:, 2:2 + H, 2 + 8 * q:10 + 8 * q], Xi[:, :, 8 * q:8 * q + 8], ACT.Copy).then_inc(p2H_done, 1)

                act.wait_ge(zero2, b + 1)
                act.wait_ge(xa_done, (b + 1) * 8)
                for q in range(8):
                    act.wait_ge(ik_ready, b * 8 + (q + 1))
                    if q >= 2:
                        act.wait_ge(xb_done, b * 8 + (q - 1))
                    act.activation(absv[CB:128, q % 2, :], bank[2 + q % 2][CB:128, :], ACT.Abs).then_inc(abs_done, 1)
                    if q >= 1:
                        padded2(q - 1)
                padded2(7)

            def layer2(b):
                for r in range(NR2):
                    act.wait_ge(c2_ready, b * NR2 + (r + 1))
                    act.activation(Xc[:, r * CROWS * HC:(r + 1) * CROWS * HC], bank[r % 2][:, 0:CROWS * HC], ACT.Identity, bias=b3[:, 2:3]).then_inc(c2_done, 1)
                for q in range(XT):
                    n = min(4, HC - 4 * q) if q < 17 else min(4, NR - 4 * (q - 17))
                    to = XhH[:, 4 * q:4 * q + n, :] if q < 17 else XrH[:, :, 4 * (q - 17):4 * (q - 17) + n].rearrange("p c k -> p k c")
                    act.wait_ge(xt_ready, b * XT + (q + 1))
                    act.activation(to, bank[2 + q % 4][0:HC, 0:n * C].rearrange("p (w c) -> p w c", w=n), ACT.Copy).then_inc(xt_act, 1)
                for g in range(NRG):
                    act.wait_ge(r1_ready, b * NRG + (g + 1))
                    if g >= 2:
                        act.wait_ge(ry_done, b * NRG + (g - 1))
                    act.activation(RlR[:, g % 2, :], bank[g % 2][0:RC * NR, 0:HU], ACT.Relu, scale=0.8 * GAIN).then_inc(rr_done, 1)

                def saved(G, s):
                    act.wait_ge(s1_ready, G + 1 + START)
                    act.activation(S1H[:, s, :], bank[s][0:HC, 0:2 * HU], ACT.Copy).then_inc(s1h_done, 1)

                def relus(G, s):
                    act.wait_ge(s2_ready, G + 1)
                    act.wait_ge(y_done, G - 1 + START)
                    act.activation(Rl[:, s, :], bank[2 + 2 * s][:, 0:2 * HU], ACT.Relu, scale=0.8 * GAIN).then_inc(relu_done, 1)

                G0 = b * NGR
                saved(G0, 0)
                saved(G0 + 1, 1)
                relus(G0, 0)
                with act.Fori(0, NGR // 2 - 1) as j:
                    for s in range(2):
                        G = b * NGR + j * 2 + s
                        saved(G + 2, s)
                        relus(G + 1, 1 - s)
                relus(G0 + (NGR - 1), 1)

            def layer3(b):
                def deviations(q):
                    act.wait_ge(ss_done, b * NG3 + (q + 1))
                    act.activation(sd3[:, q % 4, :], ss3[:, q % 4, :], ACT.Sqrt, scale=1.0 / (HD - 1)).then_inc(sd_done, 1)

                def resampled(p):
                    act.wait_ge(s4_ready, b * 8 + (p + 1))
                    w = slice(8 * ORDER[p], 8 * ORDER[p] + 8)
                    act.activation(Xi[:, :, w], bank[p % 2][:, :].rearrange("p (w h) -> p h w", w=8), ACT.Copy).then_inc(s4_act, 1)

                resampled(0)
                for q in range(NG3):
                    if q % 4 == 0 and q // 2 + 2 < 8:
                        resampled(q // 2 + 2)
                    act.wait_ge(tok_ready, b * NG3 + (q + 1))
                    if q >= 2:
                        act.wait_ge(ss_done, b * NG3 + (q - 1))
                    act.activation(sq3[:, q % 2, :], psT[q % 4][:, :], ACT.Square).then_inc(sq3_done, 1)
                    if q >= 1:
                        deviations(q - 1)
                deviations(NG3 - 1)

                def final(k):
                    act.wait_ge(t_done, b * NB + (k + 1) + START)
                    act.wait_ge(out_sem[k % 2], (b * (NB // 2) + k // 2) * 16 + START)
                    act.activation(oo[:, k % 2, :], tt[:, k % 2, :], ACT.Gelu).then_inc(o_done, 1)

                for k in range(NB):
                    act.wait_ge(u_ready, b * NB + (k + 1))
                    if k >= 2:
                        act.wait_ge(o2_ready, b * NB + (k - 1))
                    act.activation(uu[:, k % 2, :], bank[k % 2][:, :], ACT.Gelu).then_inc(u_done, 1)
                    if k >= 1:
                        final(k - 1)
                final(NB - 1)

            act.wait_ge(w_in, 16 * len(weights))
            act.wait_ge(setup, 2)
            act.activation(bn1s[:, :], bn[:, 3:4], ACT.Sqrt, bias=eps5[0:CB, :]).then_inc(setup, 1)
            act.activation(cgs[:, :], cgp[:, 4:5], ACT.Sqrt, bias=eps5[0:MID, :]).then_inc(setup, 1)
            act.wait_ge(setup, 4)

            with act.Fori(0, B) as b:
                prep(b)
                row(b * NB, slice(0, BW))
                blocks(act, b, one)
                layer1(b)
                layer2(b)
                layer3(b)

        @block.vector
        def _(v):
            def prep(b):
                for k in range(NB):
                    ck = slice(k * BW, (k + 1) * BW)
                    if k >= 1:
                        maximum(b * NB, 4 * k - 4)
                        maximum(b * NB, 4 * k - 3)
                    v.wait_ge(thH_done, b * NB + (k + 1))
                    v.tensor_tensor(ThL[0:CB, ck], bank[k % 2][0:CB, :], ThH[0:CB, ck].bitcast(f32), ALU.subtract).then_inc(thL_done, 1)
                    if k >= 1:
                        maximum(b * NB, 4 * k - 2)
                        maximum(b * NB, 4 * k - 1)
                    v.wait_ge(phH_done, b * NB + (k + 1))
                    v.tensor_tensor(PhS[CB:128, ck], bank[(2, 5)[k % 2]][CB:128, :], PhS[CB:128, ck].bitcast(f32), ALU.subtract).then_inc(phL_done, 1)
                    v.wait_ge(gh_done, b * NB + (k + 1))
                    v.tensor_tensor(gL[:, 4 * k:4 * k + 4, 0:CB], bank[6 + k % 2][:, 0:4 * CB].rearrange("p (s k) -> p s k", s=4),
                                    gH[:, 4 * k:4 * k + 4, 0:CB].bitcast(f32), ALU.subtract).then_inc(g_done, 1)
                for s in range(MC - 4, MC):
                    maximum(b * NB, s)

            def maximum(g, s):
                k, t = divmod(s, 4)
                v.wait_ge(a_ready, g * MC + (s + 1) + START)
                v.reduce_max(mx8[:, t, k:k + 1], psA[s % 2][:, :], AX.X).then_inc(a_used, 1)

            def maxima(g):
                v.wait_ge(a_used, (g + 1) * MC)
                v.reduce_max(mxn[:, :], mx8[:, :, :], AX.X).then_inc(mx_step, 1)
                v.wait_ge(mx_step, g * 2 + 1)
                v.tensor_copy(mxr[:, :], mxn[:, :]).then_inc(mx_step, 1)
                v.wait_ge(mx_step, g * 2 + 2)
                v.tensor_copy(mxHL[:, :, 0], mxr[:, :].bitcast(f32))
                v.tensor_tensor(mxHL[:, :, 1], mxn[:, :], mxr[:, :].bitcast(f32), ALU.subtract).then_inc(mx_ready, 1)
                v.wait_ge(mx_ready, g + 1)

            def padded1(b, k):
                v.wait_ge(p1H_done, b * NB + (k + 1))
                r = slice(DIL + 8 * k, DIL + 8 * k + 8)
                v.tensor_tensor(PL1[:, r, DIL:DIL + W], Xi[:, 8 * k:8 * k + 8, :], PH1[:, r, DIL:DIL + W].bitcast(f32), ALU.subtract).then_inc(p1L_done, 1)

            def quarter(g, q):
                v.wait_ge(z_ready, g + 1 + START)
                v.reciprocal(rec[:, q * 128:(q + 1) * 128], psQ[:, q * 128:(q + 1) * 128]).then_inc(rec_ready, 1)

            def update(g):
                v.wait_ge(rec_ready, 4 * (g + 1))
                v.wait_ge(x1_done, g + START)
                v.tensor_tensor(upd[:, :], psZ[:, :], rec[:, :], ALU.mult).then_inc(upd_ready, 1)

            def one(b, j, par):
                g = b * NB + j
                for i in range(MC):
                    if i == 0 and not is_last(j):
                        v.tensor_copy(TA[:, 1 - par, :], ThH[0:CB, columns(j + 1)]).then_inc(ta_ready, 1)
                    if i % 2 == 0:
                        v.wait_ge(ph_done, g * MC + (i + 1))
                        v.tensor_tensor(PL[:, i % 4, :], P[:, i % 4, :], PH[:, i % 4, :].bitcast(f32), ALU.subtract).then_inc(pl_even, 1)
                    if not is_last(j):
                        for s in max_steps(i - MAX_LAG):
                            maximum(g + 1, s)
                        if i == ROW_STEP:
                            maxima(g + 1)
                    if not is_first(j) and i % 2 == 1 and 5 <= i < 13:
                        quarter(g - 1, (i - 5) // 2)
                    if i == 13 and not is_first(j):
                        update(g - 1)
                    if is_last(j) and i in PAD_STEPS:
                        padded1(b, PAD_STEPS.index(i))

            def layer1(b):
                for r in range(NB):
                    v.wait_ge(c1_moved, b * NB + (r + 1))
                    if r >= 2:
                        v.wait_ge(f_done, b * NB + (r - 1))
                    v.tensor_tensor(c1s[:, r % 2, :], bank[r % 2][0:CB, :], c1t[:, r % 2, :], ALU.add).then_inc(c1_summed, 1)
                    if r == 0:
                        for q in range(4):
                            quarter(b * NB + (NB - 1), q)
                        update(b * NB + (NB - 1))
                    if r == 2:
                        padded1(b, NB - 1)
                for q in range(1, W // 4, 2):
                    v.wait_ge(tr_ready, b * 16 + (q + 1))
                    v.tensor_copy(F1[:, 4 * q:4 * q + 4, :], bank[2 + q % 2][0:H, 0:4 * CR].rearrange("p (w c) -> p w c", w=4)).then_inc(tr_dve, 1)
                v.wait_ge(gram_ready, b + 1)
                v.tensor_copy(gram[:, :], bank[4][0:CB, 0:CB]).then_inc(gram_step, 1)
                v.wait_ge(gram_step, b * GS + 1)
                v.tensor_tensor_reduce(out=dmat[:, :], in0=gram[:, :], in1=ident[0:CB, 0:CB], scale=1.0, scalar=0.0, op0=ALU.mult, op1=ALU.add,
                                       accum_out=gdiag[:, 0:1]).then_inc(gram_step, 1)
                v.wait_ge(gram_step, b * GS + 3)
                v.reciprocal(rden[:, 0:1], den[:, 0:1]).then_inc(gram_step, 1)
                v.wait_ge(gram_step, b * GS + 4)
                v.tensor_scalar(dmat[:, :], ident[0:CB, 0:CB], rden[:, 0:1], None, ALU.mult)
                v.tensor_scalar(rden[:, 1:2], rden[:, 0:1], tauc[:, 0:1], float(N), ALU.mult, ALU.mult).then_inc(gram_step, 1)
                for q in range(1, CR // 4, 2):
                    v.wait_ge(ht_ready, b * 17 + (q + 1))
                    for s in range(2):
                        last = v.tensor_copy(T1[s * W:(s + 1) * W, :, 4 * q:4 * q + 4], bank[5 + q % 2][0:W, 0:8 * KH].rearrange("p (c s k) -> p s k c", c=4, s=2)[:, s])
                    last.then_inc(ht_dve, 1)
                v.wait_ge(gram_step, b * GS + 6)
                v.scalar_tensor_tensor(out=alog[:, :], in0=bank[4][0:CB, CB:2 * CB], scalar=rden[:, 1:2], in1=headneg[:, :], op0=ALU.mult, op1=ALU.add).then_inc(gram_step, 1)
                v.wait_ge(gram_step, b * GS + 7)
                v.tensor_reduce(amax[:, 0:1], alog[:, :], AX.X, ALU.max, negate=True).then_inc(gram_step, 1)
                v.wait_ge(gram_step, b * GS + 9)
                v.reciprocal(asum[:, 1:2], asum[:, 0:1]).then_inc(gram_step, 1)
                v.wait_ge(gram_step, b * GS + 10)
                v.tensor_scalar(aexp[:, :], aexp[:, :], asum[:, 1:2], None, ALU.mult).then_inc(gram_step, 1)
                v.wait_ge(gram_step, b * GS + 12)
                v.tensor_copy(att[:, 0:CB], bank[4][0:CB, 2 * CB:3 * CB]).then_inc(gram_step, 1)
                v.wait_ge(wt_act, (b + 1) * 5)
                for q in range(5):
                    k0, k1 = 8 * q, min(8 * q + 8, KH)
                    v.wait_ge(cg_ready, b * 5 + (q + 1))
                    v.tensor_tensor(GT[:, k0:k1, :], FF[:, k0:k1, 0:CB], bank[q % 2][:, 0:(k1 - k0) * CB].rearrange("p (k c) -> p k c", c=CB), ALU.mult).then_inc(cg_used, 1)
                for r in range(NB):
                    v.wait_ge(root_done, b * NB + (r + 1))
                    ck = slice(r * BW, (r + 1) * BW)
                    v.tensor_tensor(X[0:CB, ck], X[0:CB, ck], rtv[:, r % 2, :], ALU.add).then_inc(xa_done, 1)
                for q in range(1, 16, 2):
                    v.wait_ge(il_ready, b * 16 + (q + 1))
                    v.tensor_copy(U[:, 4 * q:4 * q + 4, :], bank[q % 2][0:KH, :].rearrange("p (c w) -> p c w", c=4)).then_inc(il_dve, 1)

                def padded2(q):
                    v.wait_ge(p2H_done, b * 8 + (q + 1))
                    w = slice(2 + 8 * q, 10 + 8 * q)
                    v.tensor_tensor(PL2[:, 2:2 + H, w], Xi[:, :, 8 * q:8 * q + 8], PH2[:, 2:2 + H, w].bitcast(f32), ALU.subtract).then_inc(p2L_done, 1)

                for q in range(8):
                    v.wait_ge(abs_done, b * 8 + (q + 1))
                    xs = Xi[CB:128, :, 8 * q:8 * q + 8]
                    v.tensor_tensor(xs, xs, absv[CB:128, q % 2, :].rearrange("p (w h) -> p h w", w=8), ALU.add).then_inc(xb_done, 1)
                    if q >= 1:
                        padded2(q - 1)
                padded2(7)

            def layer2(b):
                image = Xc[:, :].rearrange("p (h w) -> p h w", h=HC)
                for part, (block_, r0, r1) in enumerate(((6, 0, 36), (9, 36, 54), (NR2, 54, HC))):
                    v.wait_ge(c2_done, b * NR2 + block_)
                    n = 0
                    for d in range(4, -2, -1):
                        m = min(NR // 2, 2 + d)
                        for p in range(2):
                            tap, to, of = upf[:, 2 * d + p + 2:2 * d + p + 3], Xcr[:, r0:r1, 0:m, p], image[:, r0:r1, 64 - d:64 - d + m]
                            if n >= 2:
                                v.wait_ge(fir_step, b * FIR + (part * 12 + n - 1))
                                v.scalar_tensor_tensor(out=to, in0=of, scalar=tap, in1=to, op0=ALU.mult, op1=ALU.add).then_inc(fir_step, 1)
                            else:
                                v.tensor_scalar(to, of, tap, None, ALU.mult).then_inc(fir_step, 1)
                            n += 1
                for q in range(XT):
                    n = min(4, HC - 4 * q) if q < 17 else min(4, NR - 4 * (q - 17))
                    to, of = [t[0][:, 4 * q:4 * q + n, :] if q < 17 else t[1][:, :, 4 * (q - 17):4 * (q - 17) + n].rearrange("p c k -> p k c")
                              for t in ((XhL, XrL), (XhH, XrH))]
                    v.wait_ge(xt_act, b * XT + (q + 1))
                    v.tensor_tensor(to, bank[2 + q % 4][0:HC, 0:n * C].rearrange("p (w c) -> p w c", w=n), of.bitcast(f32), ALU.subtract).then_inc(xt_dve, 1)

                def kept(g):
                    v.wait_ge(r3_ready, b * NRG + (g + 1))
                    v.tensor_copy(Zr[:, :, :, g * RC:(g + 1) * RC],
                                  bank[6 + g % 2][0:HK, 0:2 * RC * (W - WR)].rearrange("p (h c w) -> p h w c", h=2, c=RC)).then_inc(zr_done, 1)

                for g in range(NRG):
                    v.wait_ge(rr_done, b * NRG + (g + 1))
                    if g >= 2:
                        v.wait_ge(r3_ready, b * NRG + (g - 1))
                    v.scalar_tensor_tensor(out=YtR[:, g % 2, :], in0=bank[g % 2][0:RC * NR, 0:HU], scalar=0.2 * GAIN, in1=RlR[:, g % 2, :],
                                           op0=ALU.mult, op1=ALU.add).then_inc(ry_done, 1)
                    if g >= 2:
                        kept(g - 2)
                kept(NRG - 2)
                kept(NRG - 1)

                def leaky(G, s):
                    v.wait_ge(relu_done, G + 1)
                    v.wait_ge(s3_ready, G - 1 + START)
                    v.scalar_tensor_tensor(out=Yt[:, s, :], in0=bank[2 + 2 * s][:, 0:2 * HU], scalar=0.2 * GAIN, in1=Rl[:, s, :],
                                           op0=ALU.mult, op1=ALU.add).then_inc(y_done, 1)

                def keep(G, s, c):
                    v.wait_ge(s3_ready, G + 1 + START)
                    v.tensor_copy(Z[:, :, :, c], bank[6 + s][0:HK, 0:4 * W].rearrange("p (c q w) -> p q w c", c=2, q=2)).then_inc(z_done, 1)

                def rest(G, s):
                    v.wait_ge(s1h_done, G + 1)
                    v.tensor_tensor(S1L[:, s, :], bank[s][0:HC, 0:2 * HU], S1H[:, s, :].bitcast(f32), ALU.subtract).then_inc(s1_done, 1)

                G0 = b * NGR
                rest(G0, 0)
                rest(G0 + 1, 1)
                leaky(G0, 0)
                with v.Fori(0, NGR // 2 - 1) as j:
                    for s in range(2):
                        G = b * NGR + j * 2 + s
                        rest(G + 2, s)
                        leaky(G + 1, 1 - s)
                        keep(G, s, bass.ds((j * 2 + s) * 2, 2))
                leaky(G0 + (NGR - 1), 1)
                keep(G0 + (NGR - 2), 0, slice(C - 4, C - 2))
                keep(G0 + (NGR - 1), 1, slice(C - 2, C))
                v.wait_ge(z_done, (b + 1) * NGR + START)
                v.tensor_tensor(Z[:, :, WR:W, :], Z[:, :, WR:W, :], Zr[:, :, :, :], ALU.add).then_inc(z_added, 1)

            def layer3(b):
                def resampled(p):
                    v.wait_ge(s4_ready, b * 8 + (p + 1))
                    w = slice(8 * ORDER[p], 8 * ORDER[p] + 8)
                    v.tensor_copy(Xi[:, :, w], bank[p % 2][:, :].rearrange("p (w h) -> p h w", w=8)).then_inc(s4_dve, 1)

                resampled(1)
                for q in range(NG3 + 2):
                    if q % 4 == 2 and (q - 2) // 2 + 3 < 8:
                        resampled((q - 2) // 2 + 3)
                    if q < NG3:
                        v.wait_ge(sq3_done, b * NG3 + (q + 1))
                        v.reduce_sum(ss3[:, q % 4, :], sq3[:, q % 2, :].rearrange("p (g d) -> p g d", d=HD), AX.X).then_inc(ss_done, 1)
                    if 1 <= q <= NG3:
                        v.wait_ge(sd_done, b * NG3 + q)
                        v.tensor_scalar_add(sd3[:, (q - 1) % 4, :], sd3[:, (q - 1) % 4, :], EPS_BN).then_inc(rs_step, 1)
                    if q >= 2:
                        p = q - 2
                        if p >= 2:
                            v.wait_ge(kv_ready, b * NG3 + (p - 1))
                        v.wait_ge(rs_step, b * 2 * NG3 + (2 * p + 2))
                        for h in range(2):
                            last = v.tensor_tensor(kvn[:, p % 2, h, 0:2 * C].rearrange("p (g d) -> p g d", d=HD),
                                                   psT[p % 4][:, h * 2 * C:(h + 1) * 2 * C].rearrange("p (g d) -> p g d", d=HD),
                                                   rep(rs3[:, p % 4, h * 2 * HEADS:(h + 1) * 2 * HEADS], 2, HD), ALU.mult)
                        last.then_inc(kvn_done, 1)
                    if 1 <= q <= NG3:
                        v.wait_ge(rs_step, b * 2 * NG3 + (2 * (q - 1) + 1))
                        v.reciprocal(rs3[:, (q - 1) % 4, :], sd3[:, (q - 1) % 4, :]).then_inc(rs_step, 1)
                v.wait_ge(kv_ready, (b + 1) * NG3)
                v.scalar_tensor_tensor(out=kvt[:, 0, :], in0=bank[4][:, 0:C], scalar=lncol[:, 0:1], in1=lnrow[:, 0, :], op0=ALU.mult, op1=ALU.mult)
                v.scalar_tensor_tensor(out=kvt[:, 1, :], in0=bank[5][:, 0:C], scalar=lncol[:, 1:2], in1=lnrow[:, 0, :], op0=ALU.mult, op1=ALU.mult)
                v.scalar_tensor_tensor(out=wkm[:, 0:1], in0=bank[4][:, C:C + 1], scalar=lncol[:, 0:1], in1=lncol[:, 2:3], op0=ALU.mult, op1=ALU.add).then_inc(kv_step, 1)
                v.wait_ge(kv_step, 4 * b + 1)
                v.tensor_tensor(kvt[:, 0, :], kvt[:, 0, :], kvt[:, 1, :], ALU.add).then_inc(kv_step, 1)
                v.wait_ge(kv_step, 4 * b + 2)
                v.tensor_scalar(kvt[:, 1, :], lnrow[:, 1, :], wkm[:, 0:1], None, ALU.mult).then_inc(kv_step, 1)
                v.wait_ge(kv_step, 4 * b + 3)
                v.tensor_tensor(kvt[:, 0, :], kvt[:, 0, :], kvt[:, 1, :], ALU.add).then_inc(kv_step, 1)
                v.wait_ge(kv_step, 4 * b + 4)
                v.tensor_tensor(KVm[:, :], kvt[:, 0, :], headm[:, :], ALU.mult).then_inc(kvm_done, 1)
                v.wait_ge(m_ready, b + 1)
                v.tensor_tensor(MI[:, :], bank[0][:, 0:C], ident[:, :], ALU.add).then_inc(mi_done, 1)
                v.wait_ge(gt_ready, b + 1)
                v.tensor_copy(GTm[:, :], bank[0][:, C:2 * C]).then_inc(gt_done, 1)
                for k in range(NB):
                    v.wait_ge(o2_ready, b * NB + (k + 1))
                    v.wait_ge(o_done, b * NB + max(k - 1, 0) + START)
                    v.tensor_tensor(tt[:, k % 2, :], bank[6 + k % 2][:, :], X[:, k * BW:(k + 1) * BW], ALU.add).then_inc(t_done, 1)

            v.memset(eps5[:, :], EPS_BN).then_inc(setup, 1)
            v.memset(eps6[:, :], 1e-6).then_inc(setup, 1)
            v.wait_ge(w_in, 16 * len(weights))
            v.wait_ge(setup, 4)
            v.reciprocal(den[:, 0:1], bn1s[:, :])
            v.reciprocal(den[0:MID, 1:2], cgs[:, :]).then_inc(setup, 1)
            v.wait_ge(setup, 5)
            v.tensor_scalar(bn1s[:, :], den[:, 0:1], bn[:, 0:1], None, ALU.mult)
            v.tensor_scalar(cgs[:, :], den[0:MID, 1:2], cgp[:, 1:2], None, ALU.mult)
            v.tensor_tensor(rden[0:MID, 0:1], cgp[:, 0:1], cgp[:, 3:4], ALU.subtract).then_inc(setup, 1)
            v.wait_ge(setup, 6)
            v.tensor_tensor(amax[:, 0:1], bn[:, 2:3], bn1s[:, :], ALU.mult)
            v.tensor_tensor(amax[0:MID, 1:2], rden[0:MID, 0:1], cgs[:, :], ALU.mult).then_inc(setup, 1)
            v.wait_ge(setup, 7)
            v.tensor_tensor(bn1b[:, :], bn[:, 1:2], amax[:, 0:1], ALU.subtract)
            v.tensor_tensor(cgb[:, :], cgp[:, 2:3], amax[0:MID, 1:2], ALU.add)
            v.tensor_tensor(b3[:, 2:3], b3[:, 0:1], b3[:, 1:2], ALU.add)
            v.tensor_scalar_mul(upf[:, :], upf[:, :], 2.0)
            v.tensor_scalar_mul(upm[:, :], upm[:, :], 2.0).then_inc(ups, 1)
            v.wait_ge(ups, 1)
            v.tensor_copy(upH[:, :], upm[:, :]).then_inc(ups, 1)
            v.wait_ge(ups, 2)
            v.tensor_tensor(upL[:, :], upm[:, :], upH[:, :].bitcast(f32), ALU.subtract)
            v.tensor_scalar_mul(lncol[:, 2:3], lncol[:, 1:2], float(N))
            v.memset(onesq[:, :], 1.0)
            v.memset(kvn[:, :, :, 2 * C:2 * C + 1], 1.0)
            v.tensor_copy(w1s[:, :, 0:CB], w1[:, :, :])
            v.tensor_copy(w3H[:, :, :], w3[:, :, :])
            v.reduce_sum(wkm[:, :], wkv[:, :].rearrange("p (g d) -> p g d", d=HD), AX.X).then_inc(setup, 1)
            v.wait_ge(setup, 8)
            v.tensor_tensor(w1s[:, :, CB:2 * CB], w1[:, :, :], w1s[:, :, 0:CB].bitcast(f32), ALU.subtract)
            v.tensor_tensor(w3L[:, :, :], w3[:, :, :], w3H[:, :, :].bitcast(f32), ALU.subtract)
            v.tensor_scalar_mul(wkm[:, :], wkm[:, :], 1.0 / HD).then_inc(setup, 1)
            v.wait_ge(setup, 9)
            v.tensor_tensor(wkvc[:, :].rearrange("p (g d) -> p g d", d=HD), wkv[:, :].rearrange("p (g d) -> p g d", d=HD),
                            rep(wkm[:, :], 2, HD), ALU.subtract).then_inc(setup, 3)

            with v.Fori(0, B) as b:
                prep(b)
                maxima(b * NB)
                blocks(v, b, one)
                layer1(b)
                layer2(b)
                layer3(b)

        @block.gpsimd
        def _(pool):
            for s in started:
                pool.nop().then_inc(s, START)
            pool.nop().then_inc(consts, 1)

            def add(j, g):
                pool.wait_ge(upd_ready, g + 1 + START)
                pool.tensor_tensor(X[:, columns(j)], X[:, columns(j)], upd[:, :], ALU.add).then_inc(x1_done, 1)

            def one(b, j, par):
                g = b * NB + j
                for i in range(1, MC, 2):
                    pool.wait_ge(ph_done, g * MC + (i + 1))
                    pool.tensor_tensor(PL[:, i % 4, :], P[:, i % 4, :], PH[:, i % 4, :].bitcast(f32), ALU.subtract).then_inc(pl_odd, 1)
                    if i == 17 and not is_first(j):
                        add(j - 1, g - 1)
                if is_last(j):
                    add(j, g)

            def zeros(parts, d, done):
                for part in parts:
                    for edge in (part[:, 0:d, :], part[:, d + H:, :], part[:, d:d + H, 0:d], part[:, d:d + H, d + W:]):
                        last = pool.memset(edge.bitcast(f32), 0.0)
                last.then_inc(done, 1)

            with pool.Fori(0, B) as b:
                pool.wait_ge(t_done, b * NB + START)
                plain(pool)
                pool.memset(PhA[CB:CB + 2, :].bitcast(f32), -1.0).then_inc(minus_set, 1)
                pool.wait_ge(minus_set, b + 1)
                plain(pool)
                pool.memset(gH[:, :, CB:CB + 1].bitcast(f32), 1.0)
                pool.memset(gL[:, :, CB:CB + 1].bitcast(f32), 0.0)
                pool.wait_ge(thH_done, b * NB + 1)
                plain(pool)
                pool.tensor_copy(TA[:, 0, :], ThH[0:CB, 0:BW]).then_inc(ta_ready, 1)
                for k in range(NB):
                    ck = slice(k * BW, (k + 1) * BW)
                    pool.wait_ge(phH_done, b * NB + (k + 1))
                    plain(pool)
                    pool.tensor_copy(PhA[0:CB, ck], PhS[0:CB, ck]).then_inc(phA_done, 1)
                plain(pool)
                for q in range(2):
                    pool.wait_ge(out_sem[q], b * (NB // 2) * 16 + START)
                plain(pool)
                zeros((PH1, PL1), DIL, zero1)
                blocks(pool, b, one)
                pool.wait_ge(c1_ready, (b + 1) * NB)
                plain(pool)
                zeros((PH2, PL2), 2, zero2)
                pool.wait_ge(xt_dve, (b + 1) * XT)
                plain(pool)
                with pool.Fori(0, NGR // 2) as j:
                    for s in range(2):
                        pool.wait_ge(s1_ready, b * NGR + j * 2 + (s - 1) + START)
                        plain(pool)
                        pool.tensor_copy(XgH[:, s, :, :], XhH[:, :, bass.ds((j * 2 + s) * 2, 2)].rearrange("p w c -> p c w")).then_inc(xg_done, 1)
                        pool.tensor_copy(XgL[:, s, :, :], XhL[:, :, bass.ds((j * 2 + s) * 2, 2)].rearrange("p w c -> p c w")).then_inc(xg_done, 1)


def host(inp):
    z = {}
    z["x"] = np.asarray(inp["x"])
    t = np.asarray(inp["L0_conv_w_theta"]).T
    z["wth2"] = np.concatenate([t, t], 1)
    t = np.asarray(inp["L0_conv_w_phi"]).T
    z["wph2"] = np.concatenate([t, t], 1)
    z["wg"] = np.asarray(inp["L0_conv_w_g"]).T
    z["wlast"] = np.asarray(inp["L0_conv_w_last"]).T
    s = np.zeros((CB + 1, 128), np.float32)
    s[CB] = 1
    z["sumsel"] = s
    z["ident"] = np.eye(128, dtype=np.float32)
    g = lambda n: np.asarray(inp[n])
    z["w1"] = g("L1_conv_conv_w").reshape(CB, C, TAPS).transpose(1, 2, 0)
    z["bn"] = np.stack([g("L1_conv_bn1_" + k) for k in "gbmv"], 1)
    z["cgp"] = np.stack([g("L1_conv_cg1_b")] + [g("L1_conv_cgbn_" + k) for k in "gbmv"], 1)
    z["cg2b"] = g("L1_conv_cg2_b")[:, None]
    z["tauc"] = np.repeat(g("L1_conv_tau").reshape(8), 8)[:, None]
    z["eyecg"] = np.concatenate([np.eye(CB, dtype=np.float32), g("L1_conv_cg1_w")[:, :, 0, 0].T], 1)
    z["w2t"] = g("L1_conv_cg2_w")[:, :, 0, 0].T
    head = np.kron(np.eye(8), np.ones((8, 8)))
    z["headneg"] = np.where(head > 0, 0.0, -1e30)
    z["att"] = np.concatenate([head * 0, head / 8], 1)
    z["pairsum"] = np.concatenate([np.eye(CB), np.eye(CB)], 0)
    ang = 2 * np.pi * np.outer(np.arange(W), np.arange(W)) / W
    co, si = np.cos(ang), np.sin(ang)
    z["hdft"] = np.concatenate([co[:, :KH], si[:, :KH]], 1)
    z["wdft"] = np.block([[co, si], [-si, co]])
    z["iwdft"] = np.block([[co, -si], [si, co]])
    a = np.full(KH, 2.0); a[0] = a[-1] = 1
    z["ihdft"] = np.concatenate([co[:KH] * a[:, None], si[:KH] * a[:, None]], 1) / N
    z["w3"] = g("L2_conv_w").reshape(C, C, TAPS).transpose(1, 2, 0)
    z["b3"] = np.stack([g("L2_conv_b_conv"), g("L2_conv_bias"), np.zeros(C, np.float32)], 1)
    f = g("L2_conv_up_filter")
    up = np.zeros((HC, HU), np.float32)
    for i in range(HC):
        for t in range(12):
            if 0 <= 2 * i - 2 + t < HU:
                up[i, 2 * i - 2 + t] = f[t]
    z["upm"] = up
    z["upf"] = np.broadcast_to(f, (C, 12))
    f = g("L2_conv_down_filter")
    dn = np.zeros((HU, H), np.float32)
    for j in range(H):
        for t in range(12):
            dn[2 * j + t, j] = f[11 - t]
    z["dnw"] = dn[:128]
    rest = np.zeros((RC, NR, RC, W - WR), np.float32)
    for c in range(RC):
        rest[c, :, c] = dn[128:, WR:]
    z["dnr"] = rest.reshape(RC * NR, RC, W - WR)
    z["dnm"] = dn.reshape(2, HK, H).transpose(1, 0, 2)
    qkv = g("L3_conv_qkv_w").reshape(HEADS, 3, HD, C)
    z["wq"] = qkv[:, 0].reshape(C, C)
    z["wkv"] = np.concatenate([qkv[:, 1].reshape(C, C), qkv[:, 2].reshape(C, C)], 0).T
    z["o1t"], z["o2t"] = g("L3_conv_o1_w").T, g("L3_conv_o2_w").T
    z["lncol"] = np.stack([g("L3_conv_kln_w").reshape(C), g("L3_conv_kln_b").reshape(C), np.zeros(C, np.float32)], 1)
    z["lnrow"] = np.broadcast_to(np.stack([g("L3_conv_vln_w").reshape(C), g("L3_conv_vln_b").reshape(C)]), (128, 2, C))
    z["headm"] = np.kron(np.eye(HEADS), np.ones((HD, HD))) / N
    return {k: np.ascontiguousarray(v, dtype=np.float32) for k, v in z.items()}


def kernel(**inputs):
    import concourse.bacc as bacc
    from concourse import mybir as _mybir
    from concourse.bass_utils import run_bass_kernel_spmd

    nc = bacc.Bacc("TRN2", target_bir_lowering=False, num_devices=1)
    arrays = host(inputs)
    T = {k: nc.dram_tensor(k, v.shape, _mybir.dt.float32, kind="ExternalInput").ap() for k, v in arrays.items()}
    out = nc.dram_tensor("out", (B, C, H, W), _mybir.dt.float32, kind="ExternalOutput").ap()
    build(nc, T, out)
    r = run_bass_kernel_spmd(nc, [arrays], core_ids=[0])
    return r.results[0]["out"]
```
